# Optimizing a Trainium2 kernel written in Bass

```python
import numpy as np
import jax
import jax.numpy as jnp

def _softmax(x, axis=-1):
    return jax.nn.softmax(x, axis=axis)

def _gelu(x):
    return jax.nn.gelu(x, approximate=True)

def _silu(x):
    return jax.nn.silu(x)

def _sigmoid(x):
    return jax.nn.sigmoid(x)

def _layernorm(x, axis=-1, eps=1e-05):
    m = jnp.mean(x, axis=axis, keepdims=True)
    v = jnp.var(x, axis=axis, keepdims=True)
    return (x - m) / jnp.sqrt(v + eps)

def _scatter_add(tgt, idx, src, axis=0):
    return tgt.at[idx].add(src)

def _segment_sum(src, seg, n):
    return jax.ops.segment_sum(src, seg, n)
kernel_name = 'mk_gnn_resnorm_d2_gnn_r8_73ed4a'

def setup_inputs(seed: int=0):
    np.random.seed(seed)
    _w = jnp.asarray

    def _rec_inputs():
        import jax
        import jax.numpy as jnp
        _gk = jax.random.key(seed)
        x = -0.0003713 + 1 * jax.random.normal(jax.random.fold_in(_gk, 1), (12500, 256), jnp.float32)
        src = jax.random.randint(jax.random.fold_in(_gk, 2), (200000,), 0, 12500, jnp.int32)
        dst = jnp.minimum((12500 * jax.random.uniform(jax.random.fold_in(_gk, 3), (200000,)) ** 2.0).astype(jnp.int32), 99999)
        _o = jnp.argsort(dst, stable=True)
        src = src[_o]
        dst = dst[_o]
        edge_attr_18 = 0.00023367 + 0.999922 * jax.random.normal(jax.random.fold_in(_gk, 11), (200000, 18), jnp.float32)
        return (x, src, dst, edge_attr_18)
    x, src, dst, edge_attr_18 = _rec_inputs()

    def _L0_gnn_setup():
        import jax, jax.numpy as jnp
        import numpy as np
        N, E = (6250, 100000)
        DIM, H, D = (256, 16, 8)
        DH = D * H
        IN_RPE = 18
        SCALE = D ** (-0.5)
        EPS = 1e-16

        def _segment_softmax(compat, s, num_nodes):
            m = jax.ops.segment_max(compat, s, num_segments=num_nodes)
            ex = jnp.exp(compat - m[s])
            den = jax.ops.segment_sum(ex, s, num_segments=num_nodes)
            return ex / (den[s] + EPS)
        key = jax.random.key(seed)
        ks = jax.random.split(key, 10)
        x = jax.random.normal(ks[0], (N, DIM), dtype=jnp.float32)
        edge_index = jax.random.randint(ks[1], (2, E), 0, N, dtype=jnp.int64)
        edge_attr = jax.random.normal(ks[2], (E, IN_RPE), dtype=jnp.float32)
        Wqkv = jax.random.normal(ks[3], (DIM, 2 * DH + DIM), dtype=jnp.float32) * DIM ** (-0.5)
        bqkv = jnp.zeros((2 * DH + DIM,), dtype=jnp.float32)
        Wk_rpe = jax.random.normal(ks[4], (IN_RPE, DH), dtype=jnp.float32) * IN_RPE ** (-0.5)
        bk_rpe = jnp.zeros((DH,), dtype=jnp.float32)
        Wq_rpe = jax.random.normal(ks[5], (IN_RPE, DH), dtype=jnp.float32) * IN_RPE ** (-0.5)
        bq_rpe = jnp.zeros((DH,), dtype=jnp.float32)
        return {'x': x, 'edge_index': edge_index, 'edge_attr': edge_attr, 'Wqkv': Wqkv, 'bqkv': bqkv, 'Wk_rpe': Wk_rpe, 'bk_rpe': bk_rpe, 'Wq_rpe': Wq_rpe, 'bq_rpe': bq_rpe}
    _L0_gnn_all = _L0_gnn_setup()
    _L0_gnn_in = {k: v for k, v in _L0_gnn_all.items() if k in ('Wqkv', 'bqkv', 'Wk_rpe', 'bk_rpe', 'Wq_rpe', 'bq_rpe')}
    del _L0_gnn_all

    def _L1_gnn_setup():
        import jax, jax.numpy as jnp
        import numpy as np
        N_NODES = 12500
        IN_CH = 256
        OUT_CH = 256
        STALK = 4
        N_EDGES = 400000
        key = jax.random.key(seed)
        k1, k2, k3, k4, k5, k6 = jax.random.split(key, 6)
        x = jax.random.normal(k1, (N_NODES, IN_CH), dtype=jnp.float32)
        edge_index = jax.random.randint(k2, (2, N_EDGES), 0, N_NODES, dtype=jnp.int64)
        lim1 = 1.0 / np.sqrt(IN_CH)
        W_r = jax.random.uniform(k3, (IN_CH, STALK), minval=-lim1, maxval=lim1, dtype=jnp.float32)
        b_r = jax.random.uniform(k4, (STALK,), minval=-lim1, maxval=lim1, dtype=jnp.float32)
        lim2 = 1.0 / np.sqrt(STALK)
        W_o = jax.random.uniform(k5, (STALK, OUT_CH), minval=-lim2, maxval=lim2, dtype=jnp.float32)
        b_o = jax.random.uniform(k6, (OUT_CH,), minval=-lim2, maxval=lim2, dtype=jnp.float32)
        return {'x': x, 'edge_index': edge_index, 'W_r': W_r, 'b_r': b_r, 'W_o': W_o, 'b_o': b_o}
    _L1_gnn_all = _L1_gnn_setup()
    _L1_gnn_in = {k: v for k, v in _L1_gnn_all.items() if k in ('W_r', 'b_r', 'W_o', 'b_o')}
    del _L1_gnn_all
    return {'x': x, 'src': src, 'dst': dst, 'edge_attr_18': edge_attr_18, 'L0_gnn_Wqkv': _L0_gnn_in['Wqkv'], 'L0_gnn_bqkv': _L0_gnn_in['bqkv'], 'L0_gnn_Wk_rpe': _L0_gnn_in['Wk_rpe'], 'L0_gnn_bk_rpe': _L0_gnn_in['bk_rpe'], 'L0_gnn_Wq_rpe': _L0_gnn_in['Wq_rpe'], 'L0_gnn_bq_rpe': _L0_gnn_in['bq_rpe'], 'L1_gnn_W_r': _L1_gnn_in['W_r'], 'L1_gnn_b_r': _L1_gnn_in['b_r'], 'L1_gnn_W_o': _L1_gnn_in['W_o'], 'L1_gnn_b_o': _L1_gnn_in['b_o']}

def reference(x, src, dst, edge_attr_18, L0_gnn_Wqkv, L0_gnn_bqkv, L0_gnn_Wk_rpe, L0_gnn_bk_rpe, L0_gnn_Wq_rpe, L0_gnn_bq_rpe, L1_gnn_W_r, L1_gnn_b_r, L1_gnn_W_o, L1_gnn_b_o):
    import jax
    import jax.numpy as jnp

    def _L0_gnn_ref(x, edge_index, edge_attr, Wqkv, bqkv, Wk_rpe, bk_rpe, Wq_rpe, bq_rpe):
        import jax, jax.numpy as jnp
        import numpy as np
        N, E = (6250, 100000)
        DIM, H, D = (256, 16, 8)
        DH = D * H
        IN_RPE = 18
        SCALE = D ** (-0.5)
        EPS = 1e-16

        def _segment_softmax(compat, s, num_nodes):
            m = jax.ops.segment_max(compat, s, num_segments=num_nodes)
            ex = jnp.exp(compat - m[s])
            den = jax.ops.segment_sum(ex, s, num_segments=num_nodes)
            return ex / (den[s] + EPS)
        n = x.shape[0]
        e = edge_index.shape[1]
        qkv = x @ Wqkv + bqkv
        q = qkv[:, :DH].reshape(n, H, D)
        k = qkv[:, DH:2 * DH].reshape(n, H, D)
        v = qkv[:, 2 * DH:].reshape(n, H, DIM // H)
        s, t = (edge_index[0], edge_index[1])
        qe = q[s] * SCALE
        ke = k[t]
        ke = ke + (edge_attr @ Wk_rpe + bk_rpe).reshape(e, H, D)
        qe = qe + (edge_attr @ Wq_rpe + bq_rpe).reshape(e, H, D)
        compat = jnp.einsum('ehd,ehd->eh', qe, ke)
        attn = _segment_softmax(compat, s, n)
        msg = (v[t] * attn[..., None]).reshape(e, DIM)
        out = jax.ops.segment_sum(msg, s, num_segments=n)
        return out

    def _L1_gnn_ref(x, edge_index, W_r, b_r, W_o, b_o):
        import jax, jax.numpy as jnp
        import numpy as np
        N_NODES = 12500
        IN_CH = 256
        OUT_CH = 256
        STALK = 4
        N_EDGES = 400000
        x_stalk = x @ W_r + b_r
        src, dst = (edge_index[0], edge_index[1])
        diff = x_stalk[dst] - x_stalk[src]
        out = jnp.zeros_like(x_stalk)
        out = out.at[dst].add(diff)
        out = out.at[src].add(-diff)
        out = out @ W_o + b_o
        return jax.nn.gelu(out, approximate=False)
    edge_index = jnp.stack([src, dst])
    x = _layernorm(x + _L0_gnn_ref(x, edge_index, edge_attr_18, L0_gnn_Wqkv, L0_gnn_bqkv, L0_gnn_Wk_rpe, L0_gnn_bk_rpe, L0_gnn_Wq_rpe, L0_gnn_bq_rpe), axis=-1)
    x = _layernorm(x + _L1_gnn_ref(x, edge_index, L1_gnn_W_r, L1_gnn_b_r, L1_gnn_W_o, L1_gnn_b_o), axis=-1)
    return x

_drawn_inputs = setup_inputs


def setup_inputs(seed=0):
    import zlib

    import numpy as np

    out = dict(_drawn_inputs(seed))
    spreads = {'L0_gnn_bqkv': (0.0, 0.1), 'L0_gnn_bk_rpe': (0.0, 0.1), 'L0_gnn_bq_rpe': (0.0, 0.1)}
    factors = {}
    for name, (base, spread) in spreads.items():
        noise = np.random.default_rng([zlib.crc32(name.encode()), seed]).standard_normal(out[name].shape)
        drawn = base * np.exp(spread * noise) if base else spread * noise
        out[name] = jnp.asarray(drawn.astype(out[name].dtype))
    for name, factor in factors.items():
        out[name] = (out[name] * factor).astype(out[name].dtype)
    return out
```

```python
import concourse.bass as bass
from concourse import mybir
from concourse.alu_op_type import AluOpType as ALU
from contextlib import ExitStack

F32 = mybir.dt.float32
BF16 = mybir.dt.bfloat16
I32 = mybir.dt.int32
ACT = mybir.ActivationFunctionType
AX = mybir.AxisListType

P = 128
N, E = 12500, 200000
DIM, H, D, RPE, STALK = 256, 16, 8, 18, 4
DH, DV = H * D, DIM // H
HV = DV + 1
NB = -(-N // P)
NLAST = N - (NB - 1) * P
SCALE = float(D) ** -0.5
SOFT_EPS, NORM_EPS = 1e-16, 1e-5
FAR = 1e30

CT = 16
FULL = E // (P * CT)
NCH = NB
LAST_T = 12
LAST_P = (E - FULL * P * CT) // LAST_T
assert FULL + 1 == NCH and LAST_P * LAST_T + FULL * P * CT == E

G = 8
GROUPS = 2 * -(-((E + (P - 1) * NB) // P) // (2 * G))
ST = G * GROUPS
TPP = ST // P
REC = RPE + 3
ONE, LOC, DST = RPE, RPE + 1, RPE + 2
assert NB * P > N


def need(engine, sem, count):
    if not (isinstance(count, int) and count <= 0):
        engine.wait_ge(sem, count)


def rounds(engine, n, body):
    body(0)
    with engine.Fori(1, n) as i:
        body(i)


class Room:
    def __init__(self, nc, stack, stage):
        self.nc, self.stack, self.stage = nc, stack, stage

    def sb(self, name, shape, dt=F32):
        return self.stack.enter_context(self.nc.sbuf_tensor(f"{self.stage}_{name}", shape, dt))

    def ps(self, name, shape, dt=F32):
        return self.stack.enter_context(self.nc.psum_tensor(f"{self.stage}_{name}", shape, dt))

    def sem(self, name):
        return self.stack.enter_context(self.nc.semaphore(f"{self.stage}_{name}"))


def constants(nc, k, c):
    built = k.sem("built")
    counted = k.sem("counted")
    with nc.Block() as block:
        @block.gpsimd
        def _(pool):
            nc.gpsimd.memset(c["ones"][:, :], 1.0).then_inc(built, 1)
            nc.gpsimd.memset(c["zeros"][:, :], 0.0).then_inc(built, 1)
            nc.gpsimd.iota(c["row_i"][:, :], [[1, P]], base=0, channel_multiplier=0).then_inc(counted, 1)
            pool.wait_ge(built, 2)
            nc.gpsimd.affine_select(out=c["ident"][:, :], in_=c["zeros"][:, :], compare_op=ALU.not_equal,
                                    fill=1.0, base=0, pattern=[[-1, P]], channel_multiplier=1).then_inc(built, 1)
            nc.gpsimd.affine_select(out=c["before"][:, :], in_=c["ones"][:, :], compare_op=ALU.is_gt,
                                    fill=0.0, base=0, pattern=[[1, P]], channel_multiplier=-1).then_inc(built, 1)
            nc.gpsimd.affine_select(out=c["after"][:, :], in_=c["ones"][:, :], compare_op=ALU.is_gt,
                                    fill=0.0, base=0, pattern=[[-1, P]], channel_multiplier=1).then_inc(built, 1)
            pool.wait_ge(built, 5)

        @block.vector
        def _(dve):
            dve.wait_ge(counted, 1)
            nc.vector.tensor_copy(c["row"][:, :], c["row_i"][:, :]).then_inc(counted, 1)
            nc.vector.tensor_copy(c["row_bf"][:, :], c["row_i"][:, :])
            dve.wait_ge(built, 5)
            nc.vector.tensor_copy(c["ident_bf"][:, :], c["ident"][:, :])
            nc.vector.tensor_copy(c["zeros_bf"][:, :], c["zeros"][:, :])


def spread(ap, n):
    p, a = ap.shape
    return ap.unsqueeze(2).to_broadcast([p, a, n])


def over(ap, n):
    p, a = ap.shape
    return ap.unsqueeze(1).to_broadcast([p, n, a])


def project_and_count(nc, k, c, x, src, dst, Wqkv, bqkv, e, q_tab, kv_dram, rec_dram, counts):
    w = k.sb("w", [P, 2, DH * 2 + DIM])
    bias = k.sb("bias", [1, DH * 2 + DIM])
    xs = k.sb("x", [P, 2, DIM])
    xT = k.sb("xT", [P, 2, DIM])
    kv = k.sb("kv", [P, 2, DH + DIM])
    blank = k.sb("blank", [P, 104, REC])
    scratch = k.sb("scratch", [P, NCH * CT], I32)
    scratch2 = k.sb("scratch2", [P, NCH * CT], I32)
    at_bf = k.sb("at_bf", [P, NCH * CT], BF16)
    of_bf = k.sb("of_bf", [P, NCH * CT], BF16)
    hot_p = k.sb("hot_p", [P, 2, CT, P], BF16)
    hot_b = k.sb("hot_b", [P, 2, CT, NB], BF16)
    xT_ps = [k.ps(f"xT_ps{h}", [P, DIM]) for h in range(2)]
    qkv_ps = [k.ps(f"qkv_ps{h}", [P, DH * 2 + DIM]) for h in range(2)]
    count_ps = k.ps("count_ps", [P, NB])
    padded = k.sem("padded")
    weights_in = k.sem("weights_in")
    edges_in = k.sem("edges_in")
    x_in = [k.sem(f"x_in{h}") for h in range(2)]
    transposed = k.sem("transposed")
    xT_copied = k.sem("xT_copied")
    projected = k.sem("projected")
    q_copied = k.sem("q_copied")
    kv_copied = k.sem("kv_copied")
    kv_out = [k.sem(f"kv_out{h}") for h in range(2)]
    blanks_out = k.sem("blanks_out")
    index_step = k.sem("index_step")
    hot_ready = k.sem("hot_ready")
    counted = k.sem("counted")
    all_counted = k.sem("all_counted")
    BLANKS = ST * P // (P * 104)

    with nc.Block() as block:
        @block.gpsimd
        def _(pool):
            nc.gpsimd.memset(e["src"][:, NCH - 1, :], -1).then_inc(padded, 1)
            nc.gpsimd.memset(e["dst"][:, NCH - 1, :], 0).then_inc(padded, 1)
            nc.gpsimd.memset(blank[:, :, :], 0.0).then_inc(padded, 1)
            pool.wait_ge(padded, 3)
            nc.gpsimd.memset(blank[:, :, LOC:LOC + 1], -1.0).then_inc(padded, 1)
            nc.gpsimd.memset(blank[:, :, DST:DST + 1].bitcast(I32), NB * P - 1).then_inc(padded, 1)

        @block.sync
        def _(sp):
            edges = [(e["src"], src), (e["dst"], dst)]
            sp.dma_start(e["src"][:, 0:FULL, :], src[0:FULL * P * CT].rearrange("(c p j) -> p c j", p=P, j=CT)).then_inc(edges_in, 16)
            sp.wait_ge(padded, 5)
            for to, of in edges:
                sp.dma_start(to[0:LAST_P, NCH - 1, 0:LAST_T],
                             of[FULL * P * CT:E].rearrange("(p j) -> p j", j=LAST_T)).then_inc(edges_in, 16)
            sp.dma_start(w[:, :, :], Wqkv.rearrange("(a p) n -> p a n", p=P)).then_inc(weights_in, 16)
            sp.dma_start(bias[:, :], bqkv.rearrange("(a n) -> a n", a=1)).then_inc(weights_in, 16)
            sp.dma_start(e["dst"][:, 0:FULL, :], dst[0:FULL * P * CT].rearrange("(c p j) -> p c j", p=P, j=CT)).then_inc(edges_in, 16)

            def load(b, h, i, rows=P):
                need(sp, transposed, 2 * i + h - 1)
                sp.dma_start(xs[0:rows, h, :], x[bass.ds(b * P, rows), :]).then_inc(x_in[h], 16)
            load(0, 0, 0)
            load(1, 1, 0)
            with sp.Fori(1, NB // 2 - 1) as i:
                for h in range(2):
                    load(2 * i + h, h, i)
            load(NB - 2, 0, NB // 2 - 1)
            load(NB - 1, 1, NB // 2 - 1, NLAST)
            for n in range(BLANKS):
                sp.dma_start(rec_dram[n * P * 104:(n + 1) * P * 104, :].rearrange("(p r) w -> p r w", p=P),
                             blank[:, :, :]).then_inc(blanks_out, 16)
            sp.wait_ge(blanks_out, 16 * BLANKS)
            sp.wait_ge(edges_in, 64)

        @block.vector
        def _(dve):
            dve.wait_ge(edges_in, 64)
            flat = e["src"][:, :, :].rearrange("p c j -> p (c j)")
            nc.vector.tensor_copy(e["src_f"][:, :], flat).then_inc(index_step, 1)
            nc.vector.tensor_scalar(scratch[:, :], flat, P - 1, None, ALU.bitwise_and).then_inc(index_step, 1)
            nc.vector.tensor_scalar(scratch2[:, :], flat, 7, None, ALU.arith_shift_right).then_inc(index_step, 1)
            dve.wait_ge(index_step, 3)
            nc.vector.tensor_copy(at_bf[:, :], scratch[:, :]).then_inc(index_step, 1)
            nc.vector.tensor_copy(of_bf[:, :], scratch2[:, :]).then_inc(index_step, 1)
            nc.vector.tensor_copy(e["at"][:, :], scratch[:, :])
            nc.vector.tensor_copy(e["of"][:, :], scratch2[:, :])
            dve.wait_ge(index_step, 5)

            def body(i):
                for h in range(2):
                    g = 2 * i + h
                    need(dve, counted, g - 1)
                    nc.vector.tensor_tensor(hot_p[:, h], over(c["row_bf"][:, :], CT),
                                            spread(at_bf[:, bass.ds(g * CT, CT)], P), ALU.is_equal).then_inc(hot_ready, 1)
                    nc.vector.tensor_tensor(hot_b[:, h], over(c["row_bf"][:, 0:NB], CT),
                                            spread(of_bf[:, bass.ds(g * CT, CT)], NB), ALU.is_equal).then_inc(hot_ready, 1)
            rounds(dve, NCH // 2, body)

        @block.tensor
        def _(pe):
            pe.wait_ge(weights_in, 32)
            nc.tensor.matmul(count_ps[:, :], c["zeros_bf"][:, :], c["zeros_bf"][:, 0:NB], start=True, stop=False)

            def body(i):
                for h in range(2):
                    g = 2 * i + h
                    pe.wait_ge(x_in[h], 16 * i + 16)
                    need(pe, xT_copied, g - 1)
                    for a in range(2):
                        last = nc.tensor.transpose(xT_ps[h][:, a * P:(a + 1) * P], xs[:, h, a * P:(a + 1) * P], c["ident"][:, :])
                    last.then_inc(transposed, 1)
                    pe.wait_ge(hot_ready, 2 * g + 2)
                    for j in range(CT):
                        last = nc.tensor.matmul(count_ps[:, :], hot_p[:, h, j], hot_b[:, h, j], start=False, stop=False)
                    last.then_inc(counted, 1)
                    pe.wait_ge(xT_copied, g + 1)
                    need(pe, kv_copied, g - 1)
                    for a in range(2):
                        nc.tensor.matmul(qkv_ps[h][:, :], xT[:, h, a * P:(a + 1) * P], w[:, a], start=(a == 0), stop=False)
                    nc.tensor.matmul(qkv_ps[h][:, :], c["ones"][0:1, :], bias[0:1, :], start=False, stop=True).then_inc(projected, 1)
            rounds(pe, NB // 2, body)
            nc.tensor.matmul(count_ps[:, :], c["zeros_bf"][:, :], c["zeros_bf"][:, 0:NB], start=False, stop=True).then_inc(all_counted, 1)

        @block.scalar
        def _(act):
            def body(i):
                for h in range(2):
                    g = 2 * i + h
                    act.wait_ge(transposed, g + 1)
                    need(act, projected, g - 1)
                    nc.scalar.activation(xT[:, h, :], xT_ps[h][:, :], ACT.Copy).then_inc(xT_copied, 1)
                    act.wait_ge(projected, g + 1)
                    nc.scalar.activation(q_tab[:, bass.ds(g, 1), :].rearrange("p a d -> p (a d)"), qkv_ps[h][:, 0:DH], ACT.Copy, scale=SCALE).then_inc(q_copied, 1)
                    need(act, kv_out[h], 16 * i)
                    nc.scalar.activation(kv[:, h, :], qkv_ps[h][:, DH:], ACT.Copy).then_inc(kv_copied, 1)
                    act.wait_ge(kv_copied, g + 1)
                    act.dma_start(kv_dram[bass.ds(g * P, P), :], kv[:, h, :]).then_inc(kv_out[h], 16)
            rounds(act, NB // 2, body)
            act.wait_ge(all_counted, 1)
            nc.scalar.activation(counts[:, :], count_ps[:, :], ACT.Copy).then_inc(all_counted, 1)
            for h in range(2):
                act.wait_ge(kv_out[h], 16 * (NB // 2))
            act.wait_ge(all_counted, 2)
            act.wait_ge(q_copied, NB)


def place_nodes(nc, k, c, counts, base, blocks_dram):
    within = k.ps("within", [P, NB])
    total = k.ps("total", [P, NB])
    filled = k.sb("filled", [P, NB])
    filled_i = k.sb("filled_i", [P, NB], I32)
    tiles_i = k.sb("tiles_i", [P, NB], I32)
    tiles = k.sb("tiles", [P, NB])
    ends = k.sb("ends", [P, NB])
    starts = k.sb("starts", [P, NB])
    number_i = k.sb("number_i", [P, TPP], I32)
    number = k.sb("number", [P, TPP])
    passed = k.sb("passed", [P, TPP, NB])
    block_f = k.sb("block_f", [P, TPP])
    block_i = k.sb("block_i", [P, TPP], I32)
    summed = k.sem("summed")
    numbered = k.sem("numbered")
    step = k.sem("step")
    found = k.sem("found")
    blocks_out = k.sem("blocks_out")
    with nc.Block() as block:
        @block.gpsimd
        def _(pool):
            nc.gpsimd.iota(number_i[:, :], [[1, TPP]], base=0, channel_multiplier=TPP).then_inc(numbered, 1)

        @block.tensor
        def _(pe):
            nc.tensor.matmul(within[:, :], c["before"][:, :], counts[:, :], start=True, stop=True)
            nc.tensor.matmul(total[:, :], c["ones"][:, :], counts[:, :], start=True, stop=True).then_inc(summed, 1)

        @block.vector
        def _(dve):
            steps = [0]

            def then(ins):
                steps[0] += 1
                ins.then_inc(step, 1)
                dve.wait_ge(step, steps[0])
            dve.wait_ge(numbered, 1)
            then(nc.vector.tensor_copy(number[:, :], number_i[:, :]))
            dve.wait_ge(summed, 1)
            then(nc.vector.tensor_scalar(filled[:, :], total[:, :], float(P - 1), None, ALU.add))
            then(nc.vector.tensor_copy(filled_i[:, :], filled[:, :]))
            then(nc.vector.tensor_scalar(tiles_i[:, :], filled_i[:, :], 7, None, ALU.logical_shift_right))
            then(nc.vector.tensor_copy(tiles[:, :], tiles_i[:, :]))
            then(nc.vector.tensor_tensor_scan(ends[:, :], c["ones"][:, 0:NB], tiles[:, :], 0.0, ALU.mult, ALU.add))
            then(nc.vector.tensor_tensor(starts[:, :], ends[:, :], tiles[:, :], ALU.subtract))
            then(nc.vector.scalar_tensor_tensor(base[:, :], starts[:, :], float(P), within[:, :], ALU.mult, ALU.add))
            then(nc.vector.tensor_tensor(passed[:, :, :], over(ends[:, :], TPP), spread(number[:, :], NB), ALU.is_le))
            then(nc.vector.tensor_reduce(block_f[:, :], passed[:, :, :], AX.X, ALU.add))
            then(nc.vector.tensor_scalar(block_f[:, :], block_f[:, :], float(NB - 1), None, ALU.min))
            nc.vector.tensor_copy(block_i[:, :], block_f[:, :]).then_inc(found, 1)

        @block.sync
        def _(sp):
            sp.wait_ge(found, 1)
            sp.dma_start(blocks_dram.rearrange("(p j) -> p j", j=TPP), block_i[:, :]).then_inc(blocks_out, 16)
            sp.wait_ge(blocks_out, 16)


def sort_edges(nc, k, c, e, edge_attr, base, rec_dram):
    rec = k.sb("rec", [P, 2, G, REC])
    at_bf = k.sb("at_bf", [P, 2, G], BF16)
    of_bf = k.sb("of_bf", [P, 2, G], BF16)
    src_f = k.sb("src_f", [P, 2, G])
    hot_p = k.sb("hot_p", [P, 2, G, P], BF16)
    hot_b = k.sb("hot_b", [P, 2, G, NB], BF16)
    hot_pT = k.sb("hot_pT", [P, 2, P])
    table = k.sb("table", [P, 2, NB])
    junk_v = k.sb("junk_v", [P, G, NB], BF16)
    junk_r = k.sb("junk_r", [P, G, P], BF16)
    first = k.sb("first", [P, 2, G])
    rank = k.sb("rank", [P, 2, G])
    place_f = k.sb("place_f", [P, G])
    place_i = k.sb("place_i", [P, G], I32)
    row_hi = k.sb("row_hi", [P, G], I32)
    row_p = k.sb("row_p", [P, G], I32)
    row_t = k.sb("row_t", [P, G], I32)
    row_pt = k.sb("row_pt", [P, G], I32)
    row = k.sb("row", [P, 2, G], I32)
    hot_pT_ps = [k.ps(f"hot_pT_ps{s}", [P, P], BF16) for s in range(2)]
    other_ps = [k.ps(f"other_ps{s}", [P, P]) for s in range(2)]
    first_ps = [k.ps(f"first_ps{s}", [P, NB]) for s in range(2)]
    table_ps = k.ps("table_ps", [P, NB])
    one_set = k.sem("one_set")
    attr_in = [k.sem(f"attr_in{h}") for h in range(2)]
    copied_in = k.sem("copied_in")
    hot_ready = k.sem("hot_ready")
    turned = k.sem("turned")
    turned_copied = k.sem("turned_copied")
    table_made = k.sem("table_made")
    table_copied = k.sem("table_copied")
    looked_up = k.sem("looked_up")
    tile_ranked = k.sem("tile_ranked")
    step = k.sem("step")
    rows_ready = k.sem("rows_ready")
    scattered = [k.sem(f"scattered{h}") for h in range(2)]
    slot_free = k.sem("slot_free")
    pool_turn = k.sem("pool_turn")
    STEPS = 8

    with nc.Block() as block:
        @block.sync
        def _(sp):
            def load(i, chunk, parts=P, width=CT):
                for h in range(2):
                    n = min(G, width - h * G)
                    need(sp, slot_free, 2 * i + h - 1)
                    rows = edge_attr[bass.ds(chunk * P * CT, parts * width), :].rearrange("(p j) w -> p j w", j=width)
                    sp.dma_start(rec[0:parts, h, 0:n, 0:RPE], rows[:, h * G:h * G + n, :]).then_inc(attr_in[h], 16)
            load(0, 0)
            with sp.Fori(1, FULL) as i:
                load(i, i)
            load(FULL, FULL, LAST_P, LAST_T)

        @block.vector
        def _(dve):
            nc.vector.memset(rec[:, :, :, ONE:ONE + 1], 1.0).then_inc(one_set, 1)

            def body(i):
                for h in range(2):
                    g = 2 * i + h
                    cols = bass.ds(g * G, G)
                    need(dve, table_made, G * (g - 1) + 1 if not isinstance(g, int) or g > 1 else 0)
                    nc.vector.tensor_scalar(at_bf[:, h], e["at"][:, cols], 1.0, None, ALU.mult).then_inc(copied_in, 1)
                    nc.vector.tensor_scalar(of_bf[:, h], e["of"][:, cols], 1.0, None, ALU.mult).then_inc(copied_in, 1)
                    nc.vector.tensor_scalar(src_f[:, h], e["src_f"][:, cols], 1.0, None, ALU.mult).then_inc(copied_in, 1)
                    dve.wait_ge(copied_in, 3 * g + 3)
                    nc.vector.tensor_tensor(hot_p[:, h], over(c["row_bf"][:, :], G), spread(at_bf[:, h], P), ALU.is_equal).then_inc(hot_ready, 1)
                    nc.vector.tensor_tensor(hot_b[:, h], over(c["row_bf"][:, 0:NB], G), spread(of_bf[:, h], NB), ALU.is_equal).then_inc(hot_ready, 1)
                    dve.wait_ge(hot_ready, 2 * g + 2)
                    for j in range(G):
                        t = G * g + j
                        dve.wait_ge(turned, t + 1)
                        nc.vector.scalar_tensor_tensor(junk_r[:, j], other_ps[j % 2][:, :], src_f[:, h, j:j + 1], c["after"][:, :],
                                                       ALU.is_equal, ALU.mult, accum_out=rank[:, h, j:j + 1]).then_inc(tile_ranked, 1)
                        dve.wait_ge(looked_up, t + 1)
                        nc.vector.scalar_tensor_tensor(junk_v[:, j], first_ps[j % 2][:, :], 1.0, hot_b[:, h, j],
                                                       ALU.mult, ALU.mult, accum_out=first[:, h, j:j + 1]).then_inc(tile_ranked, 1)
                    dve.wait_ge(tile_ranked, 2 * G * (g + 1))

                    n = [STEPS * g]

                    def then(ins):
                        n[0] = n[0] + 1
                        ins.then_inc(step, 1)
                        dve.wait_ge(step, n[0])
                    then(nc.vector.tensor_tensor(place_f[:, :], first[:, h], rank[:, h], ALU.add))
                    then(nc.vector.tensor_copy(place_i[:, :], place_f[:, :]))
                    then(nc.vector.tensor_scalar(row_hi[:, :], place_i[:, :], 10, 10, ALU.logical_shift_right, ALU.logical_shift_left))
                    then(nc.vector.tensor_scalar(row_p[:, :], place_i[:, :], P - 1, 3, ALU.bitwise_and, ALU.logical_shift_left))
                    then(nc.vector.tensor_scalar(row_t[:, :], place_i[:, :], 7, G - 1, ALU.logical_shift_right, ALU.bitwise_and))
                    then(nc.vector.tensor_tensor(row_pt[:, :], row_p[:, :], row_t[:, :], ALU.bitwise_or))
                    need(dve, slot_free, g - 1)
                    then(nc.vector.tensor_scalar(rec[:, h, :, LOC], e["at"][:, cols], 1.0, None, ALU.mult))
                    then(nc.vector.tensor_scalar(rec[:, h, :, DST].bitcast(I32), e["dst"][:, :, :].rearrange("p c j -> p (c j)")[:, cols], 1.0, None, ALU.mult))
                    nc.vector.tensor_tensor(row[:, h], row_hi[:, :], row_pt[:, :], ALU.bitwise_or).then_inc(rows_ready, 1)
            rounds(dve, NCH, body)

        @block.tensor
        def _(pe):
            nc.tensor.matmul(table_ps[:, :], c["ident"][:, :], base[:, :], start=True, stop=True).then_inc(table_made, 1)

            def body(i):
                for h in range(2):
                    g = 2 * i + h

                    def turn(j):
                        t = G * g + j
                        need(pe, turned_copied, t - 1)
                        nc.tensor.transpose(hot_pT_ps[j % 2][:, :], hot_p[:, h, j], c["ident_bf"][:, :])
                        need(pe, tile_ranked, 2 * (t - 1))
                        nc.tensor.transpose(other_ps[j % 2][:, :], src_f[:, h, j:j + 1].to_broadcast([P, P]), c["ident"][:, :]).then_inc(turned, 1)
                    pe.wait_ge(hot_ready, 2 * g + 2)
                    turn(0)
                    for j in range(G):
                        t = G * g + j
                        if j + 1 < G:
                            turn(j + 1)
                        pe.wait_ge(turned_copied, t + 1)
                        pe.wait_ge(table_copied, t + 1)
                        need(pe, tile_ranked, 2 * (t - 1))
                        nc.tensor.matmul(first_ps[j % 2][:, :], hot_pT[:, j % 2], table[:, j % 2], start=True, stop=True).then_inc(looked_up, 1)
                        nc.tensor.matmul(table_ps[:, :], hot_p[:, h, j], hot_b[:, h, j], start=False, stop=True, skip_group_check=True).then_inc(table_made, 1)
            rounds(pe, NCH, body)

        @block.scalar
        def _(act):
            def body(i):
                for h in range(2):
                    for j in range(G):
                        t = G * (2 * i + h) + j
                        act.wait_ge(turned, t + 1)
                        need(act, looked_up, t - 1)
                        nc.scalar.activation(hot_pT[:, j % 2], hot_pT_ps[j % 2][:, :], ACT.Copy).then_inc(turned_copied, 1)
                        act.wait_ge(table_made, t + 1)
                        nc.scalar.activation(table[:, j % 2], table_ps[:, :], ACT.Copy).then_inc(table_copied, 1)
            rounds(act, NCH, body)

        @block.gpsimd
        def _(pool):
            pool.wait_ge(one_set, 1)

            def group(i, h, parts=P, tiles=G):
                g = 2 * i + h
                pool.wait_ge(attr_in[h], 16 * i + 16)
                pool.sem_inc(pool_turn)
                pool.wait_ge(rows_ready, g + 1)
                pool.sem_inc(pool_turn)
                for j in range(tiles):
                    nc.gpsimd.indirect_dma_start(rec_dram[:, :], bass.IndirectOffsetOnAxis(ap=row[0:parts, h, j:j + 1], axis=0),
                                                 rec[0:parts, h, j], None).then_inc(scattered[h], 16)
                    if j == 2 and not (isinstance(g, int) and g == 0):
                        pool.wait_ge(scattered[1 - h], 16 * G * (i + h))
                        pool.sem_inc(slot_free)

            def body(i):
                for h in range(2):
                    group(i, h)
            body(0)
            with pool.Fori(1, FULL) as i:
                body(i)
            group(FULL, 0, LAST_P, G)
            group(FULL, 1, LAST_P, LAST_T - G)
            pool.wait_ge(scattered[0], 16 * G * (FULL + 1))
            pool.wait_ge(scattered[1], 16 * (G * FULL + LAST_T - G))


def attend(nc, k, c, Wk_rpe, bk_rpe, Wq_rpe, bq_rpe, q_tab, kv_dram, rec_dram, blocks_dram, sums):
    SUM = DIM + H
    rpe = k.sb("rpe", [ONE + 1, 2 * DH])
    rec = k.sb("rec", [P, 2, G, REC])
    tile_block = k.sb("tile_block", [1, 2, G], I32)
    kv = k.sb("kv", [P, 2, G, DH + SUM])
    hot = k.sb("hot", [P, 2, G, P])
    hotT = k.sb("hotT", [P, G, P])
    recT = k.sb("recT", [ONE + 1, 4, P])
    loc16 = k.sb("loc16", [P, G, H])
    locT = k.sb("locT", [P, P])
    fresh = k.sb("fresh", [P, P + 1])
    drop = k.sb("drop", [P, P])
    run = k.sb("run", [P, P])
    lasts = k.sb("lasts", [P, P])
    compat = k.sb("compat", [P, G, H])
    lastsT = k.sb("lastsT", [P, G, H + 1])
    absent = k.sb("absent", [P, G])
    maxima = k.sb("maxima", [P, NB, H])
    before = k.sb("before", [P, H])
    fall = k.sb("fall", [P, H])
    keep = k.sb("keep", [P, H])
    shifted = k.sb("shifted", [P, G, H])
    qk_ps = [k.ps(f"qk_ps{s}", [P, 2, 2 * DH]) for s in range(2)]
    hotT_ps = k.ps("hotT_ps", [P, 4, P])
    recT_ps = k.ps("recT_ps", [P, 4, P])
    sum_ps = [k.ps(f"sum_ps{s}", [P, SUM]) for s in range(2)]
    turn_ps = k.ps("turn_ps", [P, 2, P])
    node_ps = k.ps("node_ps", [P, 512])
    lastsT_ps = node_ps[:, 0:P]
    tops = node_ps[:, P:P + G * (H + 1)].rearrange("p (t w) -> p t w", t=G)
    spread_ps = node_ps[:, 3 * P:4 * P].rearrange("p (t w) -> p t w", t=G)

    rpe_in = k.sem("rpe_in")
    cleared = k.sem("cleared")
    rec_in = [k.sem(f"rec_in{h}") for h in range(2)]
    gathered = [k.sem(f"gathered{h}") for h in range(2)]
    pool_turn = k.sem("pool_turn")
    hot_ready = k.sem("hot_ready")
    loc_spread = k.sem("loc_spread")
    hot_turned = k.sem("hot_turned")
    rec_turned = k.sem("rec_turned")
    hot_copied = k.sem("hot_copied")
    rec_copied = k.sem("rec_copied")
    pair_ready = k.sem("pair_ready")
    pair_keyed = k.sem("pair_keyed")
    pair_used = k.sem("pair_used")
    loc_turned = k.sem("loc_turned")
    loc_copied = k.sem("loc_copied")
    compat_ready = k.sem("compat_ready")
    compat_turned = k.sem("compat_turned")
    scan_step = k.sem("scan_step")
    lasts_ready = k.sem("lasts_ready")
    lasts_turned = k.sem("lasts_turned")
    lasts_copied = k.sem("lasts_copied")
    tops_ready = k.sem("tops_ready")
    before_kept = k.sem("before_kept")
    absent_ready = k.sem("absent_ready")
    maximum_taken = k.sem("maximum_taken")
    maxima_spread = k.sem("maxima_spread")
    fall_ready = k.sem("fall_ready")
    keep_ready = k.sem("keep_ready")
    scaled = k.sem("scaled")
    shift_done = k.sem("shift_done")
    exp_done = k.sem("exp_done")
    weighted = k.sem("weighted")
    tile_summed = k.sem("tile_summed")
    tile_added = k.sem("tile_added")

    with nc.Block() as block:
        @block.sync
        def _(sp):
            sp.dma_start(rpe[0:RPE, 0:DH], Wq_rpe).then_inc(rpe_in, 16)
            sp.dma_start(rpe[0:RPE, DH:], Wk_rpe).then_inc(rpe_in, 16)
            sp.dma_start(rpe[ONE:ONE + 1, 0:DH], bq_rpe.rearrange("(a n) -> a n", a=1)).then_inc(rpe_in, 16)
            sp.dma_start(rpe[ONE:ONE + 1, DH:], bk_rpe.rearrange("(a n) -> a n", a=1)).then_inc(rpe_in, 16)

            def body(i):
                for h in range(2):
                    g = 2 * i + h
                    need(sp, compat_ready, g - 1)
                    sp.dma_start(rec[:, h, :, :], rec_dram[bass.ds(g * G * P, G * P), :].rearrange("(p t) w -> p t w", t=G)).then_inc(rec_in[h], 16)
                    sp.dma_start(tile_block[:, h, :], blocks_dram[bass.ds(g * G, G)].rearrange("(a t) -> a t", a=1)).then_inc(rec_in[h], 16)
            rounds(sp, GROUPS // 2, body)
            sp.wait_ge(rpe_in, 64)

        @block.gpsimd
        def _(pool):
            def body(i):
                for h in range(2):
                    g = 2 * i + h
                    pool.wait_ge(rec_in[h], 32 * i + 32)
                    pool.sem_inc(pool_turn)
                    if not (isinstance(i, int) and i == 0):
                        pool.wait_ge(tile_summed, G * (g - 1))
                        pool.sem_inc(pool_turn)
                    for t in range(G):
                        nc.gpsimd.indirect_dma_start(kv[:, h, t, 0:DH + DIM], None, kv_dram[:, :],
                                                     bass.IndirectOffsetOnAxis(ap=rec[:, h, t, DST:DST + 1].bitcast(I32), axis=0)).then_inc(gathered[h], 16)
            rounds(pool, GROUPS // 2, body)

        @block.scalar
        def _(act):
            def body(i):
                for h in range(2):
                    g = 2 * i + h
                    act.wait_ge(rec_in[h], 32 * i + 32)
                    need(act, loc_turned, g)
                    nc.scalar.activation(loc16[:, :, :], spread(rec[:, h, :, LOC], H), ACT.Copy).then_inc(loc_spread, 1)
                    for z in range(2):
                        act.wait_ge(hot_turned, 2 * g + z + 1)
                        need(act, maxima_spread, g)
                        nc.scalar.activation(hotT[:, 4 * z:4 * z + 4], hotT_ps[:, :, :], ACT.Copy).then_inc(hot_copied, 1)
                        act.wait_ge(rec_turned, 2 * g + z + 1)
                        need(act, pair_ready, 4 * g + 2 * z)
                        nc.scalar.activation(recT[:, :], recT_ps[0:ONE + 1, :, :], ACT.Copy).then_inc(rec_copied, 1)
                    act.wait_ge(loc_turned, g + 1)
                    need(act, lasts_ready, g)
                    nc.scalar.activation(locT[:, :], turn_ps[:, 0], ACT.Copy).then_inc(loc_copied, 1)
                    act.wait_ge(lasts_turned, g + 1)
                    need(act, tops_ready, g)
                    nc.scalar.activation(lastsT[:, :, 0:H], lastsT_ps.rearrange("p (t w) -> p t w", t=G), ACT.Copy).then_inc(lasts_copied, 1)
                    act.wait_ge(fall_ready, g + 1)
                    need(act, scaled, g)
                    nc.scalar.activation(keep[:, :], fall[:, :], ACT.Exp).then_inc(keep_ready, 1)
                    act.wait_ge(shift_done, g + 1)
                    nc.scalar.activation(kv[:, h, :, DH + DIM:], shifted[:, :, :], ACT.Exp).then_inc(exp_done, 1)
            rounds(act, GROUPS // 2, body)

        @block.vector
        def _(dve):
            nc.vector.memset(sums[:, :, :], 0.0).then_inc(cleared, 1)
            nc.vector.memset(maxima[:, :, :], -FAR).then_inc(cleared, 1)
            nc.vector.memset(fresh[:, :], 1.0).then_inc(cleared, 1)
            nc.vector.memset(lastsT[:, :, H:], 1.0).then_inc(cleared, 1)
            dve.wait_ge(cleared, 4)

            def body(i):
                for h in range(2):
                    g = 2 * i + h
                    dve.wait_ge(rec_in[h], 32 * i + 32)
                    need(dve, tile_summed, G * (g - 1))
                    nc.vector.tensor_tensor(hot[:, h], over(c["row"][:, :], G), spread(rec[:, h, :, LOC], P), ALU.is_equal).then_inc(hot_ready, 1)
                    block_of = [dve.value_load(tile_block[0:1, h, t:t + 1], min_val=0, max_val=NB - 1) for t in range(G)]
                    dve.wait_ge(gathered[h], 16 * G * (i + 1))
                    for u in range(G // 2):
                        keys = kv[:, h, 2 * u:2 * u + 2, 0:DH]
                        dve.wait_ge(pair_ready, 4 * g + u + 1)
                        nc.vector.tensor_tensor(keys, keys, qk_ps[u % 2][:, :, DH:], ALU.add).then_inc(pair_keyed, 1)
                        dve.wait_ge(pair_keyed, 4 * g + u + 1)
                        nc.vector.tensor_tensor(keys, keys, qk_ps[u % 2][:, :, 0:DH], ALU.mult).then_inc(pair_used, 1)
                    dve.wait_ge(pair_used, 4 * g + 4)
                    nc.vector.tensor_reduce(compat[:, :, :], kv[:, h, :, 0:DH].rearrange("p t (h d) -> p t h d", h=H), AX.X, ALU.add).then_inc(compat_ready, 1)
                    dve.wait_ge(loc_copied, g + 1)
                    nc.vector.tensor_tensor(fresh[:, 1:P], locT[:, 1:P], locT[:, 0:P - 1], ALU.not_equal).then_inc(scan_step, 1)
                    dve.wait_ge(scan_step, 3 * g + 1)
                    nc.vector.tensor_scalar(drop[:, :], fresh[:, 0:P], -FAR, None, ALU.mult).then_inc(scan_step, 1)
                    dve.wait_ge(scan_step, 3 * g + 2)
                    dve.wait_ge(compat_turned, g + 1)
                    nc.vector.tensor_tensor_scan(run[:, :], drop[:, :], turn_ps[:, 1], -FAR, ALU.add, ALU.max).then_inc(scan_step, 1)
                    dve.wait_ge(scan_step, 3 * g + 3)
                    nc.vector.tensor_tensor(lasts[:, :], run[:, :], fresh[:, 1:P + 1], ALU.mult).then_inc(lasts_ready, 1)
                    nc.vector.tensor_scalar(before[:, :], maxima[:, bass.ds(block_of[0], 1), :].rearrange("p a h -> p (a h)"), 1.0, None, ALU.mult).then_inc(before_kept, 1)
                    dve.wait_ge(tops_ready, g + 1)
                    nc.vector.tensor_scalar(absent[:, :], tops[:, :, H], 0.5, -FAR, ALU.is_lt, ALU.mult).then_inc(absent_ready, 1)
                    dve.wait_ge(absent_ready, g + 1)
                    for t in range(G):
                        top = maxima[:, bass.ds(block_of[t], 1), :].rearrange("p a h -> p (a h)")
                        need(dve, maximum_taken, G * g + t)
                        nc.vector.scalar_tensor_tensor(top, tops[:, t, 0:H], absent[:, t:t + 1], top, ALU.add, ALU.max).then_inc(maximum_taken, 1)
                    dve.wait_ge(maximum_taken, G * (g + 1))
                    dve.wait_ge(before_kept, g + 1)
                    nc.vector.tensor_tensor(fall[:, :], before[:, :], maxima[:, bass.ds(block_of[0], 1), :].rearrange("p a h -> p (a h)"), ALU.subtract).then_inc(fall_ready, 1)
                    dve.wait_ge(maxima_spread, g + 1)
                    nc.vector.tensor_tensor(shifted[:, :, :], compat[:, :, :], spread_ps, ALU.subtract).then_inc(shift_done, 1)
                    dve.wait_ge(keep_ready, g + 1)
                    old = sums[:, bass.ds(block_of[0], 1), :]
                    need(dve, tile_added, G * g)
                    nc.vector.tensor_tensor(old[:, :, 0:DIM].rearrange("p a (h d) -> p (a h) d", h=H), old[:, :, 0:DIM].rearrange("p a (h d) -> p (a h) d", h=H), spread(keep[:, :], DV), ALU.mult).then_inc(scaled, 1)
                    nc.vector.tensor_tensor(old[:, :, DIM:].rearrange("p a h -> p (a h)"), old[:, :, DIM:].rearrange("p a h -> p (a h)"), keep[:, :], ALU.mult).then_inc(scaled, 1)
                    dve.wait_ge(exp_done, g + 1)
                    for t in range(G):
                        values = kv[:, h, t, DH:DH + DIM].rearrange("p (h d) -> p h d", h=H)
                        nc.vector.tensor_tensor(values, values, spread(kv[:, h, t, DH + DIM:], DV), ALU.mult).then_inc(weighted, 1)
                    dve.wait_ge(scaled, 2 * g + 2)
                    for t in range(G):
                        dve.wait_ge(tile_summed, G * g + t + 1)
                        need(dve, tile_added, G * g + t)
                        into = sums[:, bass.ds(block_of[t], 1), :].rearrange("p a n -> p (a n)")
                        nc.vector.tensor_tensor(into, into, sum_ps[t % 2][:, :], ALU.add).then_inc(tile_added, 1)
            rounds(dve, GROUPS // 2, body)

        @block.tensor
        def _(pe):
            pe.wait_ge(cleared, 4)
            pe.wait_ge(rpe_in, 64)

            def body(i):
                for h in range(2):
                    g = 2 * i + h
                    pe.wait_ge(rec_in[h], 32 * i + 32)
                    pe.wait_ge(hot_ready, g + 1)
                    for z in range(2):
                        need(pe, hot_copied, 2 * g + z)
                        for t in range(4):
                            last = nc.tensor.transpose(hotT_ps[:, t], hot[:, h, 4 * z + t], c["ident"][:, :])
                        last.then_inc(hot_turned, 1)
                        need(pe, rec_copied, 2 * g + z)
                        for t in range(4):
                            last = nc.tensor.transpose(recT_ps[0:ONE + 1, t], rec[:, h, 4 * z + t, 0:ONE + 1], c["ident"][:, :])
                        last.then_inc(rec_turned, 1)
                    pe.wait_ge(loc_spread, g + 1)
                    need(pe, lasts_ready, g)
                    nc.tensor.transpose(turn_ps[:, 0], loc16[:, :, :].rearrange("p t h -> p (t h)"), c["ident"][:, :]).then_inc(loc_turned, 1)
                    block_of = [pe.value_load(tile_block[0:1, h, t:t + 1], min_val=0, max_val=NB - 1) for t in range(G)]
                    for u in range(G // 2):
                        pe.wait_ge(rec_copied, 2 * g + u // 2 + 1)
                        pe.wait_ge(hot_copied, 2 * g + u // 2 + 1)
                        need(pe, pair_used, 4 * g + u - 1)
                        for w in range(2):
                            t = 2 * u + w
                            nc.tensor.matmul(qk_ps[u % 2][:, w, DH:], recT[:, t % 4], rpe[:, DH:], start=True, stop=True)
                            nc.tensor.matmul(qk_ps[u % 2][:, w, 0:DH], recT[:, t % 4], rpe[:, 0:DH], start=True, stop=False)
                            last = nc.tensor.matmul(qk_ps[u % 2][:, w, 0:DH], hotT[:, t], q_tab[:, bass.ds(block_of[t], 1), :].rearrange("p a d -> p (a d)"), start=False, stop=True)
                        last.then_inc(pair_ready, 1)
                    pe.wait_ge(compat_ready, g + 1)
                    pe.wait_ge(loc_copied, g + 1)
                    nc.tensor.transpose(turn_ps[:, 1], compat[:, :, :].rearrange("p t h -> p (t h)"), c["ident"][:, :]).then_inc(compat_turned, 1)
                    pe.wait_ge(lasts_ready, g + 1)
                    need(pe, shift_done, g)
                    nc.tensor.transpose(lastsT_ps, lasts[:, :], c["ident"][:, :]).then_inc(lasts_turned, 1)
                    pe.wait_ge(lasts_copied, g + 1)
                    for t in range(G):
                        last = nc.tensor.matmul(tops[:, t], hot[:, h, t], lastsT[:, t], start=True, stop=True)
                    last.then_inc(tops_ready, 1)
                    pe.wait_ge(maximum_taken, G * (g + 1))
                    for t in range(G):
                        last = nc.tensor.matmul(spread_ps[:, t], hotT[:, t], maxima[:, bass.ds(block_of[t], 1), :].rearrange("p a h -> p (a h)"), start=True, stop=True)
                    last.then_inc(maxima_spread, 1)
                    pe.wait_ge(exp_done, g + 1)
                    for t in range(G):
                        pe.wait_ge(weighted, G * g + t + 1)
                        need(pe, tile_added, G * g + t - 1)
                        nc.tensor.matmul(sum_ps[t % 2][:, :], hot[:, h, t], kv[:, h, t, DH:], start=True, stop=True).then_inc(tile_summed, 1)
            rounds(pe, GROUPS // 2, body)




class Norm:
    def __init__(self, nc, k):
        self.nc = nc
        self.rows = k.sb("rows", [P, 2, DIM])
        self.stats = k.sb("stats", [P, 2, 6])
        self.all_stats = k.sb("all_stats", [P, NB, 6])
        self.mean = k.sb("mean", [P, NB])
        self.scale = k.sb("scale", [P, NB])
        self.gap = k.sb("gap", [P, NB])
        self.between = k.sb("between", [P, NB])
        self.within = k.sb("within", [P, NB])
        self.scaling = k.sb("scaling", [P, 4, 2])
        self.rows_ready = k.sem("rows_ready")
        self.rows_kept = k.sem("rows_kept")
        self.stats_ready = k.sem("stats_ready")
        self.stats_kept = k.sem("stats_kept")
        self.step = k.sem("step")
        self.guarded = k.sem("guarded")
        self.rooted = k.sem("rooted")
        self.scaling_ready = k.sem("scaling_ready")

    def take(self, dve, g, h):
        dve.wait_ge(self.rows_ready, g + 1)
        self.nc.vector.bn_stats(self.stats[:, h], self.rows[:, h]).then_inc(self.stats_ready, 1)
        dve.wait_ge(self.stats_ready, g + 1)
        self.nc.vector.tensor_scalar(self.all_stats[:, bass.ds(g, 1), :].rearrange("p a w -> p (a w)"), self.stats[:, h], 1.0, None, ALU.mult).then_inc(self.stats_kept, 1)

    def keep(self, act, sums, g, h):
        act.wait_ge(self.rows_ready, g + 1)
        self.nc.scalar.activation(sums[:, bass.ds(g, 1), 0:DIM].rearrange("p a n -> p (a n)"), self.rows[:, h], ACT.Copy).then_inc(self.rows_kept, 1)

    def combine(self, dve):
        n = [0]

        def then(ins):
            n[0] += 1
            ins.then_inc(self.step, 1)
            dve.wait_ge(self.step, n[0])
        v = self.nc.vector
        m0, m1 = self.all_stats[:, :, 1], self.all_stats[:, :, 4]
        s0, s1 = self.all_stats[:, :, 2], self.all_stats[:, :, 5]
        dve.wait_ge(self.stats_kept, NB)
        then(v.tensor_tensor(self.mean[:, :], m0, m1, ALU.add))
        then(v.tensor_scalar(self.mean[:, :], self.mean[:, :], 0.5, None, ALU.mult))
        then(v.tensor_tensor(self.gap[:, :], m0, m1, ALU.subtract))
        then(v.tensor_scalar(self.gap[:, :], self.gap[:, :], 0.5, None, ALU.mult))
        then(v.tensor_tensor(self.between[:, :], self.gap[:, :], self.gap[:, :], ALU.mult))
        then(v.tensor_tensor(self.within[:, :], s0, s1, ALU.add))
        then(v.tensor_scalar(self.within[:, :], self.within[:, :], 1.0 / DIM, NORM_EPS, ALU.mult, ALU.add))
        v.tensor_tensor(self.within[:, :], self.within[:, :], self.between[:, :], ALU.add).then_inc(self.guarded, 1)
        dve.wait_ge(self.rooted, 1)
        then(v.reciprocal(self.scale[:, :], self.between[:, :]))

    def root(self, act):
        act.wait_ge(self.guarded, 1)
        self.nc.scalar.activation(self.between[:, :], self.within[:, :], ACT.Sqrt).then_inc(self.rooted, 1)

    def apply(self, dve, sums, g, h, out):
        v = self.nc.vector
        v.tensor_scalar(self.scaling[:, h, 0:1], self.mean[:, bass.ds(g, 1)], 1.0, None, ALU.mult).then_inc(self.scaling_ready, 1)
        v.tensor_scalar(self.scaling[:, h, 1:2], self.scale[:, bass.ds(g, 1)], 1.0, None, ALU.mult).then_inc(self.scaling_ready, 1)
        dve.wait_ge(self.scaling_ready, 2 * g + 2)
        return v.tensor_scalar(out, sums[:, bass.ds(g, 1), 0:DIM].rearrange("p a n -> p (a n)"),
                               self.scaling[:, h, 0:1], self.scaling[:, h, 1:2], ALU.subtract, ALU.mult)


def finish_attention(nc, k, c, x, sums, W_r, b_r, stalk, stalks_dram):
    norm = Norm(nc, k)
    xs = k.sb("xs", [P, 2, DIM])
    mixed = k.sb("mixed", [P, 2, DIM])
    inverse = k.sb("inverse", [P, 2, H])
    normal = k.sb("normal", [P, 2, DIM])
    normalT = k.sb("normalT", [P, 2, DIM])
    weight = k.sb("weight", [P, 2, STALK])
    bias = k.sb("bias", [1, STALK])
    one = k.sb("one", [1, P])
    normalT_ps = [k.ps(f"normalT_ps{h}", [P, DIM]) for h in range(2)]
    stalk_ps = [k.ps(f"stalk_ps{h}", [P, 512]) for h in range(2)]
    one_set = k.sem("one_set")
    weights_in = k.sem("weights_in")
    x_in = [k.sem(f"x_in{h}") for h in range(2)]
    den_step = k.sem("den_step")
    mix_step = k.sem("mix_step")
    normalised = k.sem("normalised")
    kept = k.sem("kept")
    turned = k.sem("turned")
    turned_copied = k.sem("turned_copied")
    stalked = k.sem("stalked")
    stalk_copied = k.sem("stalk_copied")
    stalks_out = k.sem("stalks_out")
    with nc.Block() as block:
        @block.sync
        def _(sp):
            sp.dma_start(weight[:, :, :], W_r.rearrange("(a p) n -> p a n", p=P)).then_inc(weights_in, 16)
            sp.dma_start(bias[:, :], b_r.rearrange("(a n) -> a n", a=1)).then_inc(weights_in, 16)

            def load(b, h, i, rows=P):
                need(sp, norm.rows_ready, 2 * i + h - 1)
                sp.dma_start(xs[0:rows, h, :], x[bass.ds(b * P, rows), :]).then_inc(x_in[h], 16)
            load(0, 0, 0)
            load(1, 1, 0)
            with sp.Fori(1, NB // 2 - 1) as i:
                for h in range(2):
                    load(2 * i + h, h, i)
            load(NB - 2, 0, NB // 2 - 1)
            load(NB - 1, 1, NB // 2 - 1, NLAST)
            sp.wait_ge(stalk_copied, NB)
            sp.dma_start(stalks_dram.rearrange("(b p) s -> p b s", p=P), stalk[:, :, :]).then_inc(stalks_out, 16)
            sp.wait_ge(stalks_out, 16)
            sp.wait_ge(weights_in, 32)

        @block.vector
        def _(dve):
            nc.vector.memset(one[:, :], 1.0).then_inc(one_set, 1)

            def mix(i):
                for h in range(2):
                    g = 2 * i + h
                    block_sums = sums[:, bass.ds(g, 1), :].rearrange("p a n -> p (a n)")
                    nc.vector.tensor_scalar(inverse[:, h], block_sums[:, DIM:], SOFT_EPS, None, ALU.add).then_inc(den_step, 1)
                    dve.wait_ge(den_step, 2 * g + 1)
                    nc.vector.reciprocal(inverse[:, h], inverse[:, h]).then_inc(den_step, 1)
                    dve.wait_ge(den_step, 2 * g + 2)
                    nc.vector.tensor_tensor(mixed[:, h].rearrange("p (h d) -> p h d", h=H),
                                            block_sums[:, 0:DIM].rearrange("p (h d) -> p h d", h=H), spread(inverse[:, h], DV), ALU.mult).then_inc(mix_step, 1)
                    dve.wait_ge(mix_step, g + 1)
                    dve.wait_ge(x_in[h], 16 * i + 16)
                    need(dve, norm.rows_kept, g - 1)
                    nc.vector.tensor_tensor(norm.rows[:, h], mixed[:, h], xs[:, h], ALU.add).then_inc(norm.rows_ready, 1)
                    norm.take(dve, g, h)
            rounds(dve, NB // 2, mix)
            norm.combine(dve)
            dve.wait_ge(norm.rows_kept, NB)

            def normalise(i):
                for h in range(2):
                    g = 2 * i + h
                    need(dve, turned, g - 1)
                    need(dve, kept, g - 1)
                    norm.apply(dve, sums, g, h, normal[:, h]).then_inc(normalised, 1)
            rounds(dve, NB // 2, normalise)

        @block.scalar
        def _(act):
            def keep(i):
                for h in range(2):
                    norm.keep(act, sums, 2 * i + h, h)
            rounds(act, NB // 2, keep)
            norm.root(act)

            def body(i):
                for h in range(2):
                    g = 2 * i + h
                    act.wait_ge(normalised, g + 1)
                    nc.scalar.activation(sums[:, bass.ds(g, 1), 0:DIM].rearrange("p a n -> p (a n)"), normal[:, h], ACT.Copy).then_inc(kept, 1)
                    act.wait_ge(turned, g + 1)
                    need(act, stalked, g - 1)
                    nc.scalar.activation(normalT[:, h], normalT_ps[h][:, :], ACT.Copy).then_inc(turned_copied, 1)
                    act.wait_ge(stalked, g + 1)
                    nc.scalar.activation(stalk[:, bass.ds(g, 1), :].rearrange("p a s -> p (a s)"), stalk_ps[h][:, 0:STALK], ACT.Copy).then_inc(stalk_copied, 1)
            rounds(act, NB // 2, body)
            act.wait_ge(kept, NB)

        @block.tensor
        def _(pe):
            pe.wait_ge(weights_in, 32)
            pe.wait_ge(one_set, 1)

            def body(i):
                for h in range(2):
                    g = 2 * i + h
                    pe.wait_ge(normalised, g + 1)
                    need(pe, turned_copied, g - 1)
                    for a in range(2):
                        last = nc.tensor.transpose(normalT_ps[h][:, a * P:(a + 1) * P], normal[:, h, a * P:(a + 1) * P], c["ident"][:, :])
                    last.then_inc(turned, 1)
                    pe.wait_ge(turned_copied, g + 1)
                    need(pe, stalk_copied, g - 1)
                    for a in range(2):
                        nc.tensor.matmul(stalk_ps[h][:, 0:STALK], normalT[:, h, a * P:(a + 1) * P], weight[:, a], start=(a == 0), stop=False)
                    nc.tensor.matmul(stalk_ps[h][:, 0:STALK], one[:, :], bias[:, :], start=False, stop=True).then_inc(stalked, 1)
            rounds(pe, NB // 2, body)


def diffuse(nc, k, c, stalk, stalks_dram, rec_dram, blocks_dram, flow):
    rec = k.sb("rec", [P, 2, G, REC])
    tile_block = k.sb("tile_block", [1, 2, G], I32)
    far = k.sb("far", [P, 2, G, STALK])
    dst_at = k.sb("dst_at", [P, G], I32)
    dst_of = k.sb("dst_of", [P, G], I32)
    at = k.sb("at", [P, G])
    of = k.sb("of", [P, 2, G])
    hot = k.sb("hot", [P, G, P])
    hotT = k.sb("hotT", [P, G, P])
    dst_hot = k.sb("dst_hot", [P, 2, G, P])
    differs = k.sb("differs", [P, 2, G, STALK])
    zero_mat = k.sb("zero_mat", [P, P])
    placed = k.sb("placed", [P, 4, STALK, NB])
    hotT_ps = [k.ps(f"hotT_ps{z}", [P, 4, P]) for z in range(2)]
    near_ps = k.ps("near_ps", [P, 512])
    near = near_ps[:, 0:G * STALK].rearrange("p (t s) -> p t s", t=G)
    out_ps = [k.ps(f"out_ps{h}", [P, 512]) for h in range(2)]
    into_ps = k.ps("into_ps", [P, STALK, NB])
    cleared = k.sem("cleared")
    rec_in = [k.sem(f"rec_in{h}") for h in range(2)]
    gathered = [k.sem(f"gathered{h}") for h in range(2)]
    pool_turn = k.sem("pool_turn")
    hot_ready = k.sem("hot_ready")
    hot_turned = k.sem("hot_turned")
    hot_copied = k.sem("hot_copied")
    dst_step = k.sem("dst_step")
    dst_hot_ready = k.sem("dst_hot_ready")
    near_ready = k.sem("near_ready")
    differ_ready = k.sem("differ_ready")
    placed_ready = k.sem("placed_ready")
    tile_into = k.sem("tile_into")
    out_ready = k.sem("out_ready")
    taken = k.sem("taken")
    all_into = k.sem("all_into")
    with nc.Block() as block:
        @block.sync
        def _(sp):
            def body(i):
                for h in range(2):
                    g = 2 * i + h
                    need(sp, differ_ready, g - 1)
                    sp.dma_start(rec[:, h, :, :], rec_dram[bass.ds(g * G * P, G * P), :].rearrange("(p t) w -> p t w", t=G)).then_inc(rec_in[h], 16)
                    sp.dma_start(tile_block[:, h, :], blocks_dram[bass.ds(g * G, G)].rearrange("(a t) -> a t", a=1)).then_inc(rec_in[h], 16)
            rounds(sp, GROUPS // 2, body)

        @block.gpsimd
        def _(pool):
            def body(i):
                for h in range(2):
                    g = 2 * i + h
                    pool.wait_ge(rec_in[h], 32 * i + 32)
                    pool.sem_inc(pool_turn)
                    if not (isinstance(i, int) and i == 0):
                        pool.wait_ge(differ_ready, g - 1)
                        pool.sem_inc(pool_turn)
                    for t in range(G):
                        nc.gpsimd.indirect_dma_start(far[:, h, t], None, stalks_dram[:, :],
                                                     bass.IndirectOffsetOnAxis(ap=rec[:, h, t, DST:DST + 1].bitcast(I32), axis=0)).then_inc(gathered[h], 16)
            rounds(pool, GROUPS // 2, body)

        @block.vector
        def _(dve):
            nc.vector.memset(flow[:, :, :], 0.0).then_inc(cleared, 1)
            nc.vector.memset(zero_mat[:, :], 0.0).then_inc(cleared, 1)
            dve.wait_ge(cleared, 2)

            def take(g, h, block_of):
                for t in range(G):
                    if t == 0:
                        dve.wait_ge(out_ready, g + 1)
                    need(dve, taken, G * g + t)
                    into = flow[:, bass.ds(block_of[t], 1), :].rearrange("p a s -> p (a s)")
                    nc.vector.tensor_tensor(into, into, out_ps[h][:, t * STALK:(t + 1) * STALK], ALU.subtract).then_inc(taken, 1)

            def body(i):
                for h in range(2):
                    g = 2 * i + h
                    dve.wait_ge(rec_in[h], 32 * i + 32)
                    need(dve, out_ready, g)
                    nc.vector.tensor_tensor(hot[:, :], over(c["row"][:, :], G), spread(rec[:, h, :, LOC], P), ALU.is_equal).then_inc(hot_ready, 1)
                    block_of = [dve.value_load(tile_block[0:1, h, t:t + 1], min_val=0, max_val=NB - 1) for t in range(G)]
                    need(dve, tile_into, G * (g - 1))
                    nc.vector.tensor_scalar(dst_at[:, :], rec[:, h, :, DST].bitcast(I32), P - 1, None, ALU.bitwise_and).then_inc(dst_step, 1)
                    nc.vector.tensor_scalar(dst_of[:, :], rec[:, h, :, DST].bitcast(I32), 7, None, ALU.logical_shift_right).then_inc(dst_step, 1)
                    dve.wait_ge(dst_step, 4 * g + 2)
                    nc.vector.tensor_copy(at[:, :], dst_at[:, :]).then_inc(dst_step, 1)
                    nc.vector.tensor_copy(of[:, h], dst_of[:, :]).then_inc(dst_step, 1)
                    dve.wait_ge(dst_step, 4 * g + 4)
                    nc.vector.tensor_tensor(dst_hot[:, h], over(c["row"][:, :], G), spread(at[:, :], P), ALU.is_equal).then_inc(dst_hot_ready, 1)
                    dve.wait_ge(near_ready, g + 1)
                    dve.wait_ge(gathered[h], 16 * G * (i + 1))
                    nc.vector.tensor_tensor(differs[:, h], far[:, h], near, ALU.subtract).then_inc(differ_ready, 1)
                    dve.wait_ge(differ_ready, g + 1)
                    for t in range(G):
                        need(dve, tile_into, G * g + t - 3)
                        nc.vector.scalar_tensor_tensor(placed[:, t % 4], over(c["row"][:, 0:NB], STALK), of[:, h, t:t + 1],
                                                       spread(differs[:, h, t], NB), ALU.is_equal, ALU.mult).then_inc(placed_ready, 1)
                    take(g, h, block_of)
            rounds(dve, GROUPS // 2, body)
            dve.wait_ge(all_into, 1)
            dve.wait_ge(taken, ST)
            nc.vector.tensor_tensor(flow[:, :, :], flow[:, :, :], into_ps[:, :, :].rearrange("p s b -> p b s"), ALU.add).then_inc(cleared, 1)

        @block.scalar
        def _(act):
            def body(i):
                for h in range(2):
                    g = 2 * i + h
                    for z in range(2):
                        act.wait_ge(hot_turned, 2 * g + z + 1)
                        need(act, near_ready, g)
                        nc.scalar.activation(hotT[:, 4 * z:4 * z + 4], hotT_ps[z][:, :, :], ACT.Copy).then_inc(hot_copied, 1)
            rounds(act, GROUPS // 2, body)

        @block.tensor
        def _(pe):
            pe.wait_ge(cleared, 2)
            nc.tensor.matmul(into_ps[:, :, :], zero_mat[:, :], c["row"][:, 0:1].to_broadcast([P, STALK * NB]), start=True, stop=False)

            def body(i):
                for h in range(2):
                    g = 2 * i + h
                    pe.wait_ge(hot_ready, g + 1)
                    for z in range(2):
                        need(pe, hot_copied, 2 * (g - 1) + z + 1)
                        for t in range(4):
                            last = nc.tensor.transpose(hotT_ps[z][:, t], hot[:, 4 * z + t], c["ident"][:, :])
                        last.then_inc(hot_turned, 1)
                    block_of = [pe.value_load(tile_block[0:1, h, t:t + 1], min_val=0, max_val=NB - 1) for t in range(G)]
                    need(pe, differ_ready, g)
                    for t in range(G):
                        if t % 4 == 0:
                            pe.wait_ge(hot_copied, 2 * g + t // 4 + 1)
                        last = nc.tensor.matmul(near[:, t], hotT[:, t], stalk[:, bass.ds(block_of[t], 1), :].rearrange("p a s -> p (a s)"), start=True, stop=True)
                    last.then_inc(near_ready, 1)
                    pe.wait_ge(differ_ready, g + 1)
                    need(pe, taken, G * (g - 1))
                    for t in range(G):
                        last = nc.tensor.matmul(out_ps[h][:, t * STALK:(t + 1) * STALK], hot[:, t], differs[:, h, t], start=True, stop=True)
                    last.then_inc(out_ready, 1)
                    pe.wait_ge(dst_hot_ready, g + 1)
                    for t in range(G):
                        pe.wait_ge(placed_ready, G * g + t + 1)
                        nc.tensor.matmul(into_ps[:, :, :], dst_hot[:, h, t], placed[:, t % 4], start=False, stop=False).then_inc(tile_into, 1)
            rounds(pe, GROUPS // 2, body)
            nc.tensor.matmul(into_ps[:, :, :], zero_mat[:, :], c["row"][:, 0:1].to_broadcast([P, STALK * NB]), start=False, stop=True).then_inc(all_into, 1)


def finish(nc, k, c, sums, flow, W_o, b_o, out):
    norm = Norm(nc, k)
    weight = k.sb("weight", [STALK + 1, DIM])
    flows = k.sb("flows", [P, 2, STALK + 1])
    flowT = k.sb("flowT", [STALK + 1, 2, P])
    bent = k.sb("bent", [P, 2, DIM])
    normal = k.sb("normal", [P, 4, DIM])
    flowT_ps = [k.ps(f"flowT_ps{h}", [P, 512]) for h in range(2)]
    wide_ps = [k.ps(f"wide_ps{h}", [P, 512]) for h in range(2)]
    one_set = k.sem("one_set")
    weights_in = k.sem("weights_in")
    flow_copied = k.sem("flow_copied")
    turned = k.sem("turned")
    turned_copied = k.sem("turned_copied")
    widened = k.sem("widened")
    bent_ready = k.sem("bent_ready")
    normalised = k.sem("normalised")
    rows_out = [k.sem(f"rows_out{h}") for h in range(2)]
    HALF = NB // 2
    with nc.Block() as block:
        @block.sync
        def _(sp):
            sp.dma_start(weight[0:STALK, :], W_o).then_inc(weights_in, 16)
            sp.dma_start(weight[STALK:STALK + 1, :], b_o.rearrange("(a n) -> a n", a=1)).then_inc(weights_in, 16)

            def store(b, h, g, rows=P):
                sp.wait_ge(normalised, g + 1)
                sp.dma_start(out[bass.ds(b * P, rows), :], normal[0:rows, h]).then_inc(rows_out[h], 16)
            with sp.Fori(0, HALF - 1) as i:
                for h in range(2):
                    store(2 * i + h, h, 2 * i + h)
            store(NB - 2, 0, NB - 2)
            store(NB - 1, 1, NB - 1, NLAST)
            sp.wait_ge(rows_out[0], 16 * HALF)
            sp.wait_ge(rows_out[1], 16 * HALF)
            sp.wait_ge(weights_in, 32)

        @block.vector
        def _(dve):
            nc.vector.memset(flows[:, :, STALK:], 1.0).then_inc(one_set, 1)

            def lend(g, h):
                need(dve, turned, g - 1)
                nc.vector.tensor_scalar(flows[:, h, 0:STALK], flow[:, bass.ds(g, 1), :].rearrange("p a s -> p (a s)"), 1.0, None, ALU.mult).then_inc(flow_copied, 1)

            def add(i):
                for h in range(2):
                    g = 2 * i + h
                    lend(g, h)
                    dve.wait_ge(bent_ready, g + 1)
                    rows = sums[:, bass.ds(g, 1), 0:DIM].rearrange("p a n -> p (a n)")
                    need(dve, norm.rows_kept, g - 1)
                    nc.vector.tensor_tensor(norm.rows[:, h], rows, bent[:, h], ALU.add).then_inc(norm.rows_ready, 1)
                    norm.take(dve, g, h)
            rounds(dve, HALF, add)
            norm.combine(dve)
            dve.wait_ge(norm.rows_kept, NB)

            def normalise(i):
                for h in range(2):
                    g = 2 * i + h
                    need(dve, rows_out[h], 16 * i)
                    norm.apply(dve, sums, g, h, normal[:, h]).then_inc(normalised, 1)
            rounds(dve, HALF, normalise)

        @block.scalar
        def _(act):
            def body(i):
                for h in range(2):
                    g = 2 * i + h
                    act.wait_ge(turned, g + 1)
                    need(act, widened, g - 1)
                    nc.scalar.activation(flowT[:, h], flowT_ps[h][0:STALK + 1, 0:P], ACT.Copy).then_inc(turned_copied, 1)
                    act.wait_ge(widened, g + 1)
                    need(act, norm.rows_ready, g - 1)
                    nc.scalar.activation(bent[:, h], wide_ps[h][:, 0:DIM], ACT.Gelu).then_inc(bent_ready, 1)
                    norm.keep(act, sums, g, h)
            rounds(act, HALF, body)
            norm.root(act)

        @block.tensor
        def _(pe):
            pe.wait_ge(weights_in, 32)
            pe.wait_ge(one_set, 1)

            def body(i):
                for h in range(2):
                    g = 2 * i + h
                    pe.wait_ge(flow_copied, g + 1)
                    need(pe, turned_copied, g - 1)
                    nc.tensor.transpose(flowT_ps[h][0:STALK + 1, 0:P], flows[:, h], c["ident"][:, :]).then_inc(turned, 1)
                    pe.wait_ge(turned_copied, g + 1)
                    need(pe, bent_ready, g - 1)
                    nc.tensor.matmul(wide_ps[h][:, 0:DIM], flowT[:, h], weight[:, :], start=True, stop=True).then_inc(widened, 1)
            rounds(pe, HALF, body)


def graph_network(nc, x, src, dst, edge_attr, Wqkv, bqkv, Wk_rpe, bk_rpe, Wq_rpe, bq_rpe, W_r, b_r, W_o, b_o, out, scratch):
    kv_dram, rec_dram, blocks_dram, stalks_dram = scratch
    with ExitStack() as whole:
        k = Room(nc, whole, "all")
        c = {name: k.sb(name, [P, P]) for name in ("ident", "row")}
        q_tab = k.sb("q_tab", [P, NB, DH])
        with ExitStack() as sorting:
            s = Room(nc, sorting, "sorting")
            c.update({name: s.sb(name, [P, P]) for name in ("ones", "zeros", "before", "after")})
            c.update({name: s.sb(name, [P, P], BF16) for name in ("ident_bf", "zeros_bf", "row_bf")})
            c["row_i"] = s.sb("row_i", [P, P], I32)
            e = {"src": s.sb("src", [P, NCH, CT], I32), "dst": s.sb("dst", [P, NCH, CT], I32)}
            e.update({name: s.sb(name, [P, NCH * CT]) for name in ("src_f", "at", "of")})
            counts = s.sb("counts", [P, NB])
            base = s.sb("base", [P, NB])
            with ExitStack() as stage:
                constants(nc, Room(nc, stage, "const"), c)
            with ExitStack() as stage:
                project_and_count(nc, Room(nc, stage, "project"), c, x, src, dst, Wqkv, bqkv, e, q_tab, kv_dram, rec_dram, counts)
            with ExitStack() as stage:
                place_nodes(nc, Room(nc, stage, "place"), c, counts, base, blocks_dram)
            with ExitStack() as stage:
                sort_edges(nc, Room(nc, stage, "sort"), c, e, edge_attr, base, rec_dram)
        sums = k.sb("sums", [P, NB, DIM + H])
        with ExitStack() as stage:
            attend(nc, Room(nc, stage, "attend"), c, Wk_rpe, bk_rpe, Wq_rpe, bq_rpe, q_tab, kv_dram, rec_dram, blocks_dram, sums)
        stalk = k.sb("stalk", [P, NB, STALK])
        flow = k.sb("flow", [P, NB, STALK])
        with ExitStack() as stage:
            finish_attention(nc, Room(nc, stage, "settle"), c, x, sums, W_r, b_r, stalk, stalks_dram)
        with ExitStack() as stage:
            diffuse(nc, Room(nc, stage, "diffuse"), c, stalk, stalks_dram, rec_dram, blocks_dram, flow)
        with ExitStack() as stage:
            finish(nc, Room(nc, stage, "finish"), c, sums, flow, W_o, b_o, out)


_INS = ['x', 'src', 'dst', 'edge_attr_18', 'L0_gnn_Wqkv', 'L0_gnn_bqkv', 'L0_gnn_Wk_rpe', 'L0_gnn_bk_rpe',
        'L0_gnn_Wq_rpe', 'L0_gnn_bq_rpe', 'L1_gnn_W_r', 'L1_gnn_b_r', 'L1_gnn_W_o', 'L1_gnn_b_o']
_OUTS = [((N, DIM), 'float32')]
_SCRATCH = [("kv", (NB * P, DH + DIM), 'float32'), ("records", (ST * P, REC), 'float32'),
            ("tile_blocks", (ST,), 'int32'), ("stalks", (NB * P, STALK), 'float32')]


def kernel(**inputs):
    import numpy as _np
    import concourse.bacc as _bacc
    from concourse import mybir as _mybir
    from concourse.bass_utils import run_bass_kernel_spmd as _run

    nc = _bacc.Bacc("TRN2", target_bir_lowering=False, num_devices=1)
    arrays, args = {}, []
    for name in _INS:
        a = _np.ascontiguousarray(inputs[name])
        arrays[f"in_{name}_dram"] = a
        args.append(nc.dram_tensor(f"in_{name}_dram", a.shape, _mybir.dt.from_np(a.dtype), kind="ExternalInput").ap())
    for i, (shape, dtype) in enumerate(_OUTS):
        args.append(nc.dram_tensor(f"out_{i}_dram", shape, _mybir.dt.from_np(_np.dtype(dtype)), kind="ExternalOutput").ap())
    scratch = [nc.dram_tensor(f"{name}_dram", shape, _mybir.dt.from_np(_np.dtype(dtype)), kind="Internal").ap()
               for name, shape, dtype in _SCRATCH]
    graph_network(nc, *args, scratch)
    r = _run(nc, [arrays], core_ids=[0])
    return r.results[0]["out_0_dram"]
```

```python
import concourse.bass as bass
from concourse import mybir
from concourse.alu_op_type import AluOpType as ALU
from contextlib import ExitStack

F32 = mybir.dt.float32
BF16 = mybir.dt.bfloat16
I32 = mybir.dt.int32
ACT = mybir.ActivationFunctionType
AX = mybir.AxisListType

P = 128
N, E = 12500, 200000
DIM, H, D, RPE, STALK = 256, 16, 8, 18, 4
DH, DV = H * D, DIM // H
HV = DV + 1
NB = -(-N // P)
NLAST = N - (NB - 1) * P
SCALE = float(D) ** -0.5
SOFT_EPS, NORM_EPS = 1e-16, 1e-5
FAR = 1e30

CT = 16
FULL = E // (P * CT)
NCH = NB
LAST_T = 12
LAST_P = (E - FULL * P * CT) // LAST_T
assert FULL + 1 == NCH and LAST_P * LAST_T + FULL * P * CT == E

G = 8
GROUPS = 6 * -(-((E + (P - 1) * NB) // P) // (6 * G))
ST = G * GROUPS
TPP = -(-ST // P)
ATT = RPE + 1
LOC = (3 * ATT + 1) // 2
DST = LOC + 1
REC = DST + 1
BLANK = 56
assert ST % BLANK == 0
assert NB * P > N


def need(engine, sem, count):
    if not (isinstance(count, int) and count <= 0):
        engine.wait_ge(sem, count)


def rounds(engine, n, body):
    body(0)
    with engine.Fori(1, n) as i:
        body(i)


def rounds_ahead(engine, n, body):
    body(0, False)
    with engine.Fori(1, n - 1) as i:
        body(i, False)
    body(n - 1, True)


class Room:
    def __init__(self, nc, stack, stage):
        self.nc, self.stack, self.stage = nc, stack, stage

    def sb(self, name, shape, dt=F32):
        return self.stack.enter_context(self.nc.sbuf_tensor(f"{self.stage}_{name}", shape, dt))

    def ps(self, name, shape, dt=F32):
        return self.stack.enter_context(self.nc.psum_tensor(f"{self.stage}_{name}", shape, dt))

    def sem(self, name):
        return self.stack.enter_context(self.nc.semaphore(f"{self.stage}_{name}"))


def constants(nc, k, c):
    built = k.sem("built")
    counted = k.sem("counted")
    with nc.Block() as block:
        @block.gpsimd
        def _(pool):
            nc.gpsimd.memset(c["ones"][:, :], 1.0).then_inc(built, 1)
            nc.gpsimd.memset(c["zeros"][:, :], 0.0).then_inc(built, 1)
            nc.gpsimd.iota(c["row_i"][:, :], [[1, P]], base=0, channel_multiplier=0).then_inc(counted, 1)
            pool.wait_ge(built, 2)
            nc.gpsimd.affine_select(out=c["ident"][:, :], in_=c["zeros"][:, :], compare_op=ALU.not_equal,
                                    fill=1.0, base=0, pattern=[[-1, P]], channel_multiplier=1).then_inc(built, 1)
            nc.gpsimd.affine_select(out=c["before"][:, :], in_=c["ones"][:, :], compare_op=ALU.is_gt,
                                    fill=0.0, base=0, pattern=[[1, P]], channel_multiplier=-1).then_inc(built, 1)
            nc.gpsimd.affine_select(out=c["after"][:, :], in_=c["ones"][:, :], compare_op=ALU.is_gt,
                                    fill=0.0, base=0, pattern=[[-1, P]], channel_multiplier=1).then_inc(built, 1)
            pool.wait_ge(built, 5)

        @block.vector
        def _(dve):
            dve.wait_ge(counted, 1)
            nc.vector.tensor_copy(c["row"][:, :], c["row_i"][:, :]).then_inc(counted, 1)
            nc.vector.tensor_copy(c["row_bf"][:, :], c["row_i"][:, :])
            dve.wait_ge(built, 5)
            nc.vector.tensor_copy(c["ident_bf"][:, :], c["ident"][:, :])
            nc.vector.tensor_copy(c["zeros_bf"][:, :], c["zeros"][:, :])


def spread(ap, n):
    p, a = ap.shape
    return ap.unsqueeze(2).to_broadcast([p, a, n])


def over(ap, n):
    p, a = ap.shape
    return ap.unsqueeze(1).to_broadcast([p, n, a])


def project_and_count(nc, k, c, x, src, dst, Wqkv, bqkv, e, q_dram, kv_dram, rec_dram, counts):
    w = k.sb("w", [P, 2, DH * 2 + DIM])
    bias = k.sb("bias", [1, DH * 2 + DIM])
    xs = k.sb("x", [P, 2, DIM])
    xT = k.sb("xT", [P, 2, DIM])
    q = k.sb("q", [P, 2, DH])
    kv = k.sb("kv", [P, 2, DH + DIM])
    blank = k.sb("blank", [P, BLANK, REC])
    scratch = k.sb("scratch", [P, NCH * CT], I32)
    scratch2 = k.sb("scratch2", [P, NCH * CT], I32)
    at_bf = k.sb("at_bf", [P, NCH * CT], BF16)
    of_bf = k.sb("of_bf", [P, NCH * CT], BF16)
    hot_p = k.sb("hot_p", [P, 2, CT, P], BF16)
    hot_b = k.sb("hot_b", [P, 2, CT, NB], BF16)
    xT_ps = [k.ps(f"xT_ps{h}", [P, DIM]) for h in range(2)]
    qkv_ps = [k.ps(f"qkv_ps{h}", [P, DH * 2 + DIM]) for h in range(2)]
    count_ps = k.ps("count_ps", [P, NB])
    padded = k.sem("padded")
    weights_in = k.sem("weights_in")
    edges_in = k.sem("edges_in")
    x_in = [k.sem(f"x_in{h}") for h in range(2)]
    transposed = k.sem("transposed")
    xT_copied = k.sem("xT_copied")
    projected = k.sem("projected")
    q_copied = k.sem("q_copied")
    kv_copied = k.sem("kv_copied")
    rows_out = [k.sem(f"rows_out{h}") for h in range(2)]
    blanks_out = k.sem("blanks_out")
    index_step = k.sem("index_step")
    hot_ready = k.sem("hot_ready")
    counted = k.sem("counted")
    all_counted = k.sem("all_counted")
    BLANKS = ST // BLANK

    with nc.Block() as block:
        @block.gpsimd
        def _(pool):
            nc.gpsimd.memset(e["src"][:, NCH - 1, :], -1).then_inc(padded, 1)
            nc.gpsimd.memset(e["dst"][:, NCH - 1, :], 0).then_inc(padded, 1)
            nc.gpsimd.memset(blank[:, :, :], 0.0).then_inc(padded, 1)
            pool.wait_ge(padded, 3)
            nc.gpsimd.memset(blank[:, :, LOC:LOC + 1], -1.0).then_inc(padded, 1)
            nc.gpsimd.memset(blank[:, :, DST:DST + 1].bitcast(I32), NB * P - 1).then_inc(padded, 1)

        @block.sync
        def _(sp):
            edges = [(e["src"], src), (e["dst"], dst)]
            sp.dma_start(e["src"][:, 0:FULL, :], src[0:FULL * P * CT].rearrange("(c p j) -> p c j", p=P, j=CT)).then_inc(edges_in, 16)
            sp.wait_ge(padded, 5)
            for to, of in edges:
                sp.dma_start(to[0:LAST_P, NCH - 1, 0:LAST_T],
                             of[FULL * P * CT:E].rearrange("(p j) -> p j", j=LAST_T)).then_inc(edges_in, 16)
            sp.dma_start(w[:, :, :], Wqkv.rearrange("(a p) n -> p a n", p=P)).then_inc(weights_in, 16)
            sp.dma_start(bias[:, :], bqkv.rearrange("(a n) -> a n", a=1)).then_inc(weights_in, 16)
            sp.dma_start(e["dst"][:, 0:FULL, :], dst[0:FULL * P * CT].rearrange("(c p j) -> p c j", p=P, j=CT)).then_inc(edges_in, 16)

            def load(b, h, i, rows=P):
                need(sp, transposed, 2 * i + h - 1)
                sp.dma_start(xs[0:rows, h, :], x[bass.ds(b * P, rows), :]).then_inc(x_in[h], 16)
            load(0, 0, 0)
            load(1, 1, 0)
            with sp.Fori(1, NB // 2 - 1) as i:
                for h in range(2):
                    load(2 * i + h, h, i)
            load(NB - 2, 0, NB // 2 - 1)
            load(NB - 1, 1, NB // 2 - 1, NLAST)
            for n in range(BLANKS):
                sp.dma_start(rec_dram[n * P * BLANK:(n + 1) * P * BLANK, :].rearrange("(p r) w -> p r w", p=P),
                             blank[:, :, :]).then_inc(blanks_out, 16)
            sp.wait_ge(blanks_out, 16 * BLANKS)
            sp.wait_ge(edges_in, 64)

        @block.vector
        def _(dve):
            dve.wait_ge(edges_in, 64)
            flat = e["src"][:, :, :].rearrange("p c j -> p (c j)")
            nc.vector.tensor_copy(e["src_f"][:, :], flat).then_inc(index_step, 1)
            nc.vector.tensor_scalar(scratch[:, :], flat, P - 1, None, ALU.bitwise_and).then_inc(index_step, 1)
            nc.vector.tensor_scalar(scratch2[:, :], flat, 7, None, ALU.arith_shift_right).then_inc(index_step, 1)
            dve.wait_ge(index_step, 3)
            nc.vector.tensor_copy(at_bf[:, :], scratch[:, :]).then_inc(index_step, 1)
            nc.vector.tensor_copy(of_bf[:, :], scratch2[:, :]).then_inc(index_step, 1)
            nc.vector.tensor_copy(e["at"][:, :], scratch[:, :])
            nc.vector.tensor_copy(e["of"][:, :], scratch2[:, :])
            dve.wait_ge(index_step, 5)

            def body(i):
                for h in range(2):
                    g = 2 * i + h
                    need(dve, counted, g - 1)
                    nc.vector.tensor_tensor(hot_p[:, h], over(c["row_bf"][:, :], CT),
                                            spread(at_bf[:, bass.ds(g * CT, CT)], P), ALU.is_equal).then_inc(hot_ready, 1)
                    nc.vector.tensor_tensor(hot_b[:, h], over(c["row_bf"][:, 0:NB], CT),
                                            spread(of_bf[:, bass.ds(g * CT, CT)], NB), ALU.is_equal).then_inc(hot_ready, 1)
            rounds(dve, NCH // 2, body)

        @block.tensor
        def _(pe):
            pe.wait_ge(weights_in, 32)
            nc.tensor.matmul(count_ps[:, :], c["zeros_bf"][:, :], c["zeros_bf"][:, 0:NB], start=True, stop=False)

            def body(i):
                for h in range(2):
                    g = 2 * i + h
                    pe.wait_ge(x_in[h], 16 * i + 16)
                    need(pe, xT_copied, g - 1)
                    for a in range(2):
                        last = nc.tensor.transpose(xT_ps[h][:, a * P:(a + 1) * P], xs[:, h, a * P:(a + 1) * P], c["ident"][:, :])
                    last.then_inc(transposed, 1)
                    pe.wait_ge(hot_ready, 2 * g + 2)
                    for j in range(CT):
                        last = nc.tensor.matmul(count_ps[:, :], hot_p[:, h, j], hot_b[:, h, j], start=False, stop=False)
                    last.then_inc(counted, 1)
                    pe.wait_ge(xT_copied, g + 1)
                    need(pe, kv_copied, g - 1)
                    for a in range(2):
                        nc.tensor.matmul(qkv_ps[h][:, :], xT[:, h, a * P:(a + 1) * P], w[:, a], start=(a == 0), stop=False)
                    nc.tensor.matmul(qkv_ps[h][:, :], c["ones"][0:1, :], bias[0:1, :], start=False, stop=True).then_inc(projected, 1)
            rounds(pe, NB // 2, body)
            nc.tensor.matmul(count_ps[:, :], c["zeros_bf"][:, :], c["zeros_bf"][:, 0:NB], start=False, stop=True).then_inc(all_counted, 1)

        @block.scalar
        def _(act):
            def body(i):
                for h in range(2):
                    g = 2 * i + h
                    act.wait_ge(transposed, g + 1)
                    need(act, projected, g - 1)
                    nc.scalar.activation(xT[:, h, :], xT_ps[h][:, :], ACT.Copy).then_inc(xT_copied, 1)
                    act.wait_ge(projected, g + 1)
                    need(act, rows_out[h], 32 * i)
                    nc.scalar.activation(q[:, h, :], qkv_ps[h][:, 0:DH], ACT.Copy, scale=SCALE).then_inc(q_copied, 1)
                    nc.scalar.activation(kv[:, h, :], qkv_ps[h][:, DH:], ACT.Copy).then_inc(kv_copied, 1)
                    act.wait_ge(q_copied, g + 1)
                    act.dma_start(q_dram[bass.ds(g, 1), :, :].rearrange("a p d -> p (a d)"), q[:, h, :]).then_inc(rows_out[h], 16)
                    act.wait_ge(kv_copied, g + 1)
                    act.dma_start(kv_dram[bass.ds(g * P, P), :], kv[:, h, :]).then_inc(rows_out[h], 16)
            rounds(act, NB // 2, body)
            act.wait_ge(all_counted, 1)
            nc.scalar.activation(counts[:, :], count_ps[:, :], ACT.Copy).then_inc(all_counted, 1)
            for h in range(2):
                act.wait_ge(rows_out[h], 32 * (NB // 2))
            act.wait_ge(all_counted, 2)


def place_nodes(nc, k, c, counts, base, blocks_dram):
    within = k.ps("within", [P, NB])
    total = k.ps("total", [P, NB])
    filled = k.sb("filled", [P, NB])
    filled_i = k.sb("filled_i", [P, NB], I32)
    tiles_i = k.sb("tiles_i", [P, NB], I32)
    tiles = k.sb("tiles", [P, NB])
    ends = k.sb("ends", [P, NB])
    starts = k.sb("starts", [P, NB])
    number_i = k.sb("number_i", [P, TPP], I32)
    number = k.sb("number", [P, TPP])
    passed = k.sb("passed", [P, TPP, NB])
    block_f = k.sb("block_f", [P, TPP])
    block_i = k.sb("block_i", [P, TPP], I32)
    summed = k.sem("summed")
    numbered = k.sem("numbered")
    step = k.sem("step")
    found = k.sem("found")
    blocks_out = k.sem("blocks_out")
    with nc.Block() as block:
        @block.gpsimd
        def _(pool):
            nc.gpsimd.iota(number_i[:, :], [[1, TPP]], base=0, channel_multiplier=TPP).then_inc(numbered, 1)

        @block.tensor
        def _(pe):
            nc.tensor.matmul(within[:, :], c["before"][:, :], counts[:, :], start=True, stop=True)
            nc.tensor.matmul(total[:, :], c["ones"][:, :], counts[:, :], start=True, stop=True).then_inc(summed, 1)

        @block.vector
        def _(dve):
            steps = [0]

            def then(ins):
                steps[0] += 1
                ins.then_inc(step, 1)
                dve.wait_ge(step, steps[0])
            dve.wait_ge(numbered, 1)
            then(nc.vector.tensor_copy(number[:, :], number_i[:, :]))
            dve.wait_ge(summed, 1)
            then(nc.vector.tensor_scalar(filled[:, :], total[:, :], float(P - 1), None, ALU.add))
            then(nc.vector.tensor_copy(filled_i[:, :], filled[:, :]))
            then(nc.vector.tensor_scalar(tiles_i[:, :], filled_i[:, :], 7, None, ALU.logical_shift_right))
            then(nc.vector.tensor_copy(tiles[:, :], tiles_i[:, :]))
            then(nc.vector.tensor_tensor_scan(ends[:, :], c["ones"][:, 0:NB], tiles[:, :], 0.0, ALU.mult, ALU.add))
            then(nc.vector.tensor_tensor(starts[:, :], ends[:, :], tiles[:, :], ALU.subtract))
            then(nc.vector.scalar_tensor_tensor(base[:, :], starts[:, :], float(P), within[:, :], ALU.mult, ALU.add))
            then(nc.vector.tensor_tensor(passed[:, :, :], over(ends[:, :], TPP), spread(number[:, :], NB), ALU.is_le))
            then(nc.vector.tensor_reduce(block_f[:, :], passed[:, :, :], AX.X, ALU.add))
            then(nc.vector.tensor_scalar(block_f[:, :], block_f[:, :], float(NB - 1), None, ALU.min))
            nc.vector.tensor_copy(block_i[:, :], block_f[:, :]).then_inc(found, 1)

        @block.sync
        def _(sp):
            sp.wait_ge(found, 1)
            sp.dma_start(blocks_dram.rearrange("(p j) -> p j", j=TPP), block_i[:, :]).then_inc(blocks_out, 16)
            sp.wait_ge(blocks_out, 16)


def sort_edges(nc, k, c, e, edge_attr, base, rec_dram):
    attr = k.sb("attr", [P, 2, G, RPE])
    rest = k.sb("rest", [P, G, RPE])
    rec = k.sb("rec", [P, 2, G, REC])
    parts = rec[:, :, :, :].bitcast(BF16)
    high, middle, low = (parts[:, :, :, n * ATT:n * ATT + RPE] for n in range(3))
    at_bf = k.sb("at_bf", [P, 2, G], BF16)
    of_bf = k.sb("of_bf", [P, 2, G], BF16)
    src_f = k.sb("src_f", [P, 2, G])
    hot_p = k.sb("hot_p", [P, 2, G, P], BF16)
    hot_b = k.sb("hot_b", [P, 2, G, NB], BF16)
    hot_pT = k.sb("hot_pT", [P, 2, P])
    table = k.sb("table", [P, 2, NB])
    junk_v = k.sb("junk_v", [P, G, NB], BF16)
    junk_r = k.sb("junk_r", [P, G, P], BF16)
    first = k.sb("first", [P, 2, G])
    rank = k.sb("rank", [P, 2, G])
    place_i = k.sb("place_i", [P, G], I32)
    row_hi = k.sb("row_hi", [P, G], I32)
    row_p = k.sb("row_p", [P, G], I32)
    row_t = k.sb("row_t", [P, G], I32)
    row_pt = k.sb("row_pt", [P, G], I32)
    row = k.sb("row", [P, 2, G], I32)
    hot_pT_ps = [k.ps(f"hot_pT_ps{s}", [P, P], BF16) for s in range(2)]
    other_ps = [k.ps(f"other_ps{s}", [P, P]) for s in range(2)]
    first_ps = [k.ps(f"first_ps{s}", [P, NB]) for s in range(2)]
    table_ps = k.ps("table_ps", [P, NB])
    one_set = k.sem("one_set")
    attr_in = [k.sem(f"attr_in{h}") for h in range(2)]
    copied_in = k.sem("copied_in")
    hot_ready = k.sem("hot_ready")
    turned = k.sem("turned")
    turned_copied = k.sem("turned_copied")
    table_made = k.sem("table_made")
    table_copied = k.sem("table_copied")
    looked_up = k.sem("looked_up")
    tile_ranked = k.sem("tile_ranked")
    step = k.sem("step")
    scattered = [k.sem(f"scattered{h}") for h in range(2)]
    slot_free = k.sem("slot_free")
    pool_turn = k.sem("pool_turn")
    STEPS = 12

    with nc.Block() as block:
        @block.sync
        def _(sp):
            sp.wait_ge(one_set, 3)

            def load(i, chunk, parts=P, width=CT):
                for h in range(2):
                    n = min(G, width - h * G)
                    need(sp, step, STEPS * (2 * i + h - 1))
                    rows = edge_attr[bass.ds(chunk * P * CT, parts * width), :].rearrange("(p j) w -> p j w", j=width)
                    sp.dma_start(attr[0:parts, h, 0:n, :], rows[:, h * G:h * G + n, :]).then_inc(attr_in[h], 16)
            load(0, 0)
            with sp.Fori(1, FULL) as i:
                load(i, i)
            load(FULL, FULL, LAST_P, LAST_T)

        @block.vector
        def _(dve):
            nc.vector.memset(attr[:, :, :, :], 0.0).then_inc(one_set, 1)
            nc.vector.memset(parts[:, :, :, :], 0.0).then_inc(one_set, 1)
            dve.wait_ge(one_set, 2)
            nc.vector.memset(parts[:, :, :, RPE:ATT], 1.0).then_inc(one_set, 1)

            def copy_in(g, h):
                cols = bass.ds(g * G, G)
                need(dve, table_made, G * (g - 1) + 1 if not isinstance(g, int) or g > 1 else 0)
                nc.vector.tensor_scalar(at_bf[:, h], e["at"][:, cols], 1.0, None, ALU.mult).then_inc(copied_in, 1)
                nc.vector.tensor_scalar(of_bf[:, h], e["of"][:, cols], 1.0, None, ALU.mult).then_inc(copied_in, 1)
                nc.vector.tensor_scalar(src_f[:, h], e["src_f"][:, cols], 1.0, None, ALU.mult).then_inc(copied_in, 1)

            def light_p(g, h, z):
                half = slice(z * G // 2, (z + 1) * G // 2)
                dve.wait_ge(copied_in, 3 * g + 3)
                nc.vector.tensor_tensor(hot_p[:, h, half], over(c["row_bf"][:, :], G // 2), spread(at_bf[:, h, half], P), ALU.is_equal).then_inc(hot_ready, 1)

            def light_b(g, h, z):
                half = slice(z * G // 2, (z + 1) * G // 2)
                nc.vector.tensor_tensor(hot_b[:, h, half], over(c["row_bf"][:, 0:NB], G // 2), spread(of_bf[:, h, half], NB), ALU.is_equal).then_inc(hot_ready, 1)

            def add_rank(g, h):
                need(dve, slot_free, g - 1)
                nc.vector.tensor_tensor(place_i[:, :], first[:, h], rank[:, h], ALU.add).then_inc(step, 1)
                dve.wait_ge(attr_in[h], 8 * (g - h) + 16)
                nc.vector.tensor_scalar(high[:, h], attr[:, h], 1.0, None, ALU.mult).then_inc(step, 1)

            def cut_place(g, h):
                dve.wait_ge(step, STEPS * g + 2)
                nc.vector.tensor_scalar(row_hi[:, :], place_i[:, :], 10, 10, ALU.logical_shift_right, ALU.logical_shift_left).then_inc(step, 1)
                nc.vector.tensor_scalar(row_p[:, :], place_i[:, :], P - 1, 3, ALU.bitwise_and, ALU.logical_shift_left).then_inc(step, 1)
                nc.vector.tensor_scalar(row_t[:, :], place_i[:, :], 7, G - 1, ALU.logical_shift_right, ALU.bitwise_and).then_inc(step, 1)
                nc.vector.tensor_tensor(rest[:, :, :], attr[:, h], high[:, h], ALU.subtract).then_inc(step, 1)

            def middle_part(g, h):
                dve.wait_ge(step, STEPS * g + 6)
                nc.vector.tensor_tensor(row_pt[:, :], row_p[:, :], row_t[:, :], ALU.bitwise_or).then_inc(step, 1)
                nc.vector.tensor_scalar(middle[:, h], rest[:, :, :], 1.0, None, ALU.mult).then_inc(step, 1)
                nc.vector.tensor_scalar(rec[:, h, :, LOC], e["at"][:, bass.ds(g * G, G)], 1.0, None, ALU.mult).then_inc(step, 1)
                nc.vector.tensor_scalar(rec[:, h, :, DST].bitcast(I32), e["dst"][:, :, :].rearrange("p c j -> p (c j)")[:, bass.ds(g * G, G)],
                                        1.0, None, ALU.mult).then_inc(step, 1)

            def low_part(g, h):
                dve.wait_ge(step, STEPS * g + 8)
                nc.vector.tensor_tensor(low[:, h], rest[:, :, :], middle[:, h], ALU.subtract).then_inc(step, 1)
                nc.vector.tensor_tensor(row[:, h], row_hi[:, :], row_pt[:, :], ALU.bitwise_or).then_inc(step, 1)
            copy_in(0, 0)
            for z in range(2):
                light_p(0, 0, z)
                light_b(0, 0, z)

            def body(i, last):
                for h in range(2):
                    g = 2 * i + h
                    starts = isinstance(g, int) and g == 0
                    for j in range(G):
                        t = G * g + j
                        dve.wait_ge(turned, t + 1)
                        nc.vector.scalar_tensor_tensor(junk_r[:, j], other_ps[j % 2][:, :], src_f[:, h, j:j + 1], c["after"][:, :],
                                                       ALU.is_equal, ALU.mult, accum_out=rank[:, h, j:j + 1]).then_inc(tile_ranked, 1)
                        if not (last and h == 1):
                            if j == 0:
                                copy_in(g + 1, 1 - h)
                            elif j in (1, 2):
                                light_p(g + 1, 1 - h, j - 1)
                            elif j in (3, 4):
                                light_b(g + 1, 1 - h, j - 3)
                        if not starts:
                            if j == 4:
                                add_rank(g - 1, 1 - h)
                            elif j == 5:
                                cut_place(g - 1, 1 - h)
                            elif j == 6:
                                middle_part(g - 1, 1 - h)
                            elif j == 7:
                                low_part(g - 1, 1 - h)
                        dve.wait_ge(looked_up, t + 1)
                        nc.vector.scalar_tensor_tensor(junk_v[:, j], first_ps[j % 2][:, :], 1.0, hot_b[:, h, j],
                                                       ALU.mult, ALU.mult, accum_out=first[:, h, j:j + 1]).then_inc(tile_ranked, 1)
                    dve.wait_ge(tile_ranked, 2 * G * (g + 1))
                if last:
                    for part in (add_rank, cut_place, middle_part, low_part):
                        part(g, h)
            rounds_ahead(dve, NCH, body)

        @block.tensor
        def _(pe):
            nc.tensor.matmul(table_ps[:, :], c["ident"][:, :], base[:, :], start=True, stop=True).then_inc(table_made, 1)

            def turn(g, h, j):
                t = G * g + j
                if j == 0:
                    pe.wait_ge(hot_ready, 4 * g + 4)
                need(pe, turned_copied, t - 1)
                nc.tensor.transpose(hot_pT_ps[j % 2][:, :], hot_p[:, h, j], c["ident_bf"][:, :])
                need(pe, tile_ranked, 2 * t - 3)
                nc.tensor.transpose(other_ps[j % 2][:, :], src_f[:, h, j:j + 1].to_broadcast([P, P]), c["ident"][:, :]).then_inc(turned, 1)
            turn(0, 0, 0)
            turn(0, 0, 1)

            def body(i, last):
                for h in range(2):
                    g = 2 * i + h
                    for j in range(G):
                        t = G * g + j
                        pe.wait_ge(table_copied, t + 1)
                        nc.tensor.matmul(table_ps[:, :], hot_p[:, h, j], hot_b[:, h, j], start=False, stop=True, skip_group_check=True).then_inc(table_made, 1)
                        pe.wait_ge(turned_copied, t + 1)
                        need(pe, tile_ranked, 2 * (t - 1))
                        nc.tensor.matmul(first_ps[j % 2][:, :], hot_pT[:, j % 2], table[:, j % 2], start=True, stop=True).then_inc(looked_up, 1)
                        if j + 2 < G:
                            turn(g, h, j + 2)
                        elif not (last and h == 1):
                            turn(g + 1, 1 - h, j + 2 - G)
            rounds_ahead(pe, NCH, body)

        @block.scalar
        def _(act):
            def body(i):
                for h in range(2):
                    for j in range(G):
                        t = G * (2 * i + h) + j
                        act.wait_ge(table_made, t + 1)
                        need(act, looked_up, t - 1)
                        nc.scalar.activation(table[:, j % 2], table_ps[:, :], ACT.Copy).then_inc(table_copied, 1)
                        act.wait_ge(turned, t + 1)
                        nc.scalar.activation(hot_pT[:, j % 2], hot_pT_ps[j % 2][:, :], ACT.Copy).then_inc(turned_copied, 1)
            rounds(act, NCH, body)

        @block.gpsimd
        def _(pool):
            pool.wait_ge(one_set, 3)

            def group(i, h, parts=P, tiles=G):
                g = 2 * i + h
                pool.wait_ge(step, STEPS * (g + 1))
                pool.sem_inc(pool_turn)
                for j in range(tiles):
                    nc.gpsimd.indirect_dma_start(rec_dram[:, :], bass.IndirectOffsetOnAxis(ap=row[0:parts, h, j:j + 1], axis=0),
                                                 rec[0:parts, h, j], None).then_inc(scattered[h], 16)
                    if j == 2 and not (isinstance(g, int) and g == 0):
                        pool.wait_ge(scattered[1 - h], 16 * G * (i + h))
                        pool.sem_inc(slot_free)

            def body(i):
                for h in range(2):
                    group(i, h)
            body(0)
            with pool.Fori(1, FULL) as i:
                body(i)
            group(FULL, 0, LAST_P, G)
            group(FULL, 1, LAST_P, LAST_T - G)
            pool.wait_ge(scattered[0], 16 * G * (FULL + 1))
            pool.wait_ge(scattered[1], 16 * (G * FULL + LAST_T - G))


class Turn:
    def __init__(self, i, r):
        self.i, self.r = i + r // 3, r % 3
        self.g = 3 * self.i + self.r
        self.slot = self.r
        self.used = self.i + 1

    def after(self, n):
        return Turn(self.i, self.r + n)


def walk(engine, first, last, groups, step):
    def plain(g):
        step(Turn(g // 3, g % 3), lambda n: 0 <= g + n < groups)
    for g in range(first, 6):
        plain(g)
    with engine.Fori(2, groups // 3 - 1) as i:
        for r in range(3):
            step(Turn(i, r), lambda n: True)
    for g in range(groups - 3, last + 1):
        plain(g)


def packed_blocks(engine, packed, g):
    words = [engine.value_load(packed[0:1, bass.ds(2 * g + n, 1)]) for n in range(2)]
    return [((words[t // 4] >> (8 * (t % 4))) & 127).with_bounds(min_val=0, max_val=NB - 1) for t in range(G)]


def attend(nc, k, c, Wk_rpe, bk_rpe, Wq_rpe, bq_rpe, q_dram, kv_dram, rec_dram, blocks_dram, packed, sums):
    SUM = DIM + H
    K6 = 6 * ATT
    split = k.sb("split", [ATT, 3, 2 * DH], BF16)
    rpe6 = k.sb("rpe6", [K6, 2 * DH], BF16)
    rec = k.sb("rec", [P, 3, G, REC])
    parts = rec[:, :, :, :].bitcast(BF16)
    tile_block = k.sb("tile_block", [P, TPP * P], I32)
    lifted = k.sb("lifted", [1, ST // 4], I32)
    new_block = k.sb("new_block", [P, ST])
    q = k.sb("q", [P, G, DH])
    kv = k.sb("kv", [P, 3, G, DH + SUM])
    hot = k.sb("hot", [P, 3, G, P])
    hotT = k.sb("hotT", [P, 3, G, P])
    rec6 = k.sb("rec6", [P, G, 6, ATT], BF16)
    recT = k.sb("recT", [K6, G, P], BF16)
    ident_bf = k.sb("ident_bf", [P, P], BF16)
    loc16 = k.sb("loc16", [P, G, H])
    locT = k.sb("locT", [P, 3, P])
    fresh = k.sb("fresh", [P, P + 1])
    drop = k.sb("drop", [P, P])
    run = k.sb("run", [P, P])
    lasts = k.sb("lasts", [P, P])
    compat = k.sb("compat", [P, G, H])
    lastsT = k.sb("lastsT", [P, G, H + 1])
    absent = k.sb("absent", [P, G])
    ROWS = H * (G + 1)
    drop_row = k.sb("drop_row", [P, ROWS + 1])
    found_row = k.sb("found_row", [P, ROWS])
    forward = k.sb("forward", [P, ROWS])
    maxima_row = k.sb("maxima_row", [P, ROWS])
    drops, found, maxima = (row[:, 0:ROWS].rearrange("p (h t) -> p h t", h=H) for row in (drop_row, found_row, maxima_row))
    fall = k.sb("fall", [P, H])
    keep = k.sb("keep", [P, H])
    shifted = k.sb("shifted", [P, G, H])
    qk_ps = [k.ps(f"qk_ps{s}", [P, 2, 2 * DH]) for s in range(2)]
    hotT_ps = k.ps("hotT_ps", [P, 4, P])
    recT_ps = k.ps("recT_ps", [P, G, P], BF16)
    sum_ps = [k.ps(f"sum_ps{s}", [P, 512]) for s in range(2)]
    turn_ps = k.ps("turn_ps", [P, 4, P])
    node_ps = k.ps("node_ps", [P, 512])
    lastsT_ps = node_ps[:, 0:P]
    tops = node_ps[:, P:P + G * (H + 1)].rearrange("p (t w) -> p t w", t=G)
    spread_ps = node_ps[:, 3 * P:4 * P].rearrange("p (t w) -> p t w", t=G)

    rpe_in = k.sem("rpe_in")
    rpe_step = k.sem("rpe_step")
    rpe_placed = k.sem("rpe_placed")
    cleared = k.sem("cleared")
    blocks_in = k.sem("blocks_in")
    packing = k.sem("packing")
    rec_in = [k.sem(f"rec_in{s}") for s in range(3)]
    q_in = [k.sem(f"q_in{u}") for u in range(G // 2)]
    gathered = [k.sem(f"gathered{s}") for s in range(3)]
    pool_turn = k.sem("pool_turn")
    sp_turn = k.sem("sp_turn")
    rec6_built = k.sem("rec6_built")
    loc_spread = k.sem("loc_spread")
    distance = k.sem("distance")
    hot_built = k.sem("hot_built")
    hot_turned = k.sem("hot_turned")
    hot_copied = k.sem("hot_copied")
    rec_turned = k.sem("rec_turned")
    rec_copied = k.sem("rec_copied")
    loc_turned = k.sem("loc_turned")
    loc_copied = k.sem("loc_copied")
    pair_ready = k.sem("pair_ready")
    pair_keyed = k.sem("pair_keyed")
    pair_used = k.sem("pair_used")
    compat_ready = k.sem("compat_ready")
    compat_turned = k.sem("compat_turned")
    scan_step = k.sem("scan_step")
    lasts_ready = k.sem("lasts_ready")
    lasts_turned = k.sem("lasts_turned")
    lasts_copied = k.sem("lasts_copied")
    tops_ready = k.sem("tops_ready")
    maximum_step = k.sem("maximum_step")
    maximum_taken = k.sem("maximum_taken")
    maxima_spread = k.sem("maxima_spread")
    fall_ready = k.sem("fall_ready")
    keep_ready = k.sem("keep_ready")
    scaled = k.sem("scaled")
    shift_done = k.sem("shift_done")
    exp_done = k.sem("exp_done")
    weighted = k.sem("weighted")
    tile_summed = k.sem("tile_summed")
    tile_added = k.sem("tile_added")

    weights = k.sb("weights", [ATT, 2 * DH])
    left = k.sb("left", [ATT, 2 * DH])
    with nc.Block() as block:
        @block.sync
        def _(sp):
            sp.dma_start(tile_block[:, :], blocks_dram.rearrange("(a t) -> a t", a=1).to_broadcast([P, TPP * P])).then_inc(blocks_in, 16)
            sp.dma_start(weights[0:RPE, 0:DH], Wq_rpe).then_inc(rpe_in, 16)
            sp.dma_start(weights[0:RPE, DH:], Wk_rpe).then_inc(rpe_in, 16)
            sp.dma_start(weights[RPE:ATT, 0:DH], bq_rpe.rearrange("(a n) -> a n", a=1)).then_inc(rpe_in, 16)
            sp.dma_start(weights[RPE:ATT, DH:], bk_rpe.rearrange("(a n) -> a n", a=1)).then_inc(rpe_in, 16)
            sp.wait_ge(rpe_step, 5)
            for row, part in enumerate((0, 1, 2, 0, 1, 0)):
                sp.dma_start(rpe6[row * ATT:(row + 1) * ATT, :], split[:, part]).then_inc(rpe_placed, 16)
            sp.wait_ge(rpe_placed, 96)
            sp.wait_ge(rpe_in, 64)
            sp.wait_ge(blocks_in, 16)
            sp.wait_ge(packing, 7)

            def load_records(turn):
                need(sp, compat_ready, turn.g - 2)
                sp.dma_start(rec[:, turn.slot], rec_dram[bass.ds(turn.g * (G * P), G * P), :].rearrange("(p t) w -> p t w", t=G)).then_inc(rec_in[turn.slot], 16)

            def load_queries(turn):
                block_of = packed_blocks(sp, packed, turn.g)
                for u in range(G // 2):
                    if not (isinstance(turn.g, int) and turn.g == 0):
                        sp.wait_ge(pair_ready, 4 * turn.g + u - 3)
                        sp.sem_inc(sp_turn)
                    for t in (2 * u, 2 * u + 1):
                        sp.dma_start(q[:, t], q_dram[bass.ds(block_of[t], 1), :, :].rearrange("a p d -> p (a d)")).then_inc(q_in[u], 16)

            def step(turn, inside):
                load_queries(turn)
                if inside(2):
                    load_records(turn.after(2))
            load_records(Turn(0, 0))
            load_records(Turn(0, 1))
            walk(sp, 0, GROUPS - 1, GROUPS, step)

        @block.gpsimd
        def _(pool):
            def gather(turn, inside):
                pool.wait_ge(rec_in[turn.slot], 16 * turn.used)
                pool.sem_inc(pool_turn)
                if not (isinstance(turn.g, int) and turn.g < 3):
                    pool.wait_ge(tile_summed, G * (turn.g - 2))
                    pool.sem_inc(pool_turn)
                for t in range(G):
                    nc.gpsimd.indirect_dma_start(kv[:, turn.slot, t, 0:DH + DIM], None, kv_dram[:, :],
                                                 bass.IndirectOffsetOnAxis(ap=rec[:, turn.slot, t, DST:DST + 1].bitcast(I32), axis=0)).then_inc(gathered[turn.slot], 16)
            walk(pool, 0, GROUPS - 1, GROUPS, gather)

        @block.scalar
        def _(act):
            def matrices(turn):
                act.wait_ge(rec_in[turn.slot], 16 * turn.used)
                need(act, rec_turned, turn.g)
                mine = parts[:, turn.slot]
                for a, n, part in ((0, 3, 0), (3, 2, 1), (5, 1, 2)):
                    nc.scalar.activation(rec6[:, :, a:a + n], mine[:, :, part * ATT:(part + 1) * ATT].unsqueeze(2).to_broadcast([P, G, n, ATT]), ACT.Copy).then_inc(rec6_built, 1)
                need(act, loc_turned, turn.g)
                nc.scalar.activation(loc16[:, :, :], spread(rec[:, turn.slot, :, LOC], H), ACT.Copy).then_inc(loc_spread, 1)

            def one_hots(turn):
                need(act, tile_summed, G * (turn.g - 2))
                for t in range(G):
                    nc.scalar.activation(hot[:, turn.slot, t], c["row"][:, :], ACT.Abs, bias=rec[:, turn.slot, t, LOC:LOC + 1], scale=-1.0).then_inc(distance, 1)
                act.wait_ge(distance, G * (turn.g + 1))
                nc.scalar.activation(hot[:, turn.slot], hot[:, turn.slot], ACT.Relu, bias=1.0, scale=-1.0).then_inc(hot_built, 1)

            def step(turn, inside):
                g, after, then = turn.g, turn.after(1), turn.after(2)
                if inside(-1):
                    act.wait_ge(shift_done, g)
                    nc.scalar.activation(kv[:, turn.after(-1).slot, :, DH + DIM:], shifted[:, :, :], ACT.Exp).then_inc(exp_done, 1)
                if inside(1):
                    act.wait_ge(loc_turned, g + 2)
                    nc.scalar.activation(locT[:, after.slot], turn_ps[:, 0], ACT.Copy).then_inc(loc_copied, 1)
                    for z in range(2):
                        act.wait_ge(hot_turned, 2 * g + z + 3)
                        need(act, maxima_spread, g - 1)
                        nc.scalar.activation(hotT[:, after.slot, 4 * z:4 * z + 4], hotT_ps[:, :, :], ACT.Copy).then_inc(hot_copied, 1)
                        if z == 0:
                            act.wait_ge(rec_turned, g + 2)
                            need(act, pair_ready, 4 * (g + 1))
                            nc.scalar.activation(recT[:, :, :], recT_ps[0:K6, :, :], ACT.Copy).then_inc(rec_copied, 1)
                if inside(2):
                    matrices(then)
                if inside(0):
                    act.wait_ge(lasts_turned, g + 1)
                    need(act, tops_ready, g)
                    nc.scalar.activation(lastsT[:, :, 0:H], lastsT_ps.rearrange("p (t w) -> p t w", t=G), ACT.Copy).then_inc(lasts_copied, 1)
                if inside(2):
                    one_hots(then)
                if inside(0):
                    act.wait_ge(fall_ready, g + 1)
                    need(act, scaled, 2 * g)
                    nc.scalar.activation(keep[:, :], fall[:, :], ACT.Exp).then_inc(keep_ready, 1)
            walk(act, -2, GROUPS, GROUPS, step)

        @block.vector
        def _(dve):
            nc.vector.memset(sums[:, :, :], 0.0).then_inc(cleared, 1)
            nc.vector.memset(maxima_row[:, :], -FAR).then_inc(cleared, 1)
            nc.vector.memset(drop_row[:, :], -FAR).then_inc(cleared, 1)
            nc.vector.memset(new_block[:, 0:1], 0.0).then_inc(cleared, 1)
            nc.vector.memset(fresh[:, :], 1.0).then_inc(cleared, 1)
            nc.vector.memset(lastsT[:, :, H:], 1.0).then_inc(cleared, 1)
            nc.vector.tensor_copy(ident_bf[:, :], c["ident"][:, :]).then_inc(cleared, 1)
            dve.wait_ge(rpe_in, 64)
            nc.vector.tensor_copy(split[:, 0], weights[:, :]).then_inc(rpe_step, 1)
            dve.wait_ge(rpe_step, 1)
            nc.vector.tensor_tensor(left[:, :], weights[:, :], split[:, 0], ALU.subtract).then_inc(rpe_step, 1)
            dve.wait_ge(rpe_step, 2)
            nc.vector.tensor_copy(split[:, 1], left[:, :]).then_inc(rpe_step, 1)
            dve.wait_ge(rpe_step, 3)
            nc.vector.tensor_tensor(split[:, 2], left[:, :], split[:, 1], ALU.subtract).then_inc(rpe_step, 2)
            dve.wait_ge(cleared, 7)
            dve.wait_ge(blocks_in, 16)
            fours = tile_block[0:1, 0:ST].rearrange("a (w n) -> a w n", n=4)
            nc.vector.tensor_copy(packed[:, :], fours[:, :, 0]).then_inc(packing, 1)
            for n in range(1, 4):
                dve.wait_ge(packing, 2 * n - 1)
                nc.vector.tensor_scalar(lifted[:, :], fours[:, :, n], 8 * n, None, ALU.logical_shift_left).then_inc(packing, 1)
                dve.wait_ge(packing, 2 * n)
                nc.vector.tensor_tensor(packed[:, :], packed[:, :], lifted[:, :], ALU.bitwise_or).then_inc(packing, 1)
            nc.vector.tensor_tensor(new_block[:, 1:], tile_block[:, 1:ST], tile_block[:, 0:ST - 1], ALU.not_equal).then_inc(packing, 1)
            dve.wait_ge(packing, 8)
            nc.vector.tensor_scalar(new_block[:, 1:], new_block[:, 1:], -FAR, None, ALU.mult).then_inc(packing, 1)
            dve.wait_ge(packing, 9)

            def key(turn, u):
                keys = kv[:, turn.slot, 2 * u:2 * u + 2, 0:DH]
                dve.wait_ge(pair_ready, 4 * turn.g + u + 1)
                nc.vector.tensor_tensor(keys, keys, qk_ps[u % 2][:, :, DH:], ALU.add).then_inc(pair_keyed, 1)

            def ask(turn, u):
                keys = kv[:, turn.slot, 2 * u:2 * u + 2, 0:DH]
                dve.wait_ge(pair_keyed, 4 * turn.g + u + 1)
                nc.vector.tensor_tensor(keys, keys, qk_ps[u % 2][:, :, 0:DH], ALU.mult).then_inc(pair_used, 1)

            def weigh(past, u):
                pair = kv[:, past.slot, 2 * u:2 * u + 2]
                values = pair[:, :, DH:DH + DIM].rearrange("p t (h d) -> p t h d", h=H)
                nc.vector.tensor_tensor(values, values, pair[:, :, DH + DIM:].unsqueeze(3).to_broadcast([P, 2, H, DV]), ALU.mult).then_inc(weighted, 1)

            def add(past, block_of, t):
                need(dve, tile_added, G * past.g + t)
                dve.wait_ge(tile_summed, G * past.g + t + 1)
                into = sums[:, bass.ds(block_of[t], 1), :].rearrange("p a n -> p (a n)")
                nc.vector.tensor_tensor(into, into, sum_ps[t % 2][:, 0:SUM], ALU.add).then_inc(tile_added, 1)

            def step(turn, inside):
                g, past = turn.g, turn.after(-1)
                if inside(0):
                    dve.wait_ge(gathered[turn.slot], 16 * G * turn.used)
                    key(turn, 0)
                    key(turn, 1)
                    ask(turn, 0)
                    ask(turn, 1)
                if inside(-1):
                    dve.wait_ge(maxima_spread, g)
                    nc.vector.tensor_tensor(shifted[:, :, :], compat[:, :, :], spread_ps, ALU.subtract).then_inc(shift_done, 1)
                if inside(0):
                    key(turn, 2)
                    key(turn, 3)
                    ask(turn, 2)
                    ask(turn, 3)
                    dve.wait_ge(pair_used, 4 * g + 4)
                    nc.vector.tensor_reduce(compat[:, :, :], kv[:, turn.slot, :, 0:DH].rearrange("p t (h d) -> p t h d", h=H), AX.X, ALU.add).then_inc(compat_ready, 1)
                if inside(-1):
                    block_of = packed_blocks(dve, packed, past.g)
                if inside(0):
                    need(dve, maximum_taken, g)
                    nc.vector.tensor_scalar(drops[:, :, 1:G + 1], over(new_block[:, bass.ds(g * G, G)], H), 1.0, None, ALU.mult).then_inc(maximum_step, 1)
                    nc.vector.tensor_scalar(found[:, :, 0:1], maxima[:, :, G:G + 1], 1.0, None, ALU.mult).then_inc(maximum_step, 1)
                if inside(-1):
                    old = sums[:, bass.ds(block_of[0], 1), :]
                    values, weight = old[:, :, 0:DIM].rearrange("p a (h d) -> p (a h) d", h=H), old[:, :, DIM:].rearrange("p a h -> p (a h)")
                    dve.wait_ge(keep_ready, g)
                    need(dve, tile_added, G * past.g)
                    nc.vector.tensor_tensor(values, values, spread(keep[:, :], DV), ALU.mult).then_inc(scaled, 1)
                    nc.vector.tensor_tensor(weight, weight, keep[:, :], ALU.mult).then_inc(scaled, 1)
                    dve.wait_ge(exp_done, g)
                    weigh(past, 0)
                if inside(0):
                    dve.wait_ge(loc_copied, g + 1)
                    nc.vector.tensor_tensor(fresh[:, 1:P], locT[:, turn.slot, 1:P], locT[:, turn.slot, 0:P - 1], ALU.not_equal).then_inc(scan_step, 1)
                if inside(-1):
                    weigh(past, 1)
                if inside(0):
                    dve.wait_ge(scan_step, 3 * g + 1)
                    nc.vector.tensor_scalar(drop[:, :], fresh[:, 0:P], -FAR, None, ALU.mult).then_inc(scan_step, 1)
                if inside(-1):
                    dve.wait_ge(scaled, 2 * g)
                    add(past, block_of, 0)
                    weigh(past, 2)
                if inside(0):
                    dve.wait_ge(scan_step, 3 * g + 2)
                    dve.wait_ge(compat_turned, g + 1)
                    nc.vector.tensor_tensor_scan(run[:, :], drop[:, :], turn_ps[:, 1], -FAR, ALU.add, ALU.max).then_inc(scan_step, 1)
                if inside(-1):
                    add(past, block_of, 1)
                    weigh(past, 3)
                if inside(0):
                    dve.wait_ge(scan_step, 3 * g + 3)
                    nc.vector.tensor_tensor(lasts[:, :], run[:, :], fresh[:, 1:P + 1], ALU.mult).then_inc(lasts_ready, 1)
                if inside(-1):
                    for t in (2, 3, 4):
                        add(past, block_of, t)
                if inside(0):
                    dve.wait_ge(tops_ready, g + 1)
                    nc.vector.tensor_scalar(absent[:, :], tops[:, :, H], 0.5, -FAR, ALU.is_lt, ALU.mult).then_inc(maximum_step, 1)
                if inside(-1):
                    add(past, block_of, 5)
                if inside(0):
                    dve.wait_ge(maximum_step, 5 * g + 3)
                    nc.vector.tensor_tensor(found[:, :, 1:].rearrange("p h t -> p t h"), tops[:, :, 0:H], spread(absent[:, :], H), ALU.add).then_inc(maximum_step, 1)
                if inside(-1):
                    add(past, block_of, 6)
                if inside(0):
                    dve.wait_ge(maximum_step, 5 * g + 4)
                    nc.vector.tensor_tensor_scan(forward[:, :], drop_row[:, 0:ROWS], found_row[:, :], -FAR, ALU.add, ALU.max).then_inc(maximum_step, 1)
                if inside(-1):
                    add(past, block_of, 7)
                if inside(0):
                    dve.wait_ge(maximum_step, 5 * g + 5)
                    nc.vector.tensor_tensor_scan(maxima_row[:, ::-1], drop_row[:, ROWS:0:-1], forward[:, ::-1], -FAR, ALU.add, ALU.max).then_inc(maximum_taken, 1)
                    dve.wait_ge(maximum_taken, g + 1)
                    nc.vector.tensor_tensor(fall[:, :], found[:, :, 0], maxima[:, :, 0], ALU.subtract).then_inc(fall_ready, 1)
            walk(dve, 0, GROUPS, GROUPS, step)

        @block.tensor
        def _(pe):
            pe.wait_ge(cleared, 7)
            pe.wait_ge(rpe_placed, 96)

            def turn_hot(turn, z):
                need(pe, hot_copied, 2 * turn.g + z)
                for t in range(4):
                    last = nc.tensor.transpose(hotT_ps[:, t], hot[:, turn.slot, 4 * z + t], c["ident"][:, :])
                last.then_inc(hot_turned, 1)

            def pair(turn, u):
                need(pe, pair_used, 4 * turn.g + u - 1)
                if u % 2 == 0:
                    pe.wait_ge(hot_copied, 2 * turn.g + u // 2 + 1)
                pe.wait_ge(q_in[u], 32 * (turn.g + 1))
                for w in range(2):
                    t = 2 * u + w
                    nc.tensor.matmul(qk_ps[u % 2][:, w, :], recT[:, t], rpe6[:, :], start=True, stop=False)
                    last = nc.tensor.matmul(qk_ps[u % 2][:, w, 0:DH], hotT[:, turn.slot, t], q[:, t], start=False, stop=True)
                last.then_inc(pair_ready, 1)

            def sum_tile(past, t):
                if t % 2 == 0:
                    pe.wait_ge(weighted, 4 * past.g + t // 2 + 1)
                need(pe, tile_added, G * past.g + t - 1)
                nc.tensor.matmul(sum_ps[t % 2][:, 0:SUM], hot[:, past.slot, t], kv[:, past.slot, t, DH:], start=True, stop=True).then_inc(tile_summed, 1)

            def step(turn, inside):
                g, past, after = turn.g, turn.after(-1), turn.after(1)
                if inside(1):
                    pe.wait_ge(loc_spread, g + 2)
                    need(pe, lasts_ready, g)
                    nc.tensor.transpose(turn_ps[:, 0], loc16[:, :, :].rearrange("p t h -> p (t h)"), c["ident"][:, :]).then_inc(loc_turned, 1)
                    pe.wait_ge(hot_built, g + 2)
                    turn_hot(after, 0)
                    pe.wait_ge(rec6_built, 3 * (g + 2))
                    need(pe, rec_copied, g + 1)
                    for t in range(G):
                        last = nc.tensor.transpose(recT_ps[0:K6, t], rec6[:, t].rearrange("p a w -> p (a w)"), ident_bf[:, :])
                    last.then_inc(rec_turned, 1)
                    turn_hot(after, 1)
                if inside(0):
                    pe.wait_ge(compat_ready, g + 1)
                    pe.wait_ge(loc_copied, g + 2 if inside(1) else g + 1)
                    nc.tensor.transpose(turn_ps[:, 1], compat[:, :, :].rearrange("p t h -> p (t h)"), c["ident"][:, :]).then_inc(compat_turned, 1)
                if inside(-1):
                    for t in range(4):
                        sum_tile(past, t)
                if inside(0):
                    pe.wait_ge(lasts_ready, g + 1)
                    need(pe, shift_done, g)
                    nc.tensor.transpose(lastsT_ps, lasts[:, :], c["ident"][:, :]).then_inc(lasts_turned, 1)
                if inside(-1):
                    sum_tile(past, 4)
                if inside(0):
                    pe.wait_ge(lasts_copied, g + 1)
                    for t in range(G):
                        last = nc.tensor.matmul(tops[:, t], hot[:, turn.slot, t], lastsT[:, t], start=True, stop=True)
                    last.then_inc(tops_ready, 1)
                if inside(-1):
                    for t in range(5, G):
                        sum_tile(past, t)
                if inside(1):
                    pe.wait_ge(rec_copied, g + 2)
                    pair(after, 0)
                    pair(after, 1)
                if inside(0):
                    pe.wait_ge(maximum_taken, g + 1)
                    for t in range(G):
                        last = nc.tensor.matmul(spread_ps[:, t], hotT[:, turn.slot, t], maxima[:, :, t + 1], start=True, stop=True)
                    last.then_inc(maxima_spread, 1)
                if inside(1):
                    pair(after, 2)
                    pair(after, 3)
            walk(pe, -1, GROUPS, GROUPS, step)


class Norm:
    def __init__(self, nc, k):
        self.nc = nc
        self.rows = k.sb("rows", [P, 2, DIM])
        self.stats = k.sb("stats", [P, 2, 6])
        self.all_stats = k.sb("all_stats", [P, NB, 6])
        self.mean = k.sb("mean", [P, NB])
        self.scale = k.sb("scale", [P, NB])
        self.gap = k.sb("gap", [P, NB])
        self.between = k.sb("between", [P, NB])
        self.within = k.sb("within", [P, NB])
        self.scaling = k.sb("scaling", [P, 4, 2])
        self.rows_ready = k.sem("rows_ready")
        self.rows_kept = k.sem("rows_kept")
        self.stats_ready = k.sem("stats_ready")
        self.stats_kept = k.sem("stats_kept")
        self.step = k.sem("step")
        self.guarded = k.sem("guarded")
        self.rooted = k.sem("rooted")
        self.scaling_ready = k.sem("scaling_ready")

    def take(self, dve, g, h):
        dve.wait_ge(self.rows_ready, g + 1)
        self.nc.vector.bn_stats(self.stats[:, h], self.rows[:, h]).then_inc(self.stats_ready, 1)
        dve.wait_ge(self.stats_ready, g + 1)
        self.nc.vector.tensor_scalar(self.all_stats[:, bass.ds(g, 1), :].rearrange("p a w -> p (a w)"), self.stats[:, h], 1.0, None, ALU.mult).then_inc(self.stats_kept, 1)

    def keep(self, act, sums, g, h):
        act.wait_ge(self.rows_ready, g + 1)
        self.nc.scalar.activation(sums[:, bass.ds(g, 1), 0:DIM].rearrange("p a n -> p (a n)"), self.rows[:, h], ACT.Copy).then_inc(self.rows_kept, 1)

    def combine(self, dve):
        n = [0]

        def then(ins):
            n[0] += 1
            ins.then_inc(self.step, 1)
            dve.wait_ge(self.step, n[0])
        v = self.nc.vector
        m0, m1 = self.all_stats[:, :, 1], self.all_stats[:, :, 4]
        s0, s1 = self.all_stats[:, :, 2], self.all_stats[:, :, 5]
        dve.wait_ge(self.stats_kept, NB)
        then(v.tensor_tensor(self.mean[:, :], m0, m1, ALU.add))
        then(v.tensor_scalar(self.mean[:, :], self.mean[:, :], 0.5, None, ALU.mult))
        then(v.tensor_tensor(self.gap[:, :], m0, m1, ALU.subtract))
        then(v.tensor_scalar(self.gap[:, :], self.gap[:, :], 0.5, None, ALU.mult))
        then(v.tensor_tensor(self.between[:, :], self.gap[:, :], self.gap[:, :], ALU.mult))
        then(v.tensor_tensor(self.within[:, :], s0, s1, ALU.add))
        then(v.tensor_scalar(self.within[:, :], self.within[:, :], 1.0 / DIM, NORM_EPS, ALU.mult, ALU.add))
        v.tensor_tensor(self.within[:, :], self.within[:, :], self.between[:, :], ALU.add).then_inc(self.guarded, 1)
        dve.wait_ge(self.rooted, 1)
        then(v.reciprocal(self.scale[:, :], self.between[:, :]))

    def root(self, act):
        act.wait_ge(self.guarded, 1)
        self.nc.scalar.activation(self.between[:, :], self.within[:, :], ACT.Sqrt).then_inc(self.rooted, 1)

    def apply(self, dve, sums, g, h, out):
        v = self.nc.vector
        v.tensor_scalar(self.scaling[:, h, 0:1], self.mean[:, bass.ds(g, 1)], 1.0, None, ALU.mult).then_inc(self.scaling_ready, 1)
        v.tensor_scalar(self.scaling[:, h, 1:2], self.scale[:, bass.ds(g, 1)], 1.0, None, ALU.mult).then_inc(self.scaling_ready, 1)
        dve.wait_ge(self.scaling_ready, 2 * g + 2)
        return v.tensor_scalar(out, sums[:, bass.ds(g, 1), 0:DIM].rearrange("p a n -> p (a n)"),
                               self.scaling[:, h, 0:1], self.scaling[:, h, 1:2], ALU.subtract, ALU.mult)


def finish_attention(nc, k, c, x, sums, W_r, b_r, stalk, stalks_dram):
    norm = Norm(nc, k)
    xs = k.sb("xs", [P, 2, DIM])
    mixed = k.sb("mixed", [P, 2, DIM])
    inverse = k.sb("inverse", [P, 2, H])
    normal = k.sb("normal", [P, 2, DIM])
    normalT = k.sb("normalT", [P, 2, DIM])
    weight = k.sb("weight", [P, 2, STALK])
    bias = k.sb("bias", [1, STALK])
    one = k.sb("one", [1, P])
    normalT_ps = [k.ps(f"normalT_ps{h}", [P, DIM]) for h in range(2)]
    stalk_ps = [k.ps(f"stalk_ps{h}", [P, 512]) for h in range(2)]
    one_set = k.sem("one_set")
    weights_in = k.sem("weights_in")
    x_in = [k.sem(f"x_in{h}") for h in range(2)]
    den_step = k.sem("den_step")
    mix_step = k.sem("mix_step")
    normalised = k.sem("normalised")
    kept = k.sem("kept")
    turned = k.sem("turned")
    turned_copied = k.sem("turned_copied")
    stalked = k.sem("stalked")
    stalk_copied = k.sem("stalk_copied")
    stalks_out = k.sem("stalks_out")
    with nc.Block() as block:
        @block.sync
        def _(sp):
            sp.dma_start(weight[:, :, :], W_r.rearrange("(a p) n -> p a n", p=P)).then_inc(weights_in, 16)
            sp.dma_start(bias[:, :], b_r.rearrange("(a n) -> a n", a=1)).then_inc(weights_in, 16)

            def load(b, h, i, rows=P):
                need(sp, norm.rows_ready, 2 * i + h - 1)
                sp.dma_start(xs[0:rows, h, :], x[bass.ds(b * P, rows), :]).then_inc(x_in[h], 16)
            load(0, 0, 0)
            load(1, 1, 0)
            with sp.Fori(1, NB // 2 - 1) as i:
                for h in range(2):
                    load(2 * i + h, h, i)
            load(NB - 2, 0, NB // 2 - 1)
            load(NB - 1, 1, NB // 2 - 1, NLAST)
            sp.wait_ge(stalk_copied, NB)
            sp.dma_start(stalks_dram.rearrange("(b p) s -> p b s", p=P), stalk[:, :, :]).then_inc(stalks_out, 16)
            sp.wait_ge(stalks_out, 16)
            sp.wait_ge(weights_in, 32)

        @block.vector
        def _(dve):
            nc.vector.memset(one[:, :], 1.0).then_inc(one_set, 1)

            def mix(i):
                for h in range(2):
                    g = 2 * i + h
                    block_sums = sums[:, bass.ds(g, 1), :].rearrange("p a n -> p (a n)")
                    nc.vector.tensor_scalar(inverse[:, h], block_sums[:, DIM:], SOFT_EPS, None, ALU.add).then_inc(den_step, 1)
                    dve.wait_ge(den_step, 2 * g + 1)
                    nc.vector.reciprocal(inverse[:, h], inverse[:, h]).then_inc(den_step, 1)
                    dve.wait_ge(den_step, 2 * g + 2)
                    nc.vector.tensor_tensor(mixed[:, h].rearrange("p (h d) -> p h d", h=H),
                                            block_sums[:, 0:DIM].rearrange("p (h d) -> p h d", h=H), spread(inverse[:, h], DV), ALU.mult).then_inc(mix_step, 1)
                    dve.wait_ge(mix_step, g + 1)
                    dve.wait_ge(x_in[h], 16 * i + 16)
                    need(dve, norm.rows_kept, g - 1)
                    nc.vector.tensor_tensor(norm.rows[:, h], mixed[:, h], xs[:, h], ALU.add).then_inc(norm.rows_ready, 1)
                    norm.take(dve, g, h)
            rounds(dve, NB // 2, mix)
            norm.combine(dve)
            dve.wait_ge(norm.rows_kept, NB)

            def normalise(i):
                for h in range(2):
                    g = 2 * i + h
                    need(dve, turned, g - 1)
                    need(dve, kept, g - 1)
                    norm.apply(dve, sums, g, h, normal[:, h]).then_inc(normalised, 1)
            rounds(dve, NB // 2, normalise)

        @block.scalar
        def _(act):
            def keep(i):
                for h in range(2):
                    norm.keep(act, sums, 2 * i + h, h)
            rounds(act, NB // 2, keep)
            norm.root(act)

            def body(i):
                for h in range(2):
                    g = 2 * i + h
                    act.wait_ge(normalised, g + 1)
                    nc.scalar.activation(sums[:, bass.ds(g, 1), 0:DIM].rearrange("p a n -> p (a n)"), normal[:, h], ACT.Copy).then_inc(kept, 1)
                    act.wait_ge(turned, g + 1)
                    need(act, stalked, g - 1)
                    nc.scalar.activation(normalT[:, h], normalT_ps[h][:, :], ACT.Copy).then_inc(turned_copied, 1)
                    act.wait_ge(stalked, g + 1)
                    nc.scalar.activation(stalk[:, bass.ds(g, 1), :].rearrange("p a s -> p (a s)"), stalk_ps[h][:, 0:STALK], ACT.Copy).then_inc(stalk_copied, 1)
            rounds(act, NB // 2, body)
            act.wait_ge(kept, NB)

        @block.tensor
        def _(pe):
            pe.wait_ge(weights_in, 32)
            pe.wait_ge(one_set, 1)

            def body(i):
                for h in range(2):
                    g = 2 * i + h
                    pe.wait_ge(normalised, g + 1)
                    need(pe, turned_copied, g - 1)
                    for a in range(2):
                        last = nc.tensor.transpose(normalT_ps[h][:, a * P:(a + 1) * P], normal[:, h, a * P:(a + 1) * P], c["ident"][:, :])
                    last.then_inc(turned, 1)
                    pe.wait_ge(turned_copied, g + 1)
                    need(pe, stalk_copied, g - 1)
                    for a in range(2):
                        nc.tensor.matmul(stalk_ps[h][:, 0:STALK], normalT[:, h, a * P:(a + 1) * P], weight[:, a], start=(a == 0), stop=False)
                    nc.tensor.matmul(stalk_ps[h][:, 0:STALK], one[:, :], bias[:, :], start=False, stop=True).then_inc(stalked, 1)
            rounds(pe, NB // 2, body)


def diffuse(nc, k, c, stalk, stalks_dram, rec_dram, packed, flow):
    rec = k.sb("rec", [P, 3, G, REC])
    far = k.sb("far", [P, 3, G, STALK])
    dst_at = k.sb("dst_at", [P, G], I32)
    dst_of = k.sb("dst_of", [P, G], I32)
    at = k.sb("at", [P, 3, G])
    of = k.sb("of", [P, 3, G])
    hot = k.sb("hot", [P, 3, G, P], BF16)
    hotT = k.sb("hotT", [P, 3, G, P], BF16)
    ident_bf = k.sb("ident_bf", [P, P], BF16)
    stalk_parts = k.sb("stalk_parts", [P, NB, 3, STALK], BF16)
    stalk_left = k.sb("stalk_left", [P, NB, STALK])
    near = k.sb("near", [P, G, STALK])
    left = k.sb("left", [P, G, STALK])
    parts = k.sb("parts", [P, 3, G, 3, STALK], BF16)
    dst_hot = k.sb("dst_hot", [P, 3, G, P])
    differs = k.sb("differs", [P, 3, G, STALK])
    opposed = k.sb("opposed", [P, G, STALK])
    zero_mat = k.sb("zero_mat", [P, P])
    placed = k.sb("placed", [P, G, NB, STALK])
    hotT_ps = k.ps("hotT_ps", [P, G, P], BF16)
    near_ps = k.ps("near_ps", [P, 512])
    near_parts = near_ps[:, 0:G * 3 * STALK].rearrange("p (t n s) -> p t n s", t=G, n=3)
    flow_ps = k.ps("flow_ps", [P, NB, STALK])
    cleared = k.sem("cleared")
    rec_in = [k.sem(f"rec_in{s}") for s in range(3)]
    gathered = [k.sem(f"gathered{s}") for s in range(3)]
    sp_turn = k.sem("sp_turn")
    pool_turn = k.sem("pool_turn")
    distance = k.sem("distance")
    hot_ready = k.sem("hot_ready")
    hot_turned = k.sem("hot_turned")
    hot_copied = k.sem("hot_copied")
    dst_step = k.sem("dst_step")
    dst_distance = k.sem("dst_distance")
    dst_hot_ready = k.sem("dst_hot_ready")
    near_ready = k.sem("near_ready")
    near_step = k.sem("near_step")
    differ_ready = k.sem("differ_ready")
    opposed_ready = k.sem("opposed_ready")
    part_step = k.sem("part_step")
    parts_ready = k.sem("parts_ready")
    placed_ready = k.sem("placed_ready")
    tile_into = k.sem("tile_into")
    out_done = k.sem("out_done")
    all_into = k.sem("all_into")
    with nc.Block() as block:
        @block.sync
        def _(sp):
            def load(turn, inside):
                if not (isinstance(turn.g, int) and turn.g < 3):
                    sp.wait_ge(differ_ready, turn.g - 2)
                    sp.sem_inc(sp_turn)
                    sp.wait_ge(dst_hot_ready, turn.g - 2)
                    sp.sem_inc(sp_turn)
                sp.dma_start(rec[:, turn.slot], rec_dram[bass.ds(turn.g * (G * P), G * P), :].rearrange("(p t) w -> p t w", t=G)).then_inc(rec_in[turn.slot], 16)
            walk(sp, 0, GROUPS - 1, GROUPS, load)

        @block.gpsimd
        def _(pool):
            def gather(turn, inside):
                pool.wait_ge(rec_in[turn.slot], 16 * turn.used)
                pool.sem_inc(pool_turn)
                if not (isinstance(turn.g, int) and turn.g < 3):
                    pool.wait_ge(differ_ready, turn.g - 2)
                    pool.sem_inc(pool_turn)
                for t in range(G):
                    nc.gpsimd.indirect_dma_start(far[:, turn.slot, t], None, stalks_dram[:, :],
                                                 bass.IndirectOffsetOnAxis(ap=rec[:, turn.slot, t, DST:DST + 1].bitcast(I32), axis=0)).then_inc(gathered[turn.slot], 16)
            walk(pool, 0, GROUPS - 1, GROUPS, gather)

        @block.scalar
        def _(act):
            def one_hots(turn):
                act.wait_ge(rec_in[turn.slot], 16 * turn.used)
                need(act, out_done, turn.g - 2)
                for t in range(G):
                    nc.scalar.activation(hot[:, turn.slot, t], c["row"][:, :], ACT.Abs, bias=rec[:, turn.slot, t, LOC:LOC + 1], scale=-1.0).then_inc(distance, 1)
                act.wait_ge(distance, G * (turn.g + 1))
                nc.scalar.activation(hot[:, turn.slot], hot[:, turn.slot], ACT.Relu, bias=1.0, scale=-1.0).then_inc(hot_ready, 1)

            def dst_one_hots(turn):
                act.wait_ge(dst_step, 4 * (turn.g + 1))
                need(act, tile_into, G * (turn.g - 2))
                for t in range(G):
                    nc.scalar.activation(dst_hot[:, turn.slot, t], c["row"][:, :], ACT.Abs, bias=at[:, turn.slot, t:t + 1], scale=-1.0).then_inc(dst_distance, 1)
                act.wait_ge(dst_distance, G * (turn.g + 1))
                nc.scalar.activation(dst_hot[:, turn.slot], dst_hot[:, turn.slot], ACT.Relu, bias=1.0, scale=-1.0).then_inc(dst_hot_ready, 1)

            def step(turn, inside):
                then = turn.after(2)
                if inside(2):
                    one_hots(then)
                    need(act, near_ready, then.g - 2)
                    dst_one_hots(then)
                    act.wait_ge(hot_turned, then.g + 1)
                    nc.scalar.activation(hotT[:, then.slot], hotT_ps[:, :, :], ACT.Copy).then_inc(hot_copied, 1)
            walk(act, -2, GROUPS - 3, GROUPS, step)

        @block.vector
        def _(dve):
            nc.vector.memset(zero_mat[:, :], 0.0).then_inc(cleared, 1)
            nc.vector.tensor_copy(ident_bf[:, :], c["ident"][:, :]).then_inc(cleared, 1)
            nc.vector.tensor_copy(stalk_parts[:, :, 0], stalk[:, :, :]).then_inc(cleared, 1)
            dve.wait_ge(cleared, 3)
            nc.vector.tensor_tensor(stalk_left[:, :, :], stalk[:, :, :], stalk_parts[:, :, 0], ALU.subtract).then_inc(cleared, 1)
            dve.wait_ge(cleared, 4)
            nc.vector.tensor_copy(stalk_parts[:, :, 1], stalk_left[:, :, :]).then_inc(cleared, 1)
            dve.wait_ge(cleared, 5)
            nc.vector.tensor_tensor(stalk_parts[:, :, 2], stalk_left[:, :, :], stalk_parts[:, :, 1], ALU.subtract).then_inc(cleared, 1)

            def step(turn, inside):
                g, then = turn.g, turn.after(2)
                if inside(0):
                    dve.wait_ge(near_ready, g + 1)
                    need(dve, opposed_ready, g)
                    nc.vector.tensor_reduce(near[:, :, :], near_parts.rearrange("p t n s -> p t s n"), AX.X, ALU.add).then_inc(near_step, 1)
                    dve.wait_ge(near_step, g + 1)
                    dve.wait_ge(gathered[turn.slot], 16 * G * turn.used)
                    nc.vector.tensor_tensor(differs[:, turn.slot], far[:, turn.slot], near[:, :, :], ALU.subtract).then_inc(differ_ready, 1)
                if inside(2):
                    dve.wait_ge(rec_in[then.slot], 16 * then.used)
                    dst = rec[:, then.slot, :, DST].bitcast(I32)
                    need(dve, dst_step, 4 * then.g)
                    nc.vector.tensor_scalar(dst_at[:, :], dst, P - 1, None, ALU.bitwise_and).then_inc(dst_step, 1)
                    nc.vector.tensor_scalar(dst_of[:, :], dst, 7, None, ALU.logical_shift_right).then_inc(dst_step, 1)
                    need(dve, dst_hot_ready, then.g - 2)
                    dve.wait_ge(dst_step, 4 * then.g + 2)
                    nc.vector.tensor_copy(at[:, then.slot], dst_at[:, :]).then_inc(dst_step, 1)
                    nc.vector.tensor_copy(of[:, then.slot], dst_of[:, :]).then_inc(dst_step, 1)
                if inside(0):
                    dve.wait_ge(differ_ready, g + 1)
                    dve.wait_ge(dst_step, 4 * (g + 1))
                    for t in range(G):
                        need(dve, tile_into, G * (g - 1) + t + 1)
                        nc.vector.scalar_tensor_tensor(placed[:, t], spread(c["row"][:, 0:NB], STALK), of[:, turn.slot, t:t + 1],
                                                       over(differs[:, turn.slot, t], NB), ALU.is_equal, ALU.mult).then_inc(placed_ready, 1)
                        if t == 1:
                            need(dve, part_step, 3 * g)
                            nc.vector.tensor_scalar(opposed[:, :, :], differs[:, turn.slot], -1.0, None, ALU.mult).then_inc(opposed_ready, 1)
                        elif t == 2:
                            need(dve, out_done, g - 2)
                            dve.wait_ge(opposed_ready, g + 1)
                            nc.vector.tensor_copy(parts[:, turn.slot, :, 0], opposed[:, :, :]).then_inc(part_step, 1)
                        elif t == 3:
                            dve.wait_ge(part_step, 3 * g + 1)
                            nc.vector.tensor_tensor(left[:, :, :], opposed[:, :, :], parts[:, turn.slot, :, 0], ALU.subtract).then_inc(part_step, 1)
                        elif t == 4:
                            dve.wait_ge(part_step, 3 * g + 2)
                            nc.vector.tensor_copy(parts[:, turn.slot, :, 1], left[:, :, :]).then_inc(part_step, 1)
                        elif t == 5:
                            dve.wait_ge(part_step, 3 * g + 3)
                            nc.vector.tensor_tensor(parts[:, turn.slot, :, 2], left[:, :, :], parts[:, turn.slot, :, 1], ALU.subtract).then_inc(parts_ready, 1)
            walk(dve, -2, GROUPS - 1, GROUPS, step)
            dve.wait_ge(all_into, 1)
            nc.vector.tensor_copy(flow[:, :, :], flow_ps[:, :, :]).then_inc(cleared, 1)

        @block.tensor
        def _(pe):
            pe.wait_ge(cleared, 6)
            nc.tensor.matmul(flow_ps[:, :, :], zero_mat[:, :], c["row"][:, 0:1].to_broadcast([P, STALK * NB]), start=True, stop=False)

            def step(turn, inside):
                g, after, then = turn.g, turn.after(1), turn.after(2)
                if inside(1):
                    next_blocks = packed_blocks(pe, packed, after.g)
                if inside(0):
                    block_of = packed_blocks(pe, packed, g)
                for t in range(G):
                    if inside(0):
                        if t == 0:
                            pe.wait_ge(dst_hot_ready, g + 1)
                        pe.wait_ge(placed_ready, G * g + t + 1)
                        nc.tensor.matmul(flow_ps[:, :, :], dst_hot[:, turn.slot, t], placed[:, t], start=False, stop=False).then_inc(tile_into, 1)
                    if inside(1) and t < 4:
                        if t == 0:
                            pe.wait_ge(hot_copied, g + 2)
                            need(pe, near_step, g + 1)
                        for u in (2 * t, 2 * t + 1):
                            last = nc.tensor.matmul(near_parts[:, u].rearrange("p n s -> p (n s)"), hotT[:, after.slot, u],
                                                    stalk_parts[:, bass.ds(next_blocks[u], 1), :, :].rearrange("p a n s -> p (a n s)"), start=True, stop=True)
                        if t == 3:
                            last.then_inc(near_ready, 1)
                    if inside(2) and t >= 4:
                        if t == 4:
                            pe.wait_ge(hot_ready, g + 3)
                            need(pe, hot_copied, g + 2)
                        for u in (2 * t - G, 2 * t - G + 1):
                            last = nc.tensor.transpose(hotT_ps[:, u], hot[:, then.slot, u], ident_bf[:, :])
                        if t == G - 1:
                            last.then_inc(hot_turned, 1)
                if inside(0):
                    pe.wait_ge(parts_ready, g + 1)
                    for t in range(G):
                        for n in range(3):
                            last = nc.tensor.matmul(flow_ps[:, bass.ds(block_of[t], 1), :].rearrange("p a s -> p (a s)"), hot[:, turn.slot, t], parts[:, turn.slot, t, n], start=False, stop=False)
                    last.then_inc(out_done, 1)
            walk(pe, -2, GROUPS - 1, GROUPS, step)
            nc.tensor.matmul(flow_ps[:, :, :], zero_mat[:, :], c["row"][:, 0:1].to_broadcast([P, STALK * NB]), start=False, stop=True).then_inc(all_into, 1)


def finish(nc, k, c, sums, flow, W_o, b_o, out):
    norm = Norm(nc, k)
    weight = k.sb("weight", [STALK + 1, DIM])
    flows = k.sb("flows", [P, 2, STALK + 1])
    flowT = k.sb("flowT", [STALK + 1, 2, P])
    bent = k.sb("bent", [P, 2, DIM])
    normal = k.sb("normal", [P, 4, DIM])
    flowT_ps = [k.ps(f"flowT_ps{h}", [P, 512]) for h in range(2)]
    wide_ps = [k.ps(f"wide_ps{h}", [P, 512]) for h in range(2)]
    one_set = k.sem("one_set")
    weights_in = k.sem("weights_in")
    flow_copied = k.sem("flow_copied")
    turned = k.sem("turned")
    turned_copied = k.sem("turned_copied")
    widened = k.sem("widened")
    bent_ready = k.sem("bent_ready")
    normalised = k.sem("normalised")
    rows_out = [k.sem(f"rows_out{h}") for h in range(2)]
    HALF = NB // 2
    with nc.Block() as block:
        @block.sync
        def _(sp):
            sp.dma_start(weight[0:STALK, :], W_o).then_inc(weights_in, 16)
            sp.dma_start(weight[STALK:STALK + 1, :], b_o.rearrange("(a n) -> a n", a=1)).then_inc(weights_in, 16)

            def store(b, h, g, rows=P):
                sp.wait_ge(normalised, g + 1)
                sp.dma_start(out[bass.ds(b * P, rows), :], normal[0:rows, h]).then_inc(rows_out[h], 16)
            with sp.Fori(0, HALF - 1) as i:
                for h in range(2):
                    store(2 * i + h, h, 2 * i + h)
            store(NB - 2, 0, NB - 2)
            store(NB - 1, 1, NB - 1, NLAST)
            sp.wait_ge(rows_out[0], 16 * HALF)
            sp.wait_ge(rows_out[1], 16 * HALF)
            sp.wait_ge(weights_in, 32)

        @block.vector
        def _(dve):
            nc.vector.memset(flows[:, :, STALK:], 1.0).then_inc(one_set, 1)

            def lend(g, h):
                need(dve, turned, g - 1)
                nc.vector.tensor_scalar(flows[:, h, 0:STALK], flow[:, bass.ds(g, 1), :].rearrange("p a s -> p (a s)"), 1.0, None, ALU.mult).then_inc(flow_copied, 1)

            def add(i):
                for h in range(2):
                    g = 2 * i + h
                    lend(g, h)
                    dve.wait_ge(bent_ready, g + 1)
                    rows = sums[:, bass.ds(g, 1), 0:DIM].rearrange("p a n -> p (a n)")
                    need(dve, norm.rows_kept, g - 1)
                    nc.vector.tensor_tensor(norm.rows[:, h], rows, bent[:, h], ALU.add).then_inc(norm.rows_ready, 1)
                    norm.take(dve, g, h)
            rounds(dve, HALF, add)
            norm.combine(dve)
            dve.wait_ge(norm.rows_kept, NB)

            def normalise(i):
                for h in range(2):
                    g = 2 * i + h
                    need(dve, rows_out[h], 16 * i)
                    norm.apply(dve, sums, g, h, normal[:, h]).then_inc(normalised, 1)
            rounds(dve, HALF, normalise)

        @block.scalar
        def _(act):
            def body(i):
                for h in range(2):
                    g = 2 * i + h
                    act.wait_ge(turned, g + 1)
                    need(act, widened, g - 1)
                    nc.scalar.activation(flowT[:, h], flowT_ps[h][0:STALK + 1, 0:P], ACT.Copy).then_inc(turned_copied, 1)
                    act.wait_ge(widened, g + 1)
                    need(act, norm.rows_ready, g - 1)
                    nc.scalar.activation(bent[:, h], wide_ps[h][:, 0:DIM], ACT.Gelu).then_inc(bent_ready, 1)
                    norm.keep(act, sums, g, h)
            rounds(act, HALF, body)
            norm.root(act)

        @block.tensor
        def _(pe):
            pe.wait_ge(weights_in, 32)
            pe.wait_ge(one_set, 1)

            def body(i):
                for h in range(2):
                    g = 2 * i + h
                    pe.wait_ge(flow_copied, g + 1)
                    need(pe, turned_copied, g - 1)
                    nc.tensor.transpose(flowT_ps[h][0:STALK + 1, 0:P], flows[:, h], c["ident"][:, :]).then_inc(turned, 1)
                    pe.wait_ge(turned_copied, g + 1)
                    need(pe, bent_ready, g - 1)
                    nc.tensor.matmul(wide_ps[h][:, 0:DIM], flowT[:, h], weight[:, :], start=True, stop=True).then_inc(widened, 1)
            rounds(pe, HALF, body)


def graph_network(nc, x, src, dst, edge_attr, Wqkv, bqkv, Wk_rpe, bk_rpe, Wq_rpe, bq_rpe, W_r, b_r, W_o, b_o, out, scratch):
    q_dram, kv_dram, rec_dram, blocks_dram, stalks_dram = scratch[:5]
    with ExitStack() as whole:
        k = Room(nc, whole, "all")
        c = {name: k.sb(name, [P, P]) for name in ("ident", "row")}
        with ExitStack() as sorting:
            s = Room(nc, sorting, "sorting")
            c.update({name: s.sb(name, [P, P]) for name in ("ones", "zeros", "before", "after")})
            c.update({name: s.sb(name, [P, P], BF16) for name in ("ident_bf", "zeros_bf", "row_bf")})
            c["row_i"] = s.sb("row_i", [P, P], I32)
            e = {"src": s.sb("src", [P, NCH, CT], I32), "dst": s.sb("dst", [P, NCH, CT], I32)}
            e.update({name: s.sb(name, [P, NCH * CT]) for name in ("src_f", "at", "of")})
            counts = s.sb("counts", [P, NB])
            base = s.sb("base", [P, NB])
            with ExitStack() as stage:
                constants(nc, Room(nc, stage, "const"), c)
            with ExitStack() as stage:
                project_and_count(nc, Room(nc, stage, "project"), c, x, src, dst, Wqkv, bqkv, e, q_dram, kv_dram, rec_dram, counts)
            with ExitStack() as stage:
                place_nodes(nc, Room(nc, stage, "place"), c, counts, base, blocks_dram)
            with ExitStack() as stage:
                sort_edges(nc, Room(nc, stage, "sort"), c, e, edge_attr, base, rec_dram)
        packed = k.sb("packed", [1, ST // 4], I32)
        sums = k.sb("sums", [P, NB, DIM + H])
        with ExitStack() as stage:
            attend(nc, Room(nc, stage, "attend"), c, Wk_rpe, bk_rpe, Wq_rpe, bq_rpe, q_dram, kv_dram, rec_dram, blocks_dram, packed, sums)
        stalk = k.sb("stalk", [P, NB, STALK])
        flow = k.sb("flow", [P, NB, STALK])
        with ExitStack() as stage:
            finish_attention(nc, Room(nc, stage, "settle"), c, x, sums, W_r, b_r, stalk, stalks_dram)
        with ExitStack() as stage:
            diffuse(nc, Room(nc, stage, "diffuse"), c, stalk, stalks_dram, rec_dram, packed, flow)
        with ExitStack() as stage:
            finish(nc, Room(nc, stage, "finish"), c, sums, flow, W_o, b_o, out)


_INS = ['x', 'src', 'dst', 'edge_attr_18', 'L0_gnn_Wqkv', 'L0_gnn_bqkv', 'L0_gnn_Wk_rpe', 'L0_gnn_bk_rpe',
        'L0_gnn_Wq_rpe', 'L0_gnn_bq_rpe', 'L1_gnn_W_r', 'L1_gnn_b_r', 'L1_gnn_W_o', 'L1_gnn_b_o']
_OUTS = [((N, DIM), 'float32')]
_SCRATCH = [("queries", (NB, P, DH), 'float32'), ("kv", (NB * P, DH + DIM), 'float32'), ("records", (ST * P, REC), 'float32'),
            ("tile_blocks", (P * TPP,), 'int32'), ("stalks", (NB * P, STALK), 'float32')]


def kernel(**inputs):
    import numpy as _np
    import concourse.bacc as _bacc
    from concourse import mybir as _mybir
    from concourse.bass_utils import run_bass_kernel_spmd as _run

    nc = _bacc.Bacc("TRN2", target_bir_lowering=False, num_devices=1)
    arrays, args = {}, []
    for name in _INS:
        a = _np.ascontiguousarray(inputs[name])
        arrays[f"in_{name}_dram"] = a
        args.append(nc.dram_tensor(f"in_{name}_dram", a.shape, _mybir.dt.from_np(a.dtype), kind="ExternalInput").ap())
    for i, (shape, dtype) in enumerate(_OUTS):
        args.append(nc.dram_tensor(f"out_{i}_dram", shape, _mybir.dt.from_np(_np.dtype(dtype)), kind="ExternalOutput").ap())
    scratch = [nc.dram_tensor(f"{name}_dram", shape, _mybir.dt.from_np(_np.dtype(dtype)), kind="Internal").ap()
               for name, shape, dtype in _SCRATCH]
    graph_network(nc, *args, scratch)
    r = _run(nc, [arrays], core_ids=[0])
    return r.results[0]["out_0_dram"]
```

```python
import concourse.bass as bass
from concourse import mybir
from concourse.alu_op_type import AluOpType as ALU
from contextlib import ExitStack

F32 = mybir.dt.float32
BF16 = mybir.dt.bfloat16
I32 = mybir.dt.int32
ACT = mybir.ActivationFunctionType
AX = mybir.AxisListType

P = 128
N, E = 12500, 200000
DIM, H, D, RPE, STALK = 256, 16, 8, 18, 4
DH, DV = H * D, DIM // H
HV = DV + 1
NB = -(-N // P)
NLAST = N - (NB - 1) * P
SCALE = float(D) ** -0.5
SOFT_EPS, NORM_EPS = 1e-16, 1e-5
FAR = 1e30

CT = 16
FULL = E // (P * CT)
NCH = NB
LAST_T = 12
LAST_P = (E - FULL * P * CT) // LAST_T
assert FULL + 1 == NCH and LAST_P * LAST_T + FULL * P * CT == E

G = 8
GROUPS = 6 * -(-((E + (P - 1) * NB) // P) // (6 * G))
ST = G * GROUPS
TPP = -(-ST // P)
ATT = RPE + 1
LOC = (3 * ATT + 1) // 2
DST = LOC + 1
REC = DST + 1
BLANK = 56
assert ST % BLANK == 0
assert NB * P > N


def need(engine, sem, count):
    if not (isinstance(count, int) and count <= 0):
        engine.wait_ge(sem, count)


def rounds(engine, n, body):
    body(0)
    with engine.Fori(1, n) as i:
        body(i)


def rounds_ahead(engine, n, body):
    body(0, False)
    with engine.Fori(1, n - 1) as i:
        body(i, False)
    body(n - 1, True)


class Room:
    def __init__(self, nc, stack, stage):
        self.nc, self.stack, self.stage = nc, stack, stage

    def sb(self, name, shape, dt=F32):
        return self.stack.enter_context(self.nc.sbuf_tensor(f"{self.stage}_{name}", shape, dt))

    def ps(self, name, shape, dt=F32):
        return self.stack.enter_context(self.nc.psum_tensor(f"{self.stage}_{name}", shape, dt))

    def sem(self, name):
        return self.stack.enter_context(self.nc.semaphore(f"{self.stage}_{name}"))


def constants(nc, k, c):
    built = k.sem("built")
    counted = k.sem("counted")
    with nc.Block() as block:
        @block.gpsimd
        def _(pool):
            nc.gpsimd.memset(c["ones"][:, :], 1.0).then_inc(built, 1)
            nc.gpsimd.memset(c["zeros"][:, :], 0.0).then_inc(built, 1)
            nc.gpsimd.iota(c["row_i"][:, :], [[1, P]], base=0, channel_multiplier=0).then_inc(counted, 1)
            pool.wait_ge(built, 2)
            nc.gpsimd.affine_select(out=c["ident"][:, :], in_=c["zeros"][:, :], compare_op=ALU.not_equal,
                                    fill=1.0, base=0, pattern=[[-1, P]], channel_multiplier=1).then_inc(built, 1)
            nc.gpsimd.affine_select(out=c["before"][:, :], in_=c["ones"][:, :], compare_op=ALU.is_gt,
                                    fill=0.0, base=0, pattern=[[1, P]], channel_multiplier=-1).then_inc(built, 1)
            nc.gpsimd.affine_select(out=c["after"][:, :], in_=c["ones"][:, :], compare_op=ALU.is_gt,
                                    fill=0.0, base=0, pattern=[[-1, P]], channel_multiplier=1).then_inc(built, 1)
            pool.wait_ge(built, 5)

        @block.vector
        def _(dve):
            dve.wait_ge(counted, 1)
            nc.vector.tensor_copy(c["row"][:, :], c["row_i"][:, :]).then_inc(counted, 1)
            nc.vector.tensor_copy(c["row_bf"][:, :], c["row_i"][:, :])
            dve.wait_ge(built, 5)
            nc.vector.tensor_copy(c["ident_bf"][:, :], c["ident"][:, :])
            nc.vector.tensor_copy(c["zeros_bf"][:, :], c["zeros"][:, :])


def spread(ap, n):
    p, a = ap.shape
    return ap.unsqueeze(2).to_broadcast([p, a, n])


def over(ap, n):
    p, a = ap.shape
    return ap.unsqueeze(1).to_broadcast([p, n, a])


def project_and_count(nc, k, c, x, src, dst, Wqkv, bqkv, e, q_dram, kv_dram, rec_dram, counts):
    w = k.sb("w", [P, 2, DH * 2 + DIM])
    bias = k.sb("bias", [1, DH * 2 + DIM])
    bias_left = k.sb("bias_left", [1, DH * 2 + DIM])
    bias_parts = k.sb("bias_parts", [1, 3, DH * 2 + DIM], BF16)
    bias_rows = k.sb("bias_rows", [3, DH * 2 + DIM], BF16)
    ones_bf = k.sb("ones_bf", [3, P], BF16)
    xs = k.sb("x", [P, 2, DIM])
    xT = k.sb("xT", [P, 2, DIM])
    q = k.sb("q", [P, 2, DH])
    kv = k.sb("kv", [P, 2, DH + DIM])
    blank = k.sb("blank", [P, BLANK, REC])
    scratch = k.sb("scratch", [P, NCH * CT], I32)
    scratch2 = k.sb("scratch2", [P, NCH * CT], I32)
    at_bf = k.sb("at_bf", [P, NCH * CT], BF16)
    of_bf = k.sb("of_bf", [P, NCH * CT], BF16)
    hot_p = k.sb("hot_p", [P, 2, CT, P], BF16)
    hot_b = k.sb("hot_b", [P, 2, CT, NB], BF16)
    xT_ps = [k.ps(f"xT_ps{h}", [P, DIM]) for h in range(2)]
    qkv_ps = [k.ps(f"qkv_ps{h}", [P, DH * 2 + DIM]) for h in range(2)]
    count_ps = k.ps("count_ps", [P, NB])
    padded = k.sem("padded")
    weights_in = k.sem("weights_in")
    bias_step = k.sem("bias_step")
    bias_placed = k.sem("bias_placed")
    edges_in = k.sem("edges_in")
    x_in = [k.sem(f"x_in{h}") for h in range(2)]
    transposed = k.sem("transposed")
    xT_copied = k.sem("xT_copied")
    projected = k.sem("projected")
    q_copied = k.sem("q_copied")
    kv_copied = k.sem("kv_copied")
    rows_out = [k.sem(f"rows_out{h}") for h in range(2)]
    blanks_out = k.sem("blanks_out")
    index_step = k.sem("index_step")
    hot_ready = k.sem("hot_ready")
    counted = k.sem("counted")
    all_counted = k.sem("all_counted")
    BLANKS = ST // BLANK

    with nc.Block() as block:
        @block.gpsimd
        def _(pool):
            nc.gpsimd.memset(e["src"][:, NCH - 1, :], -1).then_inc(padded, 1)
            nc.gpsimd.memset(e["dst"][:, NCH - 1, :], 0).then_inc(padded, 1)
            nc.gpsimd.memset(blank[:, :, :], 0.0).then_inc(padded, 1)
            pool.wait_ge(padded, 3)
            nc.gpsimd.memset(blank[:, :, LOC:LOC + 1], -1.0).then_inc(padded, 1)
            nc.gpsimd.memset(blank[:, :, DST:DST + 1].bitcast(I32), NB * P - 1).then_inc(padded, 1)

        @block.sync
        def _(sp):
            edges = [(e["src"], src), (e["dst"], dst)]
            sp.dma_start(e["src"][:, 0:FULL, :], src[0:FULL * P * CT].rearrange("(c p j) -> p c j", p=P, j=CT)).then_inc(edges_in, 16)
            sp.wait_ge(padded, 5)
            for to, of in edges:
                sp.dma_start(to[0:LAST_P, NCH - 1, 0:LAST_T],
                             of[FULL * P * CT:E].rearrange("(p j) -> p j", j=LAST_T)).then_inc(edges_in, 16)
            sp.dma_start(w[:, :, :], Wqkv.rearrange("(a p) n -> p a n", p=P)).then_inc(weights_in, 16)
            sp.dma_start(bias[:, :], bqkv.rearrange("(a n) -> a n", a=1)).then_inc(weights_in, 16)
            sp.dma_start(e["dst"][:, 0:FULL, :], dst[0:FULL * P * CT].rearrange("(c p j) -> p c j", p=P, j=CT)).then_inc(edges_in, 16)

            sp.wait_ge(bias_step, 5)
            for n in range(3):
                sp.dma_start(bias_rows[n:n + 1, :], bias_parts[:, n]).then_inc(bias_placed, 16)

            def load(b, h, i, rows=P):
                need(sp, transposed, 2 * i + h - 1)
                sp.dma_start(xs[0:rows, h, :], x[bass.ds(b * P, rows), :]).then_inc(x_in[h], 16)
            load(0, 0, 0)
            load(1, 1, 0)
            with sp.Fori(1, NB // 2 - 1) as i:
                for h in range(2):
                    load(2 * i + h, h, i)
            load(NB - 2, 0, NB // 2 - 1)
            load(NB - 1, 1, NB // 2 - 1, NLAST)
            for n in range(BLANKS):
                sp.dma_start(rec_dram[n * P * BLANK:(n + 1) * P * BLANK, :].rearrange("(p r) w -> p r w", p=P),
                             blank[:, :, :]).then_inc(blanks_out, 16)
            sp.wait_ge(blanks_out, 16 * BLANKS)
            sp.wait_ge(edges_in, 64)

        @block.vector
        def _(dve):
            nc.vector.memset(ones_bf[:, :], 1.0).then_inc(bias_step, 1)
            dve.wait_ge(weights_in, 32)
            nc.vector.tensor_copy(bias_parts[:, 0], bias[:, :]).then_inc(bias_step, 1)
            dve.wait_ge(bias_step, 2)
            nc.vector.tensor_tensor(bias_left[:, :], bias[:, :], bias_parts[:, 0], ALU.subtract).then_inc(bias_step, 1)
            dve.wait_ge(bias_step, 3)
            nc.vector.tensor_copy(bias_parts[:, 1], bias_left[:, :]).then_inc(bias_step, 1)
            dve.wait_ge(bias_step, 4)
            nc.vector.tensor_tensor(bias_parts[:, 2], bias_left[:, :], bias_parts[:, 1], ALU.subtract).then_inc(bias_step, 1)
            dve.wait_ge(edges_in, 64)
            flat = e["src"][:, :, :].rearrange("p c j -> p (c j)")
            nc.vector.tensor_copy(e["src_f"][:, :], flat).then_inc(index_step, 1)
            nc.vector.tensor_scalar(scratch[:, :], flat, P - 1, None, ALU.bitwise_and).then_inc(index_step, 1)
            nc.vector.tensor_scalar(scratch2[:, :], flat, 7, None, ALU.arith_shift_right).then_inc(index_step, 1)
            dve.wait_ge(index_step, 3)
            nc.vector.tensor_copy(at_bf[:, :], scratch[:, :]).then_inc(index_step, 1)
            nc.vector.tensor_copy(of_bf[:, :], scratch2[:, :]).then_inc(index_step, 1)
            nc.vector.tensor_copy(e["at"][:, :], scratch[:, :])
            nc.vector.tensor_copy(e["of"][:, :], scratch2[:, :])
            dve.wait_ge(index_step, 5)

            def body(i):
                for h in range(2):
                    g = 2 * i + h
                    need(dve, counted, g - 1)
                    nc.vector.tensor_tensor(hot_p[:, h], over(c["row_bf"][:, :], CT),
                                            spread(at_bf[:, bass.ds(g * CT, CT)], P), ALU.is_equal).then_inc(hot_ready, 1)
                    nc.vector.tensor_tensor(hot_b[:, h], over(c["row_bf"][:, 0:NB], CT),
                                            spread(of_bf[:, bass.ds(g * CT, CT)], NB), ALU.is_equal).then_inc(hot_ready, 1)
            rounds(dve, NCH // 2, body)

        @block.tensor
        def _(pe):
            pe.wait_ge(weights_in, 32)
            pe.wait_ge(bias_placed, 48)
            nc.tensor.matmul(count_ps[:, :], c["zeros_bf"][:, :], c["zeros_bf"][:, 0:NB], start=True, stop=False)

            def turn(g, h, i):
                pe.wait_ge(x_in[h], 16 * i + 16)
                need(pe, xT_copied, g - 1)
                for a in range(2):
                    last = nc.tensor.transpose(xT_ps[h][:, a * P:(a + 1) * P], xs[:, h, a * P:(a + 1) * P], c["ident"][:, :])
                last.then_inc(transposed, 1)
            turn(0, 0, 0)

            def body(i, last_round):
                for h in range(2):
                    g = 2 * i + h
                    if not (last_round and h == 1):
                        turn(g + 1, 1 - h, i + h)
                    pe.wait_ge(hot_ready, 2 * g + 2)
                    for j in range(CT):
                        last = nc.tensor.matmul(count_ps[:, :], hot_p[:, h, j], hot_b[:, h, j], start=False, stop=False)
                    last.then_inc(counted, 1)
                    pe.wait_ge(xT_copied, g + 1)
                    need(pe, kv_copied, g - 1)
                    for a in range(2):
                        nc.tensor.matmul(qkv_ps[h][:, :], xT[:, h, a * P:(a + 1) * P], w[:, a], start=(a == 0), stop=False)
                    nc.tensor.matmul(qkv_ps[h][:, :], ones_bf[:, :], bias_rows[:, :], start=False, stop=True).then_inc(projected, 1)
            rounds_ahead(pe, NB // 2, body)
            nc.tensor.matmul(count_ps[:, :], c["zeros_bf"][:, :], c["zeros_bf"][:, 0:NB], start=False, stop=True).then_inc(all_counted, 1)

        @block.scalar
        def _(act):
            def copy_turned(g, h):
                act.wait_ge(transposed, g + 1)
                need(act, projected, g - 1)
                nc.scalar.activation(xT[:, h, :], xT_ps[h][:, :], ACT.Copy).then_inc(xT_copied, 1)
            copy_turned(0, 0)

            def body(i, last_round):
                for h in range(2):
                    g = 2 * i + h
                    if not (last_round and h == 1):
                        copy_turned(g + 1, 1 - h)
                    act.wait_ge(projected, g + 1)
                    need(act, rows_out[h], 32 * i)
                    nc.scalar.activation(q[:, h, :], qkv_ps[h][:, 0:DH], ACT.Copy, scale=SCALE).then_inc(q_copied, 1)
                    nc.scalar.activation(kv[:, h, :], qkv_ps[h][:, DH:], ACT.Copy).then_inc(kv_copied, 1)
                    act.wait_ge(q_copied, g + 1)
                    act.dma_start(q_dram[bass.ds(g, 1), :, :].rearrange("a p d -> p (a d)"), q[:, h, :]).then_inc(rows_out[h], 16)
                    act.wait_ge(kv_copied, g + 1)
                    act.dma_start(kv_dram[bass.ds(g * P, P), :], kv[:, h, :]).then_inc(rows_out[h], 16)
            rounds_ahead(act, NB // 2, body)
            act.wait_ge(all_counted, 1)
            nc.scalar.activation(counts[:, :], count_ps[:, :], ACT.Copy).then_inc(all_counted, 1)
            for h in range(2):
                act.wait_ge(rows_out[h], 32 * (NB // 2))
            act.wait_ge(all_counted, 2)


def place_nodes(nc, k, c, counts, base, blocks_dram):
    within = k.ps("within", [P, NB])
    total = k.ps("total", [P, NB])
    filled = k.sb("filled", [P, NB])
    filled_i = k.sb("filled_i", [P, NB], I32)
    tiles_i = k.sb("tiles_i", [P, NB], I32)
    tiles = k.sb("tiles", [P, NB])
    ends = k.sb("ends", [P, NB])
    starts = k.sb("starts", [P, NB])
    number_i = k.sb("number_i", [P, TPP], I32)
    number = k.sb("number", [P, TPP])
    passed = k.sb("passed", [P, TPP, NB])
    block_f = k.sb("block_f", [P, TPP])
    block_i = k.sb("block_i", [P, TPP], I32)
    summed = k.sem("summed")
    numbered = k.sem("numbered")
    step = k.sem("step")
    found = k.sem("found")
    blocks_out = k.sem("blocks_out")
    with nc.Block() as block:
        @block.gpsimd
        def _(pool):
            nc.gpsimd.iota(number_i[:, :], [[1, TPP]], base=0, channel_multiplier=TPP).then_inc(numbered, 1)

        @block.tensor
        def _(pe):
            nc.tensor.matmul(within[:, :], c["before"][:, :], counts[:, :], start=True, stop=True)
            nc.tensor.matmul(total[:, :], c["ones"][:, :], counts[:, :], start=True, stop=True).then_inc(summed, 1)

        @block.vector
        def _(dve):
            steps = [0]

            def then(ins):
                steps[0] += 1
                ins.then_inc(step, 1)
                dve.wait_ge(step, steps[0])
            dve.wait_ge(numbered, 1)
            then(nc.vector.tensor_copy(number[:, :], number_i[:, :]))
            dve.wait_ge(summed, 1)
            then(nc.vector.tensor_scalar(filled[:, :], total[:, :], float(P - 1), None, ALU.add))
            then(nc.vector.tensor_copy(filled_i[:, :], filled[:, :]))
            then(nc.vector.tensor_scalar(tiles_i[:, :], filled_i[:, :], 7, None, ALU.logical_shift_right))
            then(nc.vector.tensor_copy(tiles[:, :], tiles_i[:, :]))
            then(nc.vector.tensor_tensor_scan(ends[:, :], c["ones"][:, 0:NB], tiles[:, :], 0.0, ALU.mult, ALU.add))
            then(nc.vector.tensor_tensor(starts[:, :], ends[:, :], tiles[:, :], ALU.subtract))
            then(nc.vector.scalar_tensor_tensor(base[:, :], starts[:, :], float(P), within[:, :], ALU.mult, ALU.add))
            then(nc.vector.tensor_tensor(passed[:, :, :], over(ends[:, :], TPP), spread(number[:, :], NB), ALU.is_le))
            then(nc.vector.tensor_reduce(block_f[:, :], passed[:, :, :], AX.X, ALU.add))
            then(nc.vector.tensor_scalar(block_f[:, :], block_f[:, :], float(NB - 1), None, ALU.min))
            nc.vector.tensor_copy(block_i[:, :], block_f[:, :]).then_inc(found, 1)

        @block.sync
        def _(sp):
            sp.wait_ge(found, 1)
            sp.dma_start(blocks_dram.rearrange("(p j) -> p j", j=TPP), block_i[:, :]).then_inc(blocks_out, 16)
            sp.wait_ge(blocks_out, 16)


def sort_edges(nc, k, c, e, edge_attr, base, rec_dram):
    attr = k.sb("attr", [P, 2, G, RPE])
    rest = k.sb("rest", [P, G, RPE])
    rec = k.sb("rec", [P, 2, G, REC])
    parts = rec[:, :, :, :].bitcast(BF16)
    high, middle, low = (parts[:, :, :, n * ATT:n * ATT + RPE] for n in range(3))
    at_bf = k.sb("at_bf", [P, 2, G], BF16)
    of_bf = k.sb("of_bf", [P, 2, G], BF16)
    src_f = k.sb("src_f", [P, 2, G])
    hot_p = k.sb("hot_p", [P, 2, G, P], BF16)
    hot_b = k.sb("hot_b", [P, 2, G, NB], BF16)
    hot_pT = k.sb("hot_pT", [P, 2, P])
    table = k.sb("table", [P, 2, NB])
    junk_v = k.sb("junk_v", [P, G, NB], BF16)
    junk_r = k.sb("junk_r", [P, G, P], BF16)
    first = k.sb("first", [P, 2, G])
    rank = k.sb("rank", [P, 2, G])
    place_i = k.sb("place_i", [P, G], I32)
    row_hi = k.sb("row_hi", [P, G], I32)
    row_p = k.sb("row_p", [P, G], I32)
    row_t = k.sb("row_t", [P, G], I32)
    row_pt = k.sb("row_pt", [P, G], I32)
    row = k.sb("row", [P, 2, G], I32)
    hot_pT_ps = [k.ps(f"hot_pT_ps{s}", [P, P], BF16) for s in range(2)]
    other_ps = [k.ps(f"other_ps{s}", [P, P]) for s in range(2)]
    first_ps = [k.ps(f"first_ps{s}", [P, NB]) for s in range(2)]
    table_ps = k.ps("table_ps", [P, NB])
    one_set = k.sem("one_set")
    attr_in = [k.sem(f"attr_in{h}") for h in range(2)]
    copied_in = k.sem("copied_in")
    hot_ready = k.sem("hot_ready")
    turned = k.sem("turned")
    turned_copied = k.sem("turned_copied")
    table_made = k.sem("table_made")
    table_copied = k.sem("table_copied")
    looked_up = k.sem("looked_up")
    tile_ranked = k.sem("tile_ranked")
    step = k.sem("step")
    scattered = [k.sem(f"scattered{h}") for h in range(2)]
    slot_free = k.sem("slot_free")
    pool_turn = k.sem("pool_turn")
    STEPS = 12

    with nc.Block() as block:
        @block.sync
        def _(sp):
            sp.wait_ge(one_set, 3)

            def load(i, chunk, parts=P, width=CT):
                for h in range(2):
                    n = min(G, width - h * G)
                    need(sp, step, STEPS * (2 * i + h - 1))
                    rows = edge_attr[bass.ds(chunk * P * CT, parts * width), :].rearrange("(p j) w -> p j w", j=width)
                    sp.dma_start(attr[0:parts, h, 0:n, :], rows[:, h * G:h * G + n, :]).then_inc(attr_in[h], 16)
            load(0, 0)
            with sp.Fori(1, FULL) as i:
                load(i, i)
            load(FULL, FULL, LAST_P, LAST_T)

        @block.vector
        def _(dve):
            nc.vector.memset(attr[:, :, :, :], 0.0).then_inc(one_set, 1)
            nc.vector.memset(parts[:, :, :, :], 0.0).then_inc(one_set, 1)
            dve.wait_ge(one_set, 2)
            nc.vector.memset(parts[:, :, :, RPE:ATT], 1.0).then_inc(one_set, 1)

            def copy_in(g, h):
                cols = bass.ds(g * G, G)
                need(dve, table_made, G * (g - 1) + 1 if not isinstance(g, int) or g > 1 else 0)
                nc.vector.tensor_scalar(at_bf[:, h], e["at"][:, cols], 1.0, None, ALU.mult).then_inc(copied_in, 1)
                nc.vector.tensor_scalar(of_bf[:, h], e["of"][:, cols], 1.0, None, ALU.mult).then_inc(copied_in, 1)
                nc.vector.tensor_scalar(src_f[:, h], e["src_f"][:, cols], 1.0, None, ALU.mult).then_inc(copied_in, 1)

            def light_p(g, h, z):
                half = slice(z * G // 2, (z + 1) * G // 2)
                dve.wait_ge(copied_in, 3 * g + 3)
                nc.vector.tensor_tensor(hot_p[:, h, half], over(c["row_bf"][:, :], G // 2), spread(at_bf[:, h, half], P), ALU.is_equal).then_inc(hot_ready, 1)

            def light_b(g, h, z):
                half = slice(z * G // 2, (z + 1) * G // 2)
                nc.vector.tensor_tensor(hot_b[:, h, half], over(c["row_bf"][:, 0:NB], G // 2), spread(of_bf[:, h, half], NB), ALU.is_equal).then_inc(hot_ready, 1)

            def add_rank(g, h):
                need(dve, slot_free, g - 1)
                nc.vector.tensor_tensor(place_i[:, :], first[:, h], rank[:, h], ALU.add).then_inc(step, 1)
                dve.wait_ge(attr_in[h], 8 * (g - h) + 16)
                nc.vector.tensor_scalar(high[:, h], attr[:, h], 1.0, None, ALU.mult).then_inc(step, 1)

            def cut_place(g, h):
                dve.wait_ge(step, STEPS * g + 2)
                nc.vector.tensor_scalar(row_hi[:, :], place_i[:, :], 10, 10, ALU.logical_shift_right, ALU.logical_shift_left).then_inc(step, 1)
                nc.vector.tensor_scalar(row_p[:, :], place_i[:, :], P - 1, 3, ALU.bitwise_and, ALU.logical_shift_left).then_inc(step, 1)
                nc.vector.tensor_scalar(row_t[:, :], place_i[:, :], 7, G - 1, ALU.logical_shift_right, ALU.bitwise_and).then_inc(step, 1)
                nc.vector.tensor_tensor(rest[:, :, :], attr[:, h], high[:, h], ALU.subtract).then_inc(step, 1)

            def middle_part(g, h):
                dve.wait_ge(step, STEPS * g + 6)
                nc.vector.tensor_tensor(row_pt[:, :], row_p[:, :], row_t[:, :], ALU.bitwise_or).then_inc(step, 1)
                nc.vector.tensor_scalar(middle[:, h], rest[:, :, :], 1.0, None, ALU.mult).then_inc(step, 1)
                nc.vector.tensor_scalar(rec[:, h, :, LOC], e["at"][:, bass.ds(g * G, G)], 1.0, None, ALU.mult).then_inc(step, 1)
                nc.vector.tensor_scalar(rec[:, h, :, DST].bitcast(I32), e["dst"][:, :, :].rearrange("p c j -> p (c j)")[:, bass.ds(g * G, G)],
                                        1.0, None, ALU.mult).then_inc(step, 1)

            def low_part(g, h):
                dve.wait_ge(step, STEPS * g + 8)
                nc.vector.tensor_tensor(low[:, h], rest[:, :, :], middle[:, h], ALU.subtract).then_inc(step, 1)
                nc.vector.tensor_tensor(row[:, h], row_hi[:, :], row_pt[:, :], ALU.bitwise_or).then_inc(step, 1)
            copy_in(0, 0)
            for z in range(2):
                light_p(0, 0, z)
                light_b(0, 0, z)

            def body(i, last):
                for h in range(2):
                    g = 2 * i + h
                    starts = isinstance(g, int) and g == 0
                    for j in range(G):
                        t = G * g + j
                        dve.wait_ge(turned, t + 1)
                        nc.vector.scalar_tensor_tensor(junk_r[:, j], other_ps[j % 2][:, :], src_f[:, h, j:j + 1], c["after"][:, :],
                                                       ALU.is_equal, ALU.mult, accum_out=rank[:, h, j:j + 1]).then_inc(tile_ranked, 1)
                        if not (last and h == 1):
                            if j == 0:
                                copy_in(g + 1, 1 - h)
                            elif j in (1, 2):
                                light_p(g + 1, 1 - h, j - 1)
                            elif j in (3, 4):
                                light_b(g + 1, 1 - h, j - 3)
                        if not starts:
                            if j == 4:
                                add_rank(g - 1, 1 - h)
                            elif j == 5:
                                cut_place(g - 1, 1 - h)
                            elif j == 6:
                                middle_part(g - 1, 1 - h)
                            elif j == 7:
                                low_part(g - 1, 1 - h)
                        dve.wait_ge(looked_up, t + 1)
                        nc.vector.scalar_tensor_tensor(junk_v[:, j], first_ps[j % 2][:, :], 1.0, hot_b[:, h, j],
                                                       ALU.mult, ALU.mult, accum_out=first[:, h, j:j + 1]).then_inc(tile_ranked, 1)
                    dve.wait_ge(tile_ranked, 2 * G * (g + 1))
                if last:
                    for part in (add_rank, cut_place, middle_part, low_part):
                        part(g, h)
            rounds_ahead(dve, NCH, body)

        @block.tensor
        def _(pe):
            nc.tensor.matmul(table_ps[:, :], c["ident"][:, :], base[:, :], start=True, stop=True).then_inc(table_made, 1)

            def turn(g, h, j):
                t = G * g + j
                if j == 0:
                    pe.wait_ge(hot_ready, 4 * g + 4)
                need(pe, turned_copied, t - 1)
                nc.tensor.transpose(hot_pT_ps[j % 2][:, :], hot_p[:, h, j], c["ident_bf"][:, :])
                need(pe, tile_ranked, 2 * t - 3)
                nc.tensor.transpose(other_ps[j % 2][:, :], src_f[:, h, j:j + 1].to_broadcast([P, P]), c["ident"][:, :]).then_inc(turned, 1)
            turn(0, 0, 0)
            turn(0, 0, 1)

            def body(i, last):
                for h in range(2):
                    g = 2 * i + h
                    for j in range(G):
                        t = G * g + j
                        pe.wait_ge(table_copied, t + 1)
                        nc.tensor.matmul(table_ps[:, :], hot_p[:, h, j], hot_b[:, h, j], start=False, stop=True, skip_group_check=True).then_inc(table_made, 1)
                        pe.wait_ge(turned_copied, t + 1)
                        need(pe, tile_ranked, 2 * (t - 1))
                        nc.tensor.matmul(first_ps[j % 2][:, :], hot_pT[:, j % 2], table[:, j % 2], start=True, stop=True).then_inc(looked_up, 1)
                        if j + 2 < G:
                            turn(g, h, j + 2)
                        elif not (last and h == 1):
                            turn(g + 1, 1 - h, j + 2 - G)
            rounds_ahead(pe, NCH, body)

        @block.scalar
        def _(act):
            def body(i):
                for h in range(2):
                    for j in range(G):
                        t = G * (2 * i + h) + j
                        act.wait_ge(table_made, t + 1)
                        need(act, looked_up, t - 1)
                        nc.scalar.activation(table[:, j % 2], table_ps[:, :], ACT.Copy).then_inc(table_copied, 1)
                        act.wait_ge(turned, t + 1)
                        nc.scalar.activation(hot_pT[:, j % 2], hot_pT_ps[j % 2][:, :], ACT.Copy).then_inc(turned_copied, 1)
            rounds(act, NCH, body)

        @block.gpsimd
        def _(pool):
            pool.wait_ge(one_set, 3)

            def group(i, h, parts=P, tiles=G):
                g = 2 * i + h
                pool.wait_ge(step, STEPS * (g + 1))
                pool.sem_inc(pool_turn)
                for j in range(tiles):
                    nc.gpsimd.indirect_dma_start(rec_dram[:, :], bass.IndirectOffsetOnAxis(ap=row[0:parts, h, j:j + 1], axis=0),
                                                 rec[0:parts, h, j], None).then_inc(scattered[h], 16)
                    if j == 2 and not (isinstance(g, int) and g == 0):
                        pool.wait_ge(scattered[1 - h], 16 * G * (i + h))
                        pool.sem_inc(slot_free)

            def body(i):
                for h in range(2):
                    group(i, h)
            body(0)
            with pool.Fori(1, FULL) as i:
                body(i)
            group(FULL, 0, LAST_P, G)
            group(FULL, 1, LAST_P, LAST_T - G)
            pool.wait_ge(scattered[0], 16 * G * (FULL + 1))
            pool.wait_ge(scattered[1], 16 * (G * FULL + LAST_T - G))


class Turn:
    def __init__(self, i, r):
        self.i, self.r = i + r // 3, r % 3
        self.g = 3 * self.i + self.r
        self.slot = self.r
        self.used = self.i + 1

    def after(self, n):
        return Turn(self.i, self.r + n)


def walk(engine, first, last, groups, step):
    def plain(g):
        step(Turn(g // 3, g % 3), lambda n: 0 <= g + n < groups)
    for g in range(first, 6):
        plain(g)
    with engine.Fori(2, groups // 3 - 1) as i:
        for r in range(3):
            step(Turn(i, r), lambda n: True)
    for g in range(groups - 3, last + 1):
        plain(g)


def packed_blocks(engine, packed, g):
    words = [engine.value_load(packed[0:1, bass.ds(2 * g + n, 1)]) for n in range(2)]
    return [((words[t // 4] >> (8 * (t % 4))) & 127).with_bounds(min_val=0, max_val=NB - 1) for t in range(G)]


def attend(nc, k, c, Wk_rpe, bk_rpe, Wq_rpe, bq_rpe, q_dram, kv_dram, rec_dram, blocks_dram, packed, sums):
    SUM = DIM + H
    K6 = 6 * ATT
    split = k.sb("split", [ATT, 3, 2 * DH], BF16)
    rpe6 = k.sb("rpe6", [K6, 2 * DH], BF16)
    rec = k.sb("rec", [P, 3, G, REC])
    parts = rec[:, :, :, :].bitcast(BF16)
    tile_block = k.sb("tile_block", [P, TPP * P], I32)
    lifted = k.sb("lifted", [1, ST // 4], I32)
    new_block = k.sb("new_block", [P, ST])
    q = k.sb("q", [P, G, DH])
    kv = k.sb("kv", [P, 3, G, DH + SUM])
    hot = k.sb("hot", [P, 3, G, P])
    hotT = k.sb("hotT", [P, 3, G, P])
    rec6 = k.sb("rec6", [P, G, 6, ATT], BF16)
    recT = k.sb("recT", [K6, G, P], BF16)
    ident_bf = k.sb("ident_bf", [P, P], BF16)
    loc16 = k.sb("loc16", [P, G, H])
    locT = k.sb("locT", [P, 3, P])
    fresh = k.sb("fresh", [P, P + 1])
    drop = k.sb("drop", [P, P])
    run = k.sb("run", [P, P])
    lasts = k.sb("lasts", [P, P])
    compat = k.sb("compat", [P, G, H])
    lastsT = k.sb("lastsT", [P, G, H + 1])
    absent = k.sb("absent", [P, G])
    ROWS = H * (G + 1)
    drop_row = k.sb("drop_row", [P, ROWS + 1])
    found_row = k.sb("found_row", [P, ROWS])
    forward = k.sb("forward", [P, ROWS])
    maxima_row = k.sb("maxima_row", [P, ROWS])
    drops, found, maxima = (row[:, 0:ROWS].rearrange("p (h t) -> p h t", h=H) for row in (drop_row, found_row, maxima_row))
    fall = k.sb("fall", [P, H])
    keep = k.sb("keep", [P, H])
    shifted = k.sb("shifted", [P, G, H])
    qk_ps = [k.ps(f"qk_ps{s}", [P, 2, 2 * DH]) for s in range(2)]
    hotT_ps = k.ps("hotT_ps", [P, 4, P])
    recT_ps = k.ps("recT_ps", [P, G, P], BF16)
    sum_ps = [k.ps(f"sum_ps{s}", [P, 512]) for s in range(2)]
    turn_ps = k.ps("turn_ps", [P, 4, P])
    node_ps = k.ps("node_ps", [P, 512])
    lastsT_ps = node_ps[:, 0:P]
    tops = node_ps[:, P:P + G * (H + 1)].rearrange("p (t w) -> p t w", t=G)
    spread_ps = node_ps[:, 3 * P:4 * P].rearrange("p (t w) -> p t w", t=G)

    rpe_in = k.sem("rpe_in")
    rpe_step = k.sem("rpe_step")
    rpe_placed = k.sem("rpe_placed")
    cleared = k.sem("cleared")
    blocks_in = k.sem("blocks_in")
    packing = k.sem("packing")
    rec_in = [k.sem(f"rec_in{s}") for s in range(3)]
    q_in = [k.sem(f"q_in{u}") for u in range(G // 2)]
    gathered = [k.sem(f"gathered{s}") for s in range(3)]
    pool_turn = k.sem("pool_turn")
    sp_turn = k.sem("sp_turn")
    rec6_built = k.sem("rec6_built")
    loc_spread = k.sem("loc_spread")
    distance = k.sem("distance")
    hot_built = k.sem("hot_built")
    hot_turned = k.sem("hot_turned")
    hot_copied = k.sem("hot_copied")
    rec_turned = k.sem("rec_turned")
    rec_copied = k.sem("rec_copied")
    loc_turned = k.sem("loc_turned")
    loc_copied = k.sem("loc_copied")
    pair_ready = k.sem("pair_ready")
    pair_keyed = k.sem("pair_keyed")
    pair_used = k.sem("pair_used")
    compat_ready = k.sem("compat_ready")
    compat_turned = k.sem("compat_turned")
    scan_step = k.sem("scan_step")
    lasts_ready = k.sem("lasts_ready")
    lasts_turned = k.sem("lasts_turned")
    lasts_copied = k.sem("lasts_copied")
    tops_ready = k.sem("tops_ready")
    maximum_step = k.sem("maximum_step")
    maximum_taken = k.sem("maximum_taken")
    maxima_spread = k.sem("maxima_spread")
    fall_ready = k.sem("fall_ready")
    keep_ready = k.sem("keep_ready")
    scaled = k.sem("scaled")
    shift_done = k.sem("shift_done")
    exp_done = k.sem("exp_done")
    weighted = k.sem("weighted")
    tile_summed = k.sem("tile_summed")
    tile_added = k.sem("tile_added")

    weights = k.sb("weights", [ATT, 2 * DH])
    left = k.sb("left", [ATT, 2 * DH])
    with nc.Block() as block:
        @block.sync
        def _(sp):
            sp.dma_start(tile_block[:, :], blocks_dram.rearrange("(a t) -> a t", a=1).to_broadcast([P, TPP * P])).then_inc(blocks_in, 16)
            sp.dma_start(weights[0:RPE, 0:DH], Wq_rpe).then_inc(rpe_in, 16)
            sp.dma_start(weights[0:RPE, DH:], Wk_rpe).then_inc(rpe_in, 16)
            sp.dma_start(weights[RPE:ATT, 0:DH], bq_rpe.rearrange("(a n) -> a n", a=1)).then_inc(rpe_in, 16)
            sp.dma_start(weights[RPE:ATT, DH:], bk_rpe.rearrange("(a n) -> a n", a=1)).then_inc(rpe_in, 16)
            sp.wait_ge(rpe_step, 5)
            for row, part in enumerate((0, 1, 2, 0, 1, 0)):
                sp.dma_start(rpe6[row * ATT:(row + 1) * ATT, :], split[:, part]).then_inc(rpe_placed, 16)
            sp.wait_ge(rpe_placed, 96)
            sp.wait_ge(rpe_in, 64)
            sp.wait_ge(blocks_in, 16)
            sp.wait_ge(packing, 7)

            def load_records(turn):
                need(sp, compat_ready, turn.g - 2)
                sp.dma_start(rec[:, turn.slot], rec_dram[bass.ds(turn.g * (G * P), G * P), :].rearrange("(p t) w -> p t w", t=G)).then_inc(rec_in[turn.slot], 16)

            def load_queries(turn):
                block_of = packed_blocks(sp, packed, turn.g)
                for u in range(G // 2):
                    if not (isinstance(turn.g, int) and turn.g == 0):
                        sp.wait_ge(pair_ready, 4 * turn.g + u - 3)
                        sp.sem_inc(sp_turn)
                    for t in (2 * u, 2 * u + 1):
                        sp.dma_start(q[:, t], q_dram[bass.ds(block_of[t], 1), :, :].rearrange("a p d -> p (a d)")).then_inc(q_in[u], 16)

            def step(turn, inside):
                load_queries(turn)
                if inside(2):
                    load_records(turn.after(2))
            load_records(Turn(0, 0))
            load_records(Turn(0, 1))
            walk(sp, 0, GROUPS - 1, GROUPS, step)

        @block.gpsimd
        def _(pool):
            def gather(turn, inside):
                pool.wait_ge(rec_in[turn.slot], 16 * turn.used)
                pool.sem_inc(pool_turn)
                if not (isinstance(turn.g, int) and turn.g < 3):
                    pool.wait_ge(tile_summed, G * (turn.g - 2))
                    pool.sem_inc(pool_turn)
                for t in range(G):
                    nc.gpsimd.indirect_dma_start(kv[:, turn.slot, t, 0:DH + DIM], None, kv_dram[:, :],
                                                 bass.IndirectOffsetOnAxis(ap=rec[:, turn.slot, t, DST:DST + 1].bitcast(I32), axis=0)).then_inc(gathered[turn.slot], 16)
            walk(pool, 0, GROUPS - 1, GROUPS, gather)

        @block.scalar
        def _(act):
            def matrices(turn):
                act.wait_ge(rec_in[turn.slot], 16 * turn.used)
                need(act, rec_turned, turn.g)
                mine = parts[:, turn.slot]
                for a, n, part in ((0, 3, 0), (3, 2, 1), (5, 1, 2)):
                    nc.scalar.activation(rec6[:, :, a:a + n], mine[:, :, part * ATT:(part + 1) * ATT].unsqueeze(2).to_broadcast([P, G, n, ATT]), ACT.Copy).then_inc(rec6_built, 1)
                need(act, loc_turned, turn.g)
                nc.scalar.activation(loc16[:, :, :], spread(rec[:, turn.slot, :, LOC], H), ACT.Copy).then_inc(loc_spread, 1)

            def one_hots(turn):
                need(act, tile_summed, G * (turn.g - 2))
                for t in range(G):
                    nc.scalar.activation(hot[:, turn.slot, t], c["row"][:, :], ACT.Abs, bias=rec[:, turn.slot, t, LOC:LOC + 1], scale=-1.0).then_inc(distance, 1)
                act.wait_ge(distance, G * (turn.g + 1))
                nc.scalar.activation(hot[:, turn.slot], hot[:, turn.slot], ACT.Relu, bias=1.0, scale=-1.0).then_inc(hot_built, 1)

            def step(turn, inside):
                g, after, then = turn.g, turn.after(1), turn.after(2)
                if inside(-1):
                    act.wait_ge(shift_done, g)
                    nc.scalar.activation(kv[:, turn.after(-1).slot, :, DH + DIM:], shifted[:, :, :], ACT.Exp).then_inc(exp_done, 1)
                if inside(1):
                    act.wait_ge(loc_turned, g + 2)
                    nc.scalar.activation(locT[:, after.slot], turn_ps[:, 0], ACT.Copy).then_inc(loc_copied, 1)
                    for z in range(2):
                        act.wait_ge(hot_turned, 2 * g + z + 3)
                        need(act, maxima_spread, g - 1)
                        nc.scalar.activation(hotT[:, after.slot, 4 * z:4 * z + 4], hotT_ps[:, :, :], ACT.Copy).then_inc(hot_copied, 1)
                        if z == 0:
                            act.wait_ge(rec_turned, g + 2)
                            need(act, pair_ready, 4 * (g + 1))
                            nc.scalar.activation(recT[:, :, :], recT_ps[0:K6, :, :], ACT.Copy).then_inc(rec_copied, 1)
                if inside(2):
                    matrices(then)
                if inside(0):
                    act.wait_ge(lasts_turned, g + 1)
                    need(act, tops_ready, g)
                    nc.scalar.activation(lastsT[:, :, 0:H], lastsT_ps.rearrange("p (t w) -> p t w", t=G), ACT.Copy).then_inc(lasts_copied, 1)
                if inside(2):
                    one_hots(then)
                if inside(0):
                    act.wait_ge(fall_ready, g + 1)
                    need(act, scaled, 2 * g)
                    nc.scalar.activation(keep[:, :], fall[:, :], ACT.Exp).then_inc(keep_ready, 1)
            walk(act, -2, GROUPS, GROUPS, step)

        @block.vector
        def _(dve):
            nc.vector.memset(sums[:, :, :], 0.0).then_inc(cleared, 1)
            nc.vector.memset(maxima_row[:, :], -FAR).then_inc(cleared, 1)
            nc.vector.memset(drop_row[:, :], -FAR).then_inc(cleared, 1)
            nc.vector.memset(new_block[:, 0:1], 0.0).then_inc(cleared, 1)
            nc.vector.memset(fresh[:, :], 1.0).then_inc(cleared, 1)
            nc.vector.memset(lastsT[:, :, H:], 1.0).then_inc(cleared, 1)
            nc.vector.tensor_copy(ident_bf[:, :], c["ident"][:, :]).then_inc(cleared, 1)
            dve.wait_ge(rpe_in, 64)
            nc.vector.tensor_copy(split[:, 0], weights[:, :]).then_inc(rpe_step, 1)
            dve.wait_ge(rpe_step, 1)
            nc.vector.tensor_tensor(left[:, :], weights[:, :], split[:, 0], ALU.subtract).then_inc(rpe_step, 1)
            dve.wait_ge(rpe_step, 2)
            nc.vector.tensor_copy(split[:, 1], left[:, :]).then_inc(rpe_step, 1)
            dve.wait_ge(rpe_step, 3)
            nc.vector.tensor_tensor(split[:, 2], left[:, :], split[:, 1], ALU.subtract).then_inc(rpe_step, 2)
            dve.wait_ge(cleared, 7)
            dve.wait_ge(blocks_in, 16)
            fours = tile_block[0:1, 0:ST].rearrange("a (w n) -> a w n", n=4)
            nc.vector.tensor_copy(packed[:, :], fours[:, :, 0]).then_inc(packing, 1)
            for n in range(1, 4):
                dve.wait_ge(packing, 2 * n - 1)
                nc.vector.tensor_scalar(lifted[:, :], fours[:, :, n], 8 * n, None, ALU.logical_shift_left).then_inc(packing, 1)
                dve.wait_ge(packing, 2 * n)
                nc.vector.tensor_tensor(packed[:, :], packed[:, :], lifted[:, :], ALU.bitwise_or).then_inc(packing, 1)
            nc.vector.tensor_tensor(new_block[:, 1:], tile_block[:, 1:ST], tile_block[:, 0:ST - 1], ALU.not_equal).then_inc(packing, 1)
            dve.wait_ge(packing, 8)
            nc.vector.tensor_scalar(new_block[:, 1:], new_block[:, 1:], -FAR, None, ALU.mult).then_inc(packing, 1)
            dve.wait_ge(packing, 9)

            def key(turn, u):
                keys = kv[:, turn.slot, 2 * u:2 * u + 2, 0:DH]
                dve.wait_ge(pair_ready, 4 * turn.g + u + 1)
                nc.vector.tensor_tensor(keys, keys, qk_ps[u % 2][:, :, DH:], ALU.add).then_inc(pair_keyed, 1)

            def ask(turn, u):
                keys = kv[:, turn.slot, 2 * u:2 * u + 2, 0:DH]
                dve.wait_ge(pair_keyed, 4 * turn.g + u + 1)
                nc.vector.tensor_tensor(keys, keys, qk_ps[u % 2][:, :, 0:DH], ALU.mult).then_inc(pair_used, 1)

            def weigh(past, u):
                pair = kv[:, past.slot, 2 * u:2 * u + 2]
                values = pair[:, :, DH:DH + DIM].rearrange("p t (h d) -> p t h d", h=H)
                nc.vector.tensor_tensor(values, values, pair[:, :, DH + DIM:].unsqueeze(3).to_broadcast([P, 2, H, DV]), ALU.mult).then_inc(weighted, 1)

            def add(past, block_of, t):
                need(dve, tile_added, G * past.g + t)
                dve.wait_ge(tile_summed, G * past.g + t + 1)
                into = sums[:, bass.ds(block_of[t], 1), :].rearrange("p a n -> p (a n)")
                nc.vector.tensor_tensor(into, into, sum_ps[t % 2][:, 0:SUM], ALU.add).then_inc(tile_added, 1)

            def step(turn, inside):
                g, past = turn.g, turn.after(-1)
                if inside(0):
                    dve.wait_ge(gathered[turn.slot], 16 * G * turn.used)
                    key(turn, 0)
                    key(turn, 1)
                    ask(turn, 0)
                    ask(turn, 1)
                if inside(-1):
                    dve.wait_ge(maxima_spread, g)
                    nc.vector.tensor_tensor(shifted[:, :, :], compat[:, :, :], spread_ps, ALU.subtract).then_inc(shift_done, 1)
                if inside(0):
                    key(turn, 2)
                    key(turn, 3)
                    ask(turn, 2)
                    ask(turn, 3)
                    dve.wait_ge(pair_used, 4 * g + 4)
                    nc.vector.tensor_reduce(compat[:, :, :], kv[:, turn.slot, :, 0:DH].rearrange("p t (h d) -> p t h d", h=H), AX.X, ALU.add).then_inc(compat_ready, 1)
                if inside(-1):
                    block_of = packed_blocks(dve, packed, past.g)
                if inside(0):
                    need(dve, maximum_taken, g)
                    nc.vector.tensor_scalar(drops[:, :, 1:G + 1], over(new_block[:, bass.ds(g * G, G)], H), 1.0, None, ALU.mult).then_inc(maximum_step, 1)
                    nc.vector.tensor_scalar(found[:, :, 0:1], maxima[:, :, G:G + 1], 1.0, None, ALU.mult).then_inc(maximum_step, 1)
                if inside(-1):
                    old = sums[:, bass.ds(block_of[0], 1), :]
                    values, weight = old[:, :, 0:DIM].rearrange("p a (h d) -> p (a h) d", h=H), old[:, :, DIM:].rearrange("p a h -> p (a h)")
                    dve.wait_ge(keep_ready, g)
                    need(dve, tile_added, G * past.g)
                    nc.vector.tensor_tensor(values, values, spread(keep[:, :], DV), ALU.mult).then_inc(scaled, 1)
                    nc.vector.tensor_tensor(weight, weight, keep[:, :], ALU.mult).then_inc(scaled, 1)
                    dve.wait_ge(exp_done, g)
                    weigh(past, 0)
                if inside(0):
                    dve.wait_ge(loc_copied, g + 1)
                    nc.vector.tensor_tensor(fresh[:, 1:P], locT[:, turn.slot, 1:P], locT[:, turn.slot, 0:P - 1], ALU.not_equal).then_inc(scan_step, 1)
                if inside(-1):
                    weigh(past, 1)
                if inside(0):
                    dve.wait_ge(scan_step, 3 * g + 1)
                    nc.vector.tensor_scalar(drop[:, :], fresh[:, 0:P], -FAR, None, ALU.mult).then_inc(scan_step, 1)
                if inside(-1):
                    dve.wait_ge(scaled, 2 * g)
                    add(past, block_of, 0)
                    weigh(past, 2)
                if inside(0):
                    dve.wait_ge(scan_step, 3 * g + 2)
                    dve.wait_ge(compat_turned, g + 1)
                    nc.vector.tensor_tensor_scan(run[:, :], drop[:, :], turn_ps[:, 1], -FAR, ALU.add, ALU.max).then_inc(scan_step, 1)
                if inside(-1):
                    add(past, block_of, 1)
                    weigh(past, 3)
                if inside(0):
                    dve.wait_ge(scan_step, 3 * g + 3)
                    nc.vector.tensor_tensor(lasts[:, :], run[:, :], fresh[:, 1:P + 1], ALU.mult).then_inc(lasts_ready, 1)
                if inside(-1):
                    for t in range(2, 6):
                        add(past, block_of, t)
                if inside(0):
                    dve.wait_ge(tops_ready, g + 1)
                    nc.vector.tensor_scalar(absent[:, :], tops[:, :, H], 0.5, -FAR, ALU.is_lt, ALU.mult).then_inc(maximum_step, 1)
                    dve.wait_ge(maximum_step, 5 * g + 3)
                    nc.vector.tensor_tensor(found[:, :, 1:].rearrange("p h t -> p t h"), tops[:, :, 0:H], spread(absent[:, :], H), ALU.add).then_inc(maximum_step, 1)
                if inside(-1):
                    add(past, block_of, 6)
                if inside(0):
                    dve.wait_ge(maximum_step, 5 * g + 4)
                    nc.vector.tensor_tensor_scan(forward[:, :], drop_row[:, 0:ROWS], found_row[:, :], -FAR, ALU.add, ALU.max).then_inc(maximum_step, 1)
                if inside(-1):
                    add(past, block_of, 7)
                if inside(0):
                    dve.wait_ge(maximum_step, 5 * g + 5)
                    nc.vector.tensor_tensor_scan(maxima_row[:, ::-1], drop_row[:, ROWS:0:-1], forward[:, ::-1], -FAR, ALU.add, ALU.max).then_inc(maximum_taken, 1)
                    dve.wait_ge(maximum_taken, g + 1)
                    nc.vector.tensor_tensor(fall[:, :], found[:, :, 0], maxima[:, :, 0], ALU.subtract).then_inc(fall_ready, 1)
            walk(dve, 0, GROUPS, GROUPS, step)

        @block.tensor
        def _(pe):
            pe.wait_ge(cleared, 7)
            pe.wait_ge(rpe_placed, 96)

            def turn_hot(turn, z):
                need(pe, hot_copied, 2 * turn.g + z)
                for t in range(4):
                    last = nc.tensor.transpose(hotT_ps[:, t], hot[:, turn.slot, 4 * z + t], c["ident"][:, :])
                last.then_inc(hot_turned, 1)

            def pair(turn, u):
                need(pe, pair_used, 4 * turn.g + u - 1)
                if u % 2 == 0:
                    pe.wait_ge(hot_copied, 2 * turn.g + u // 2 + 1)
                pe.wait_ge(q_in[u], 32 * (turn.g + 1))
                for w in range(2):
                    t = 2 * u + w
                    nc.tensor.matmul(qk_ps[u % 2][:, w, :], recT[:, t], rpe6[:, :], start=True, stop=False)
                    last = nc.tensor.matmul(qk_ps[u % 2][:, w, 0:DH], hotT[:, turn.slot, t], q[:, t], start=False, stop=True)
                last.then_inc(pair_ready, 1)

            def sum_tile(past, t):
                if t % 2 == 0:
                    pe.wait_ge(weighted, 4 * past.g + t // 2 + 1)
                need(pe, tile_added, G * past.g + t - 1)
                nc.tensor.matmul(sum_ps[t % 2][:, 0:SUM], hot[:, past.slot, t], kv[:, past.slot, t, DH:], start=True, stop=True).then_inc(tile_summed, 1)

            def step(turn, inside):
                g, past, after = turn.g, turn.after(-1), turn.after(1)
                if inside(1):
                    pe.wait_ge(loc_spread, g + 2)
                    need(pe, lasts_ready, g)
                    nc.tensor.transpose(turn_ps[:, 0], loc16[:, :, :].rearrange("p t h -> p (t h)"), c["ident"][:, :]).then_inc(loc_turned, 1)
                    pe.wait_ge(hot_built, g + 2)
                    turn_hot(after, 0)
                    pe.wait_ge(rec6_built, 3 * (g + 2))
                    need(pe, rec_copied, g + 1)
                    for t in range(G):
                        last = nc.tensor.transpose(recT_ps[0:K6, t], rec6[:, t].rearrange("p a w -> p (a w)"), ident_bf[:, :])
                    last.then_inc(rec_turned, 1)
                    turn_hot(after, 1)
                if inside(0):
                    pe.wait_ge(compat_ready, g + 1)
                    pe.wait_ge(loc_copied, g + 2 if inside(1) else g + 1)
                    nc.tensor.transpose(turn_ps[:, 1], compat[:, :, :].rearrange("p t h -> p (t h)"), c["ident"][:, :]).then_inc(compat_turned, 1)
                if inside(-1):
                    for t in range(4):
                        sum_tile(past, t)
                if inside(0):
                    pe.wait_ge(lasts_ready, g + 1)
                    need(pe, shift_done, g)
                    nc.tensor.transpose(lastsT_ps, lasts[:, :], c["ident"][:, :]).then_inc(lasts_turned, 1)
                if inside(-1):
                    sum_tile(past, 4)
                    sum_tile(past, 5)
                if inside(0):
                    pe.wait_ge(lasts_copied, g + 1)
                    for t in range(G):
                        last = nc.tensor.matmul(tops[:, t], hot[:, turn.slot, t], lastsT[:, t], start=True, stop=True)
                    last.then_inc(tops_ready, 1)
                if inside(-1):
                    for t in range(6, G):
                        sum_tile(past, t)
                if inside(1):
                    pe.wait_ge(rec_copied, g + 2)
                    pair(after, 0)
                    pair(after, 1)
                if inside(0):
                    pe.wait_ge(maximum_taken, g + 1)
                    for t in range(G):
                        last = nc.tensor.matmul(spread_ps[:, t], hotT[:, turn.slot, t], maxima[:, :, t + 1], start=True, stop=True)
                    last.then_inc(maxima_spread, 1)
                if inside(1):
                    pair(after, 2)
                    pair(after, 3)
            walk(pe, -1, GROUPS, GROUPS, step)


CHUNK = 7
CHUNKS = NB // CHUNK
HALF = CHUNKS // 2
WHOLE = (N - (CHUNKS - 1) * CHUNK * P) // P
assert 2 * HALF * CHUNK == NB and WHOLE == CHUNK - 1


def chunk_rows(sums, g):
    return sums[:, bass.ds(g * CHUNK, CHUNK), 0:DIM]


def move_chunks(engine, move):
    move(0, 0, 0, CHUNK, P)
    move(0, 1, CHUNK, CHUNK, P)
    with engine.Fori(1, HALF - 1) as i:
        for h in range(2):
            move(i, h, (2 * i + h) * CHUNK, CHUNK, P)
    move(HALF - 1, 0, (CHUNKS - 2) * CHUNK, CHUNK, P)
    move(HALF - 1, 1, (CHUNKS - 1) * CHUNK, WHOLE, P)
    move(HALF - 1, 1, NB - 1, 1, NLAST)


class Norm:
    def __init__(self, nc, k):
        self.nc = nc
        self.all_stats = k.sb("all_stats", [P, NB, 6])
        self.mean = k.sb("mean", [P, NB])
        self.scale = k.sb("scale", [P, NB])
        self.gap = k.sb("gap", [P, NB])
        self.between = k.sb("between", [P, NB])
        self.within = k.sb("within", [P, NB])
        self.normal = k.sb("normal", [P, 2, CHUNK, DIM])
        self.rows_ready = k.sem("rows_ready")
        self.stats_ready = k.sem("stats_ready")
        self.step = k.sem("step")
        self.guarded = k.sem("guarded")
        self.rooted = k.sem("rooted")
        self.centred = k.sem("centred")
        self.normalised = k.sem("normalised")

    def take(self, sums, g):
        for j in range(CHUNK):
            self.nc.vector.bn_stats(self.all_stats[:, bass.ds(g * CHUNK + j, 1), :].rearrange("p a w -> p (a w)"),
                                    sums[:, bass.ds(g * CHUNK + j, 1), 0:DIM].rearrange("p a n -> p (a n)")).then_inc(self.stats_ready, 1)

    def combine(self, dve):
        n = [0]

        def then(ins):
            n[0] += 1
            ins.then_inc(self.step, 1)
            dve.wait_ge(self.step, n[0])
        v = self.nc.vector
        m0, m1 = self.all_stats[:, :, 1], self.all_stats[:, :, 4]
        s0, s1 = self.all_stats[:, :, 2], self.all_stats[:, :, 5]
        dve.wait_ge(self.stats_ready, NB)
        then(v.tensor_tensor(self.mean[:, :], m0, m1, ALU.add))
        then(v.tensor_scalar(self.mean[:, :], self.mean[:, :], 0.5, None, ALU.mult))
        then(v.tensor_tensor(self.gap[:, :], m0, m1, ALU.subtract))
        then(v.tensor_scalar(self.gap[:, :], self.gap[:, :], 0.5, None, ALU.mult))
        then(v.tensor_tensor(self.between[:, :], self.gap[:, :], self.gap[:, :], ALU.mult))
        then(v.tensor_tensor(self.within[:, :], s0, s1, ALU.add))
        then(v.tensor_scalar(self.within[:, :], self.within[:, :], 1.0 / DIM, NORM_EPS, ALU.mult, ALU.add))
        v.tensor_tensor(self.within[:, :], self.within[:, :], self.between[:, :], ALU.add).then_inc(self.guarded, 1)
        dve.wait_ge(self.rooted, 1)
        then(v.reciprocal(self.scale[:, :], self.between[:, :]))

    def root(self, act):
        act.wait_ge(self.guarded, 1)
        self.nc.scalar.activation(self.between[:, :], self.within[:, :], ACT.Sqrt).then_inc(self.rooted, 1)

    def apply(self, dve, sums, g, h):
        v = self.nc.vector
        v.tensor_tensor(self.normal[:, h], chunk_rows(sums, g), spread(self.mean[:, bass.ds(g * CHUNK, CHUNK)], DIM), ALU.subtract).then_inc(self.centred, 1)
        dve.wait_ge(self.centred, g + 1)
        v.tensor_tensor(self.normal[:, h], self.normal[:, h], spread(self.scale[:, bass.ds(g * CHUNK, CHUNK)], DIM), ALU.mult).then_inc(self.normalised, 1)


def finish_attention(nc, k, c, x, sums, W_r, b_r, stalk, stalks_dram):
    norm = Norm(nc, k)
    xs = k.sb("xs", [P, 2, CHUNK, DIM])
    inverse = k.sb("inverse", [P, NB, H])
    normalT = k.sb("normalT", [P, 2, CHUNK, DIM])
    weight = k.sb("weight", [P, 2, STALK])
    bias = k.sb("bias", [P, STALK])
    PAIRS = [(0, 2), (2, 2), (4, 2), (6, 1)]
    normalT_ps = [k.ps(f"normalT_ps{u}", [P, 2, DIM]) for u in range(4)]
    stalk_ps = [k.ps(f"stalk_ps{h}", [P, 512]) for h in range(2)]
    weights_in = k.sem("weights_in")
    x_in = [k.sem(f"x_in{h}") for h in range(2)]
    den_step = k.sem("den_step")
    mixed = k.sem("mixed")
    kept = k.sem("kept")
    turned = k.sem("turned")
    turned_copied = k.sem("turned_copied")
    stalked = k.sem("stalked")
    stalk_ready = k.sem("stalk_ready")
    stalks_out = k.sem("stalks_out")
    with nc.Block() as block:
        @block.sync
        def _(sp):
            sp.dma_start(weight[:, :, :], W_r.rearrange("(a p) n -> p a n", p=P)).then_inc(weights_in, 16)
            sp.dma_start(bias[:, :], b_r.rearrange("(a n) -> a n", a=1).to_broadcast([P, STALK])).then_inc(weights_in, 16)

            def load(i, h, b, blocks, rows):
                need(sp, norm.rows_ready, 2 * i + h - 1)
                sp.dma_start(xs[0:rows, h, 0:blocks, :] if blocks > 1 else xs[0:rows, h, CHUNK - 1:CHUNK, :],
                             x[bass.ds(b * P, blocks * rows), :].rearrange("(j p) n -> p j n", p=rows)).then_inc(x_in[h], 16)
            move_chunks(sp, load)
            sp.wait_ge(stalk_ready, CHUNKS)
            sp.dma_start(stalks_dram.rearrange("(b p) s -> p b s", p=P), stalk[:, :, :]).then_inc(stalks_out, 16)
            sp.wait_ge(stalks_out, 16)
            sp.wait_ge(weights_in, 32)

        @block.vector
        def _(dve):
            nc.vector.tensor_scalar(inverse[:, :, :], sums[:, :, DIM:], SOFT_EPS, None, ALU.add).then_inc(den_step, 1)
            dve.wait_ge(den_step, 1)
            nc.vector.reciprocal(inverse[:, :, :], inverse[:, :, :]).then_inc(den_step, 1)
            dve.wait_ge(den_step, 2)

            def mix(i, last):
                for h in range(2):
                    g = 2 * i + h
                    values = chunk_rows(sums, g).rearrange("p b (h d) -> p b h d", h=H)
                    need(dve, norm.rows_ready, g)
                    nc.vector.tensor_tensor(values, values, inverse[:, bass.ds(g * CHUNK, CHUNK), :].unsqueeze(3).to_broadcast([P, CHUNK, H, DV]), ALU.mult).then_inc(mixed, 1)
                    if not (isinstance(g, int) and g == 0):
                        norm.take(sums, g - 1)
                    dve.wait_ge(mixed, g + 1)
                    dve.wait_ge(x_in[h], 16 * i + (32 if last and h == 1 else 16))
                    nc.vector.tensor_tensor(chunk_rows(sums, g), chunk_rows(sums, g), xs[:, h], ALU.add).then_inc(norm.rows_ready, 1)
            rounds_ahead(dve, HALF, mix)
            dve.wait_ge(norm.rows_ready, CHUNKS)
            norm.take(sums, CHUNKS - 1)
            norm.combine(dve)
            dve.wait_ge(weights_in, 32)

            def add_bias(g, h):
                dve.wait_ge(stalked, g + 1)
                nc.vector.tensor_tensor(stalk[:, bass.ds(g * CHUNK, CHUNK), :], stalk_ps[h][:, 0:CHUNK * STALK].rearrange("p (j s) -> p j s", s=STALK),
                                        over(bias[:, :], CHUNK), ALU.add).then_inc(stalk_ready, 1)

            def normalise(i):
                for h in range(2):
                    g = 2 * i + h
                    need(dve, turned, 4 * (g - 1))
                    need(dve, kept, g - 1)
                    norm.apply(dve, sums, g, h)
                    if not (isinstance(g, int) and g == 0):
                        add_bias(g - 1, 1 - h)
            rounds(dve, HALF, normalise)
            add_bias(CHUNKS - 1, 1)

        @block.scalar
        def _(act):
            norm.root(act)

            def body(i):
                for h in range(2):
                    g = 2 * i + h
                    need(act, stalked, g - 1)
                    for u, (j, n) in enumerate(PAIRS):
                        act.wait_ge(turned, 4 * g + u + 1)
                        nc.scalar.activation(normalT[:, h, j:j + n], normalT_ps[u][:, 0:n], ACT.Copy).then_inc(turned_copied, 1)
                    act.wait_ge(norm.normalised, g + 1)
                    nc.scalar.activation(chunk_rows(sums, g), norm.normal[:, h], ACT.Copy).then_inc(kept, 1)
            rounds(act, HALF, body)
            act.wait_ge(kept, CHUNKS)

        @block.tensor
        def _(pe):
            pe.wait_ge(weights_in, 32)

            def body(i):
                for h in range(2):
                    g = 2 * i + h
                    pe.wait_ge(norm.normalised, g + 1)
                    for u, (j, n) in enumerate(PAIRS):
                        need(pe, turned_copied, 4 * (g - 1) + u + 1)
                        for t in range(n):
                            for a in range(2):
                                last = nc.tensor.transpose(normalT_ps[u][:, t, a * P:(a + 1) * P], norm.normal[:, h, j + t, a * P:(a + 1) * P], c["ident"][:, :])
                        last.then_inc(turned, 1)
                    need(pe, stalk_ready, g - 1)
                    for u, (j, n) in enumerate(PAIRS):
                        pe.wait_ge(turned_copied, 4 * g + u + 1)
                        for t in range(j, j + n):
                            for a in range(2):
                                last = nc.tensor.matmul(stalk_ps[h][:, t * STALK:(t + 1) * STALK], normalT[:, h, t, a * P:(a + 1) * P], weight[:, a], start=(a == 0), stop=(a == 1))
                    last.then_inc(stalked, 1)
            rounds(pe, HALF, body)


def diffuse(nc, k, c, stalk, stalks_dram, rec_dram, packed, flow):
    rec = k.sb("rec", [P, 3, G, REC])
    far = k.sb("far", [P, 3, G, STALK])
    dst_at = k.sb("dst_at", [P, G], I32)
    dst_of = k.sb("dst_of", [P, G], I32)
    at = k.sb("at", [P, 3, G])
    of = k.sb("of", [P, 3, G])
    hot = k.sb("hot", [P, 3, G, P], BF16)
    hotT = k.sb("hotT", [P, 3, G, P], BF16)
    ident_bf = k.sb("ident_bf", [P, P], BF16)
    stalk_parts = k.sb("stalk_parts", [P, NB, 3, STALK], BF16)
    stalk_left = k.sb("stalk_left", [P, NB, STALK])
    near = k.sb("near", [P, G, STALK])
    left = k.sb("left", [P, G, STALK])
    parts = k.sb("parts", [P, 3, G, 3, STALK], BF16)
    dst_hot = k.sb("dst_hot", [P, 3, G, P])
    differs = k.sb("differs", [P, 3, G, STALK])
    opposed = k.sb("opposed", [P, G, STALK])
    zero_mat = k.sb("zero_mat", [P, P])
    placed = k.sb("placed", [P, G, NB, STALK])
    hotT_ps = k.ps("hotT_ps", [P, G, P], BF16)
    near_ps = k.ps("near_ps", [P, 512])
    near_parts = near_ps[:, 0:G * 3 * STALK].rearrange("p (t n s) -> p t n s", t=G, n=3)
    flow_ps = k.ps("flow_ps", [P, NB, STALK])
    cleared = k.sem("cleared")
    rec_in = [k.sem(f"rec_in{s}") for s in range(3)]
    gathered = [k.sem(f"gathered{s}") for s in range(3)]
    sp_turn = k.sem("sp_turn")
    pool_turn = k.sem("pool_turn")
    distance = k.sem("distance")
    hot_ready = k.sem("hot_ready")
    hot_turned = k.sem("hot_turned")
    hot_copied = k.sem("hot_copied")
    dst_step = k.sem("dst_step")
    dst_distance = k.sem("dst_distance")
    dst_hot_ready = k.sem("dst_hot_ready")
    near_ready = k.sem("near_ready")
    near_step = k.sem("near_step")
    differ_ready = k.sem("differ_ready")
    opposed_ready = k.sem("opposed_ready")
    part_step = k.sem("part_step")
    parts_ready = k.sem("parts_ready")
    placed_ready = k.sem("placed_ready")
    tile_into = k.sem("tile_into")
    out_done = k.sem("out_done")
    all_into = k.sem("all_into")
    with nc.Block() as block:
        @block.sync
        def _(sp):
            def load(turn, inside):
                if not (isinstance(turn.g, int) and turn.g < 3):
                    sp.wait_ge(differ_ready, turn.g - 2)
                    sp.sem_inc(sp_turn)
                    sp.wait_ge(dst_hot_ready, turn.g - 2)
                    sp.sem_inc(sp_turn)
                sp.dma_start(rec[:, turn.slot], rec_dram[bass.ds(turn.g * (G * P), G * P), :].rearrange("(p t) w -> p t w", t=G)).then_inc(rec_in[turn.slot], 16)
            walk(sp, 0, GROUPS - 1, GROUPS, load)

        @block.gpsimd
        def _(pool):
            def gather(turn, inside):
                pool.wait_ge(rec_in[turn.slot], 16 * turn.used)
                pool.sem_inc(pool_turn)
                if not (isinstance(turn.g, int) and turn.g < 3):
                    pool.wait_ge(differ_ready, turn.g - 2)
                    pool.sem_inc(pool_turn)
                for t in range(G):
                    nc.gpsimd.indirect_dma_start(far[:, turn.slot, t], None, stalks_dram[:, :],
                                                 bass.IndirectOffsetOnAxis(ap=rec[:, turn.slot, t, DST:DST + 1].bitcast(I32), axis=0)).then_inc(gathered[turn.slot], 16)
            walk(pool, 0, GROUPS - 1, GROUPS, gather)

        @block.scalar
        def _(act):
            def one_hots(turn):
                act.wait_ge(rec_in[turn.slot], 16 * turn.used)
                need(act, out_done, turn.g - 2)
                for t in range(G):
                    nc.scalar.activation(hot[:, turn.slot, t], c["row"][:, :], ACT.Abs, bias=rec[:, turn.slot, t, LOC:LOC + 1], scale=-1.0).then_inc(distance, 1)
                act.wait_ge(distance, G * (turn.g + 1))
                nc.scalar.activation(hot[:, turn.slot], hot[:, turn.slot], ACT.Relu, bias=1.0, scale=-1.0).then_inc(hot_ready, 1)

            def dst_one_hots(turn):
                act.wait_ge(dst_step, 4 * (turn.g + 1))
                need(act, tile_into, G * (turn.g - 2))
                for t in range(G):
                    nc.scalar.activation(dst_hot[:, turn.slot, t], c["row"][:, :], ACT.Abs, bias=at[:, turn.slot, t:t + 1], scale=-1.0).then_inc(dst_distance, 1)
                act.wait_ge(dst_distance, G * (turn.g + 1))
                nc.scalar.activation(dst_hot[:, turn.slot], dst_hot[:, turn.slot], ACT.Relu, bias=1.0, scale=-1.0).then_inc(dst_hot_ready, 1)

            def step(turn, inside):
                then = turn.after(2)
                if inside(2):
                    one_hots(then)
                    need(act, near_ready, then.g - 2)
                    dst_one_hots(then)
                    act.wait_ge(hot_turned, then.g + 1)
                    nc.scalar.activation(hotT[:, then.slot], hotT_ps[:, :, :], ACT.Copy).then_inc(hot_copied, 1)
            walk(act, -2, GROUPS - 3, GROUPS, step)

        @block.vector
        def _(dve):
            nc.vector.memset(zero_mat[:, :], 0.0).then_inc(cleared, 1)
            nc.vector.tensor_copy(ident_bf[:, :], c["ident"][:, :]).then_inc(cleared, 1)
            nc.vector.tensor_copy(stalk_parts[:, :, 0], stalk[:, :, :]).then_inc(cleared, 1)
            dve.wait_ge(cleared, 3)
            nc.vector.tensor_tensor(stalk_left[:, :, :], stalk[:, :, :], stalk_parts[:, :, 0], ALU.subtract).then_inc(cleared, 1)
            dve.wait_ge(cleared, 4)
            nc.vector.tensor_copy(stalk_parts[:, :, 1], stalk_left[:, :, :]).then_inc(cleared, 1)
            dve.wait_ge(cleared, 5)
            nc.vector.tensor_tensor(stalk_parts[:, :, 2], stalk_left[:, :, :], stalk_parts[:, :, 1], ALU.subtract).then_inc(cleared, 1)

            def step(turn, inside):
                g, then = turn.g, turn.after(2)
                if inside(0):
                    dve.wait_ge(near_ready, g + 1)
                    need(dve, opposed_ready, g)
                    nc.vector.tensor_reduce(near[:, :, :], near_parts.rearrange("p t n s -> p t s n"), AX.X, ALU.add).then_inc(near_step, 1)
                    dve.wait_ge(near_step, g + 1)
                    dve.wait_ge(gathered[turn.slot], 16 * G * turn.used)
                    nc.vector.tensor_tensor(differs[:, turn.slot], far[:, turn.slot], near[:, :, :], ALU.subtract).then_inc(differ_ready, 1)
                if inside(2):
                    dve.wait_ge(rec_in[then.slot], 16 * then.used)
                    dst = rec[:, then.slot, :, DST].bitcast(I32)
                    need(dve, dst_step, 4 * then.g)
                    nc.vector.tensor_scalar(dst_at[:, :], dst, P - 1, None, ALU.bitwise_and).then_inc(dst_step, 1)
                    nc.vector.tensor_scalar(dst_of[:, :], dst, 7, None, ALU.logical_shift_right).then_inc(dst_step, 1)
                    need(dve, dst_hot_ready, then.g - 2)
                    dve.wait_ge(dst_step, 4 * then.g + 2)
                    nc.vector.tensor_copy(at[:, then.slot], dst_at[:, :]).then_inc(dst_step, 1)
                    nc.vector.tensor_copy(of[:, then.slot], dst_of[:, :]).then_inc(dst_step, 1)
                if inside(0):
                    dve.wait_ge(differ_ready, g + 1)
                    dve.wait_ge(dst_step, 4 * (g + 1))
                    for t in range(G):
                        need(dve, tile_into, G * (g - 1) + t + 1)
                        nc.vector.scalar_tensor_tensor(placed[:, t], spread(c["row"][:, 0:NB], STALK), of[:, turn.slot, t:t + 1],
                                                       over(differs[:, turn.slot, t], NB), ALU.is_equal, ALU.mult).then_inc(placed_ready, 1)
                        if t == 1:
                            need(dve, part_step, 3 * g)
                            nc.vector.tensor_scalar(opposed[:, :, :], differs[:, turn.slot], -1.0, None, ALU.mult).then_inc(opposed_ready, 1)
                        elif t == 2:
                            need(dve, out_done, g - 2)
                            dve.wait_ge(opposed_ready, g + 1)
                            nc.vector.tensor_copy(parts[:, turn.slot, :, 0], opposed[:, :, :]).then_inc(part_step, 1)
                        elif t == 3:
                            dve.wait_ge(part_step, 3 * g + 1)
                            nc.vector.tensor_tensor(left[:, :, :], opposed[:, :, :], parts[:, turn.slot, :, 0], ALU.subtract).then_inc(part_step, 1)
                        elif t == 4:
                            dve.wait_ge(part_step, 3 * g + 2)
                            nc.vector.tensor_copy(parts[:, turn.slot, :, 1], left[:, :, :]).then_inc(part_step, 1)
                        elif t == 5:
                            dve.wait_ge(part_step, 3 * g + 3)
                            nc.vector.tensor_tensor(parts[:, turn.slot, :, 2], left[:, :, :], parts[:, turn.slot, :, 1], ALU.subtract).then_inc(parts_ready, 1)
            walk(dve, -2, GROUPS - 1, GROUPS, step)
            dve.wait_ge(all_into, 1)
            nc.vector.tensor_copy(flow[:, :, :], flow_ps[:, :, :]).then_inc(cleared, 1)

        @block.tensor
        def _(pe):
            pe.wait_ge(cleared, 6)
            nc.tensor.matmul(flow_ps[:, :, :], zero_mat[:, :], c["row"][:, 0:1].to_broadcast([P, STALK * NB]), start=True, stop=False)

            def step(turn, inside):
                g, after, then = turn.g, turn.after(1), turn.after(2)
                for t in range(G):
                    if inside(0):
                        if t == 0:
                            pe.wait_ge(dst_hot_ready, g + 1)
                        pe.wait_ge(placed_ready, G * g + t + 1)
                        nc.tensor.matmul(flow_ps[:, :, :], dst_hot[:, turn.slot, t], placed[:, t], start=False, stop=False).then_inc(tile_into, 1)
                    if inside(1) and t < 4:
                        if t == 0:
                            next_blocks = packed_blocks(pe, packed, after.g)
                            pe.wait_ge(hot_copied, g + 2)
                            need(pe, near_step, g + 1)
                        for u in (2 * t, 2 * t + 1):
                            last = nc.tensor.matmul(near_parts[:, u].rearrange("p n s -> p (n s)"), hotT[:, after.slot, u],
                                                    stalk_parts[:, bass.ds(next_blocks[u], 1), :, :].rearrange("p a n s -> p (a n s)"), start=True, stop=True)
                        if t == 3:
                            last.then_inc(near_ready, 1)
                    if inside(0) and t == 5:
                        block_of = packed_blocks(pe, packed, g)
                    if inside(2) and t >= 4:
                        if t == 4:
                            pe.wait_ge(hot_ready, g + 3)
                            need(pe, hot_copied, g + 2)
                        for u in (2 * t - G, 2 * t - G + 1):
                            last = nc.tensor.transpose(hotT_ps[:, u], hot[:, then.slot, u], ident_bf[:, :])
                        if t == G - 1:
                            last.then_inc(hot_turned, 1)
                if inside(0):
                    pe.wait_ge(parts_ready, g + 1)
                    for t in range(G):
                        for n in range(3):
                            last = nc.tensor.matmul(flow_ps[:, bass.ds(block_of[t], 1), :].rearrange("p a s -> p (a s)"), hot[:, turn.slot, t], parts[:, turn.slot, t, n], start=False, stop=False)
                    last.then_inc(out_done, 1)
            walk(pe, -2, GROUPS - 1, GROUPS, step)
            nc.tensor.matmul(flow_ps[:, :, :], zero_mat[:, :], c["row"][:, 0:1].to_broadcast([P, STALK * NB]), start=False, stop=True).then_inc(all_into, 1)


def finish(nc, k, c, sums, flow, W_o, b_o, out):
    WITH_ONE = STALK + 1
    norm = Norm(nc, k)
    weight = k.sb("weight", [P, CHUNK, DIM])
    flows = k.sb("flows", [P, 2, P])
    flow_at = flows[:, :, 0:CHUNK * WITH_ONE].rearrange("p h (j s) -> p h j s", s=WITH_ONE)
    flowT = k.sb("flowT", [P, 2, P])
    bent = k.sb("bent", [P, 2, CHUNK, DIM])
    PAIRS = [(0, 2), (2, 2), (4, 2), (6, 1)]
    flowT_ps = [k.ps(f"flowT_ps{h}", [P, P]) for h in range(2)]
    wide_ps = [k.ps(f"wide_ps{u}", [P, 2, DIM]) for u in range(4)]
    cleared = k.sem("cleared")
    weights_in = k.sem("weights_in")
    flow_copied = k.sem("flow_copied")
    turned = k.sem("turned")
    turned_copied = k.sem("turned_copied")
    widened = k.sem("widened")
    bent_ready = k.sem("bent_ready")
    rows_out = [k.sem(f"rows_out{h}") for h in range(2)]
    with nc.Block() as block:
        @block.sync
        def _(sp):
            sp.wait_ge(cleared, 3)
            for j in range(CHUNK):
                sp.dma_start(weight[j * WITH_ONE:j * WITH_ONE + STALK, j, :], W_o).then_inc(weights_in, 16)
                sp.dma_start(weight[j * WITH_ONE + STALK:(j + 1) * WITH_ONE, j, :], b_o.rearrange("(a n) -> a n", a=1)).then_inc(weights_in, 16)

            def store(i, h, b, blocks, rows):
                sp.wait_ge(norm.normalised, 2 * i + h + 1)
                sp.dma_start(out[bass.ds(b * P, blocks * rows), :].rearrange("(j p) n -> p j n", p=rows),
                             norm.normal[0:rows, h, 0:blocks, :] if blocks > 1 else norm.normal[0:rows, h, CHUNK - 1:CHUNK, :]).then_inc(rows_out[h], 16)
            move_chunks(sp, store)
            sp.wait_ge(rows_out[0], 16 * HALF)
            sp.wait_ge(rows_out[1], 16 * (HALF + 1))
            sp.wait_ge(weights_in, 32 * CHUNK)

        @block.vector
        def _(dve):
            nc.vector.memset(weight[:, :, :], 0.0).then_inc(cleared, 1)
            nc.vector.memset(flows[:, :, :], 0.0).then_inc(cleared, 1)
            dve.wait_ge(cleared, 2)
            nc.vector.memset(flow_at[:, :, :, STALK:], 1.0).then_inc(cleared, 1)
            dve.wait_ge(cleared, 3)

            def lend(g, h):
                need(dve, turned, g - 1)
                nc.vector.tensor_scalar(flow_at[:, h, :, 0:STALK], flow[:, bass.ds(g * CHUNK, CHUNK), :], 1.0, None, ALU.mult).then_inc(flow_copied, 1)
            lend(0, 0)

            def add(i, last):
                for h in range(2):
                    g = 2 * i + h
                    if not (last and h == 1):
                        need(dve, norm.rows_ready, g)
                        lend(g + 1, 1 - h)
                    else:
                        dve.wait_ge(norm.rows_ready, g)
                    if not (isinstance(g, int) and g == 0):
                        norm.take(sums, g - 1)
                    dve.wait_ge(bent_ready, 4 * (g + 1))
                    nc.vector.tensor_tensor(chunk_rows(sums, g), chunk_rows(sums, g), bent[:, h], ALU.add).then_inc(norm.rows_ready, 1)
            rounds_ahead(dve, HALF, add)
            dve.wait_ge(norm.rows_ready, CHUNKS)
            norm.take(sums, CHUNKS - 1)
            norm.combine(dve)

            def normalise(i):
                for h in range(2):
                    need(dve, rows_out[h], 16 * i)
                    norm.apply(dve, sums, 2 * i + h, h)
            rounds(dve, HALF, normalise)

        @block.scalar
        def _(act):
            def body(i):
                for h in range(2):
                    g = 2 * i + h
                    act.wait_ge(turned, g + 1)
                    need(act, widened, 4 * (g - 1))
                    nc.scalar.activation(flowT[:, h], flowT_ps[h][:, :], ACT.Copy).then_inc(turned_copied, 1)
                    need(act, norm.rows_ready, g - 1)
                    for u, (j, n) in enumerate(PAIRS):
                        act.wait_ge(widened, 4 * g + u + 1)
                        nc.scalar.activation(bent[:, h, j:j + n], wide_ps[u][:, 0:n], ACT.Gelu).then_inc(bent_ready, 1)
            rounds(act, HALF, body)
            norm.root(act)

        @block.tensor
        def _(pe):
            pe.wait_ge(weights_in, 32 * CHUNK)

            def body(i):
                for h in range(2):
                    g = 2 * i + h
                    pe.wait_ge(flow_copied, g + 1)
                    need(pe, turned_copied, g - 1)
                    nc.tensor.transpose(flowT_ps[h][:, :], flows[:, h], c["ident"][:, :]).then_inc(turned, 1)
                    pe.wait_ge(turned_copied, g + 1)
                    for u, (j, n) in enumerate(PAIRS):
                        need(pe, bent_ready, 4 * (g - 1) + u + 1)
                        for t in range(n):
                            last = nc.tensor.matmul(wide_ps[u][:, t], flowT[:, h], weight[:, j + t], start=True, stop=True)
                        last.then_inc(widened, 1)
            rounds(pe, HALF, body)


def graph_network(nc, x, src, dst, edge_attr, Wqkv, bqkv, Wk_rpe, bk_rpe, Wq_rpe, bq_rpe, W_r, b_r, W_o, b_o, out, scratch):
    q_dram, kv_dram, rec_dram, blocks_dram, stalks_dram = scratch[:5]
    with ExitStack() as whole:
        k = Room(nc, whole, "all")
        c = {name: k.sb(name, [P, P]) for name in ("ident", "row")}
        with ExitStack() as sorting:
            s = Room(nc, sorting, "sorting")
            c.update({name: s.sb(name, [P, P]) for name in ("ones", "zeros", "before", "after")})
            c.update({name: s.sb(name, [P, P], BF16) for name in ("ident_bf", "zeros_bf", "row_bf")})
            c["row_i"] = s.sb("row_i", [P, P], I32)
            e = {"src": s.sb("src", [P, NCH, CT], I32), "dst": s.sb("dst", [P, NCH, CT], I32)}
            e.update({name: s.sb(name, [P, NCH * CT]) for name in ("src_f", "at", "of")})
            counts = s.sb("counts", [P, NB])
            base = s.sb("base", [P, NB])
            with ExitStack() as stage:
                constants(nc, Room(nc, stage, "const"), c)
            with ExitStack() as stage:
                project_and_count(nc, Room(nc, stage, "project"), c, x, src, dst, Wqkv, bqkv, e, q_dram, kv_dram, rec_dram, counts)
            with ExitStack() as stage:
                place_nodes(nc, Room(nc, stage, "place"), c, counts, base, blocks_dram)
            with ExitStack() as stage:
                sort_edges(nc, Room(nc, stage, "sort"), c, e, edge_attr, base, rec_dram)
        packed = k.sb("packed", [1, ST // 4], I32)
        sums = k.sb("sums", [P, NB, DIM + H])
        with ExitStack() as stage:
            attend(nc, Room(nc, stage, "attend"), c, Wk_rpe, bk_rpe, Wq_rpe, bq_rpe, q_dram, kv_dram, rec_dram, blocks_dram, packed, sums)
        stalk = k.sb("stalk", [P, NB, STALK])
        flow = k.sb("flow", [P, NB, STALK])
        with ExitStack() as stage:
            finish_attention(nc, Room(nc, stage, "settle"), c, x, sums, W_r, b_r, stalk, stalks_dram)
        with ExitStack() as stage:
            diffuse(nc, Room(nc, stage, "diffuse"), c, stalk, stalks_dram, rec_dram, packed, flow)
        with ExitStack() as stage:
            finish(nc, Room(nc, stage, "finish"), c, sums, flow, W_o, b_o, out)


_INS = ['x', 'src', 'dst', 'edge_attr_18', 'L0_gnn_Wqkv', 'L0_gnn_bqkv', 'L0_gnn_Wk_rpe', 'L0_gnn_bk_rpe',
        'L0_gnn_Wq_rpe', 'L0_gnn_bq_rpe', 'L1_gnn_W_r', 'L1_gnn_b_r', 'L1_gnn_W_o', 'L1_gnn_b_o']
_OUTS = [((N, DIM), 'float32')]
_SCRATCH = [("queries", (NB, P, DH), 'float32'), ("kv", (NB * P, DH + DIM), 'float32'), ("records", (ST * P, REC), 'float32'),
            ("tile_blocks", (P * TPP,), 'int32'), ("stalks", (NB * P, STALK), 'float32')]


def kernel(**inputs):
    import numpy as _np
    import concourse.bacc as _bacc
    from concourse import mybir as _mybir
    from concourse.bass_utils import run_bass_kernel_spmd as _run

    nc = _bacc.Bacc("TRN2", target_bir_lowering=False, num_devices=1)
    arrays, args = {}, []
    for name in _INS:
        a = _np.ascontiguousarray(inputs[name])
        arrays[f"in_{name}_dram"] = a
        args.append(nc.dram_tensor(f"in_{name}_dram", a.shape, _mybir.dt.from_np(a.dtype), kind="ExternalInput").ap())
    for i, (shape, dtype) in enumerate(_OUTS):
        args.append(nc.dram_tensor(f"out_{i}_dram", shape, _mybir.dt.from_np(_np.dtype(dtype)), kind="ExternalOutput").ap())
    scratch = [nc.dram_tensor(f"{name}_dram", shape, _mybir.dt.from_np(_np.dtype(dtype)), kind="Internal").ap()
               for name, shape, dtype in _SCRATCH]
    graph_network(nc, *args, scratch)
    r = _run(nc, [arrays], core_ids=[0])
    return r.results[0]["out_0_dram"]
```
